# Optimizing a Trainium2 kernel written in Bass

```python
import numpy as np
import jax
import jax.numpy as jnp

def _softmax(x, axis=-1):
    return jax.nn.softmax(x, axis=axis)

def _gelu(x):
    return jax.nn.gelu(x, approximate=True)

def _silu(x):
    return jax.nn.silu(x)

def _sigmoid(x):
    return jax.nn.sigmoid(x)

def _layernorm(x, axis=-1, eps=1e-05):
    m = jnp.mean(x, axis=axis, keepdims=True)
    v = jnp.var(x, axis=axis, keepdims=True)
    return (x - m) / jnp.sqrt(v + eps)

def _scatter_add(tgt, idx, src, axis=0):
    return tgt.at[idx].add(src)

def _segment_sum(src, seg, n):
    return jax.ops.segment_sum(src, seg, n)
kernel_name = 'mk_adj_preln_d4_adj_r2_a4d994'

def setup_inputs(seed: int=0):
    np.random.seed(seed)
    _w = jnp.asarray

    def _rec_inputs():
        import jax
        import jax.numpy as jnp
        _gk = jax.random.key(seed)
        x = 7.22e-05 + 1 * jax.random.normal(jax.random.fold_in(_gk, 1), (16, 512, 128), jnp.float32)
        _w = (1.0 + jnp.arange(512, dtype=jnp.float32)) ** (-0.5)
        _w = _w / _w.mean()
        _pij = jnp.clip(0.00390625 * _w[:, None] * _w[None, :], 0.0, 1.0)
        _a = jax.random.uniform(jax.random.fold_in(_gk, 2), (512, 512)) < _pij
        _a = jnp.logical_or(_a, jnp.swapaxes(_a, -1, -2))
        _a = jnp.logical_or(_a, jnp.eye(512, dtype=bool))
        _af = _a.astype(jnp.float32)
        _af = _af * jax.random.uniform(jax.random.fold_in(_gk, 3), (512, 512), jnp.float32, 0.05, 0.000976562)
        adj = _af
        return (x, adj)
    x, adj = _rec_inputs()

    def _L0_gnn_setup():
        import jax, jax.numpy as jnp
        import numpy as np
        N_STEPS = 8
        SPATIAL_SCALE = 1.0
        key = jax.random.key(seed)
        ks = jax.random.split(key, 6)
        B, N, D = (32, 512, 128)
        x = jax.random.normal(ks[0], (B, N, D), dtype=jnp.float32)
        adj_mx = jax.random.uniform(ks[1], (N, N), dtype=jnp.float32) / N
        alpha_train = jnp.ones((N,), dtype=jnp.float32)
        w = jnp.eye(D, dtype=jnp.float32) + 0.01 * jax.random.normal(ks[2], (D, D), dtype=jnp.float32)
        d = jax.random.uniform(ks[3], (D,), dtype=jnp.float32)
        fc_in_w = jax.random.normal(ks[4], (D, D), dtype=jnp.float32) * (1.0 / np.sqrt(D))
        fc_in_b = jnp.zeros((D,), dtype=jnp.float32)
        return {'x': x, 'adj_mx': adj_mx, 'alpha_train': alpha_train, 'w': w, 'd': d, 'fc_in_w': fc_in_w, 'fc_in_b': fc_in_b, 'vt': 0}
    _L0_gnn_all = _L0_gnn_setup()
    _L0_gnn_in = {k: v for k, v in _L0_gnn_all.items() if k in ('alpha_train', 'w', 'd', 'fc_in_w', 'fc_in_b')}
    del _L0_gnn_all

    def _L1_gnn_setup():
        import jax, jax.numpy as jnp
        import numpy as np
        B, N, C, D = (8, 1024, 128, 128)
        NEG = -1e+16
        key = jax.random.key(seed)
        k1, k2, k3, k4, k5 = jax.random.split(key, 5)
        inputs = jax.random.normal(k1, (B, N, C), dtype=jnp.float32)
        graph = jax.random.bernoulli(k2, 0.5, (N, N)).astype(jnp.float32)
        W = jax.random.normal(k3, (C, D), dtype=jnp.float32) * (1.0 / np.sqrt(C))
        b_lin = jax.random.normal(k4, (D,), dtype=jnp.float32) * 0.02
        b = jax.random.normal(k5, (D,), dtype=jnp.float32)
        return {'inputs': inputs, 'graph': graph, 'W': W, 'b_lin': b_lin, 'b': b}
    _L1_gnn_all = _L1_gnn_setup()
    _L1_gnn_in = {k: v for k, v in _L1_gnn_all.items() if k in ('W', 'b_lin', 'b')}
    del _L1_gnn_all

    def _L2_gnn_setup():
        import jax, jax.numpy as jnp
        import numpy as np
        EPS = 1e-05

        def _batchnorm(x, gamma, beta):
            mu = jnp.mean(x, axis=0)
            var = jnp.var(x, axis=0)
            return (x - mu) * jax.lax.rsqrt(var + EPS) * gamma + beta
        key = jax.random.key(seed)
        ks = jax.random.split(key, 4)
        b, n, d, h, o = (32, 1024, 128, 256, 128)
        features = jax.random.normal(ks[0], (b, n, d), dtype=jnp.float32)
        A = jax.random.uniform(ks[1], (n, n), dtype=jnp.float32)
        lim1 = float(np.sqrt(6.0 / (d + h)))
        W1 = jax.random.uniform(ks[2], (h, d), minval=-lim1, maxval=lim1, dtype=jnp.float32)
        b1 = jnp.zeros((h,), jnp.float32)
        lim2 = float(np.sqrt(6.0 / (h + o)))
        W2 = jax.random.uniform(ks[3], (o, h), minval=-lim2, maxval=lim2, dtype=jnp.float32)
        b2 = jnp.zeros((o,), jnp.float32)
        g1 = jnp.ones((h,), jnp.float32)
        be1 = jnp.zeros((h,), jnp.float32)
        g2 = jnp.ones((o,), jnp.float32)
        be2 = jnp.zeros((o,), jnp.float32)
        return {'features': features, 'A': A, 'W1': W1, 'b1': b1, 'g1': g1, 'be1': be1, 'W2': W2, 'b2': b2, 'g2': g2, 'be2': be2}
    _L2_gnn_all = _L2_gnn_setup()
    _L2_gnn_in = {k: v for k, v in _L2_gnn_all.items() if k in ('W1', 'b1', 'g1', 'be1', 'W2', 'b2', 'g2', 'be2')}
    del _L2_gnn_all

    def _L3_gnn_setup():
        import jax, jax.numpy as jnp
        import numpy as np
        B, T, D, H = (64, 1024, 128, 128)
        MAX_SKIP = 4

        def _lstm_last(Wih, Whh, bih, bhh, xs):
            N, _, Hd = xs.shape
            bias = bih + bhh

            def step(carry, x_t):
                h, c = carry
                g = x_t @ Wih.T + h @ Whh.T + bias
                i, f, gg, o = jnp.split(g, 4, axis=-1)
                c = jax.nn.sigmoid(f) * c + jax.nn.sigmoid(i) * jnp.tanh(gg)
                h = jax.nn.sigmoid(o) * jnp.tanh(c)
                return ((h, c), None)
            init = (jnp.zeros((N, Hd), xs.dtype), jnp.zeros((N, Hd), xs.dtype))
            (h_last, _), _ = jax.lax.scan(step, init, jnp.swapaxes(xs, 0, 1))
            return h_last
        key = jax.random.key(seed)
        ks = jax.random.split(key, 8)
        s = 0.05
        x = jax.random.normal(ks[0], (B, T, D), jnp.float32)
        adj = jax.random.uniform(ks[1], (T, T), jnp.float32) / T
        Wg0 = jax.random.normal(ks[2], (D, H), jnp.float32) * s
        bg0 = jnp.zeros((H,), jnp.float32)
        Wg1 = jax.random.normal(ks[3], (H, H), jnp.float32) * s
        bg1 = jnp.zeros((H,), jnp.float32)
        Wih = jax.random.normal(ks[4], (MAX_SKIP, 4 * H, H), jnp.float32) * s
        Whh = jax.random.normal(ks[5], (MAX_SKIP, 4 * H, H), jnp.float32) * s
        bih = jax.random.normal(ks[6], (MAX_SKIP, 4 * H), jnp.float32) * s
        bhh = jax.random.normal(ks[7], (MAX_SKIP, 4 * H), jnp.float32) * s
        return dict(x=x, adj=adj, Wg0=Wg0, bg0=bg0, Wg1=Wg1, bg1=bg1, Wih=Wih, Whh=Whh, bih=bih, bhh=bhh)
    _L3_gnn_all = _L3_gnn_setup()
    _L3_gnn_in = {k: v for k, v in _L3_gnn_all.items() if k in ('Wg0', 'bg0', 'Wg1', 'bg1', 'Wih', 'Whh', 'bih', 'bhh')}
    del _L3_gnn_all
    return {'x': x, 'adj': adj, 'L0_gnn_alpha_train': _L0_gnn_in['alpha_train'], 'L0_gnn_w': _L0_gnn_in['w'], 'L0_gnn_d': _L0_gnn_in['d'], 'L0_gnn_fc_in_w': _L0_gnn_in['fc_in_w'], 'L0_gnn_fc_in_b': _L0_gnn_in['fc_in_b'], 'L1_gnn_W': _L1_gnn_in['W'], 'L1_gnn_b_lin': _L1_gnn_in['b_lin'], 'L1_gnn_b': _L1_gnn_in['b'], 'L2_gnn_W1': _L2_gnn_in['W1'], 'L2_gnn_b1': _L2_gnn_in['b1'], 'L2_gnn_g1': _L2_gnn_in['g1'], 'L2_gnn_be1': _L2_gnn_in['be1'], 'L2_gnn_W2': _L2_gnn_in['W2'], 'L2_gnn_b2': _L2_gnn_in['b2'], 'L2_gnn_g2': _L2_gnn_in['g2'], 'L2_gnn_be2': _L2_gnn_in['be2'], 'L3_gnn_Wg0': _L3_gnn_in['Wg0'], 'L3_gnn_bg0': _L3_gnn_in['bg0'], 'L3_gnn_Wg1': _L3_gnn_in['Wg1'], 'L3_gnn_bg1': _L3_gnn_in['bg1'], 'L3_gnn_Wih': _L3_gnn_in['Wih'], 'L3_gnn_Whh': _L3_gnn_in['Whh'], 'L3_gnn_bih': _L3_gnn_in['bih'], 'L3_gnn_bhh': _L3_gnn_in['bhh']}

def reference(x, adj, L0_gnn_alpha_train, L0_gnn_w, L0_gnn_d, L0_gnn_fc_in_w, L0_gnn_fc_in_b, L1_gnn_W, L1_gnn_b_lin, L1_gnn_b, L2_gnn_W1, L2_gnn_b1, L2_gnn_g1, L2_gnn_be1, L2_gnn_W2, L2_gnn_b2, L2_gnn_g2, L2_gnn_be2, L3_gnn_Wg0, L3_gnn_bg0, L3_gnn_Wg1, L3_gnn_bg1, L3_gnn_Wih, L3_gnn_Whh, L3_gnn_bih, L3_gnn_bhh):
    import jax
    import jax.numpy as jnp

    def _L0_gnn_ref(x, adj_mx, alpha_train, w, d, fc_in_w, fc_in_b, vt):
        import jax, jax.numpy as jnp
        import numpy as np
        N_STEPS = 8
        SPATIAL_SCALE = 1.0
        x0 = jax.lax.stop_gradient(x)
        h = jnp.einsum('bnd,ed->bne', x, fc_in_w) + fc_in_b
        alph = jax.nn.sigmoid(alpha_train)[:, None]
        d_clamped = jnp.clip(d, 0.0, 1.0)
        w_eff = w * d_clamped @ w.T
        dt = jnp.float32(SPATIAL_SCALE / N_STEPS)

        def euler_step(h, _):
            ax = jnp.einsum('nm,bmd->bnd', adj_mx, h)
            f = alph * 0.5 * (ax - h) + h @ w_eff - h + x0
            return (h + dt * f, None)
        h, _ = jax.lax.scan(euler_step, h, None, length=N_STEPS)
        return h

    def _L1_gnn_ref(inputs, graph, W, b_lin, b):
        import jax, jax.numpy as jnp
        import numpy as np
        B, N, C, D = (8, 1024, 128, 128)
        NEG = -1e+16
        h = jnp.einsum('bnc,cd->bnd', inputs, W) + b_lin
        scores = jnp.einsum('bnd,bmd->bnm', h, h) * graph[None, :, :]
        scores = jnp.where(scores == 0.0, NEG, scores)
        attention = jax.nn.softmax(scores, axis=2)
        return jnp.einsum('bnm,bmd->bnd', attention, h) + b

    def _L2_gnn_ref(features, A, W1, b1, g1, be1, W2, b2, g2, be2):
        import jax, jax.numpy as jnp
        import numpy as np
        EPS = 1e-05

        def _batchnorm(x, gamma, beta):
            mu = jnp.mean(x, axis=0)
            var = jnp.var(x, axis=0)
            return (x - mu) * jax.lax.rsqrt(var + EPS) * gamma + beta
        b, n, d = features.shape
        A_norm = A + jnp.eye(n, dtype=A.dtype)
        deg = jnp.sum(A_norm, axis=0) + jnp.sum(A_norm, axis=1) - jnp.diagonal(A_norm)
        dinv = jax.lax.rsqrt(deg)
        A_hat = A_norm * dinv[:, None] * dinv[None, :]
        agg = jnp.einsum('nm,bmd->bnd', A_hat, features)
        x = agg.reshape(-1, d)
        h = jax.nn.relu(_batchnorm(x @ W1.T + b1, g1, be1))
        out = h @ W2.T + b2
        out = _batchnorm(out, g2, be2)
        return out.reshape(b, n, -1)

    def _L3_gnn_ref(x, adj, Wg0, bg0, Wg1, bg1, Wih, Whh, bih, bhh):
        import jax, jax.numpy as jnp
        import numpy as np
        B, T, D, H = (64, 1024, 128, 128)
        MAX_SKIP = 4

        def _lstm_last(Wih, Whh, bih, bhh, xs):
            N, _, Hd = xs.shape
            bias = bih + bhh

            def step(carry, x_t):
                h, c = carry
                g = x_t @ Wih.T + h @ Whh.T + bias
                i, f, gg, o = jnp.split(g, 4, axis=-1)
                c = jax.nn.sigmoid(f) * c + jax.nn.sigmoid(i) * jnp.tanh(gg)
                h = jax.nn.sigmoid(o) * jnp.tanh(c)
                return ((h, c), None)
            init = (jnp.zeros((N, Hd), xs.dtype), jnp.zeros((N, Hd), xs.dtype))
            (h_last, _), _ = jax.lax.scan(step, init, jnp.swapaxes(xs, 0, 1))
            return h_last
        h = jax.nn.relu(jnp.einsum('ts,bsh->bth', adj, x @ Wg0 + bg0))
        h = jax.nn.relu(jnp.einsum('ts,bsh->bth', adj, h @ Wg1 + bg1))
        Bv, Tv, Hd = h.shape
        for p in range(1, MAX_SKIP + 1):
            nw = Tv // p
            wins = h[:, :nw * p, :].reshape(Bv * nw, p, Hd)
            last = _lstm_last(Wih[p - 1], Whh[p - 1], bih[p - 1], bhh[p - 1], wins)
            idx = jnp.arange(nw) * p + (p - 1)
            h = h.at[:, idx, :].set(last.reshape(Bv, nw, Hd))
        return h
    h = jnp.maximum(_layernorm(x, axis=-1), 0.0)
    x = x + _L0_gnn_ref(h, adj, L0_gnn_alpha_train, L0_gnn_w, L0_gnn_d, L0_gnn_fc_in_w, L0_gnn_fc_in_b, 0)
    h = jnp.maximum(_layernorm(x, axis=-1), 0.0)
    x = x + _L1_gnn_ref(h, adj, L1_gnn_W, L1_gnn_b_lin, L1_gnn_b)
    h = jnp.maximum(_layernorm(x, axis=-1), 0.0)
    x = x + _L2_gnn_ref(h, adj, L2_gnn_W1, L2_gnn_b1, L2_gnn_g1, L2_gnn_be1, L2_gnn_W2, L2_gnn_b2, L2_gnn_g2, L2_gnn_be2)
    h = jnp.maximum(_layernorm(x, axis=-1), 0.0)
    x = x + _L3_gnn_ref(h, adj, L3_gnn_Wg0, L3_gnn_bg0, L3_gnn_Wg1, L3_gnn_bg1, L3_gnn_Wih, L3_gnn_Whh, L3_gnn_bih, L3_gnn_bhh)
    return x

_drawn_inputs = setup_inputs


def setup_inputs(seed=0):
    import zlib

    import numpy as np

    out = dict(_drawn_inputs(seed))
    spreads = {'L0_gnn_alpha_train': (1.0, 0.6),
     'L0_gnn_fc_in_b': (0.0, 0.276),
     'L2_gnn_b1': (0.0, 0.8),
     'L2_gnn_g1': (1.0, 0.2),
     'L2_gnn_be1': (0.0, 0.1),
     'L2_gnn_b2': (0.0, 0.8),
     'L2_gnn_g2': (1.0, 0.2),
     'L2_gnn_be2': (0.0, 0.1),
     'L3_gnn_bg0': (0.0, 0.8),
     'L3_gnn_bg1': (0.0, 0.8)}
    factors = {'L1_gnn_b_lin': 5.153,
     'L3_gnn_Wg0': 8.0,
     'L3_gnn_Wg1': 8.0,
     'L3_gnn_Wih': 8.0,
     'L3_gnn_Whh': 8.0,
     'L3_gnn_bih': 6.133,
     'L3_gnn_bhh': 6.228}
    for name, (base, spread) in spreads.items():
        noise = np.random.default_rng([zlib.crc32(name.encode()), seed]).standard_normal(out[name].shape)
        drawn = base * np.exp(spread * noise) if base else spread * noise
        out[name] = jnp.asarray(drawn.astype(out[name].dtype))
    for name, factor in factors.items():
        out[name] = (out[name] * factor).astype(out[name].dtype)
    return out
```

```python
from contextlib import ExitStack
from math import comb

import concourse.bass as bass
from concourse import mybir
from concourse.alu_op_type import AluOpType as ALU

ACT = mybir.ActivationFunctionType
AX = mybir.AxisListType
F32 = mybir.dt.float32
F32R = mybir.dt.float32r

P = 128
STEPS = 8
DT = 1.0 / STEPS
LN_EPS = 1e-5
BN_EPS = 1e-5
MASKED = -1e16
SPLIT = 3
PAIR = 2


class Split:

    def __init__(self, hi, lo):
        self.hi, self.lo = hi, lo

    def __getitem__(self, key):
        return Split(self.hi[key], self.lo[key])

    def view(self, pattern, **sizes):
        return Split(self.hi.rearrange(pattern, **sizes), self.lo.rearrange(pattern, **sizes))


def as_f32(ap):
    return ap.bitcast(F32)


def split_matmul(pe, out, w, x, start, stop, shared=False):
    pe.matmul(out, w.hi, x.hi, start=start, stop=False, skip_group_check=shared)
    pe.matmul(out, w.hi, x.lo, start=False, stop=False, skip_group_check=shared)
    return pe.matmul(out, w.lo, x.hi, start=False, stop=stop, skip_group_check=shared)


def wait_some(eng, sem, value):
    if not isinstance(value, int) or value > 0:
        eng.wait_ge(sem, value)


def apart(eng, passed):
    eng.sem_inc(passed)


def build(nc, x, adj, alpha, w, d, fc_w, fc_b, l1_w, l1_blin, l1_b, w1, b1, g1, be1, w2, b2, g2, be2,
          wg0, bg0, wg1, bg1, wih, whh, bih, bhh, out):
    B, N, D = x.shape
    KT = N // P
    PAIRS = B // PAIR
    HID = w1.shape[0] // P
    SKIP = wih.shape[0]
    GATES = 4
    assert D == P and PAIR == 2 and KT == 4 and HID == 2 and SKIP == 4

    x_rows = x.rearrange("b (k p) d -> b p k d", p=P)
    out_rows = out.rearrange("b (k p) d -> b p k d", p=P)

    top = ExitStack()
    with top:
        def sb(ctx, name, shape, dt=F32):
            return ctx.enter_context(nc.sbuf_tensor(name, shape, dt))[:]

        def sb_split(ctx, name, shape):
            return Split(sb(ctx, name + "_hi", shape, F32R), sb(ctx, name + "_lo", shape, F32R))

        def sem(name):
            return top.enter_context(nc.semaphore(name))

        bank_a = [top.enter_context(nc.psum_tensor(f"bank_a{i}", [P, 512], F32))[:] for i in range(4)]
        bank_b = [top.enter_context(nc.psum_tensor(f"bank_b{i}", [P, 512], F32))[:] for i in range(4)]

        X = sb(top, "X", [P, KT, B, D])
        ident = sb(top, "ident", [P, P])
        pow_half = sb(top, "pow_half", [P, 8])
        passed = sem("passed")
        adj_rows = sb(top, "adj_rows", [P, KT, N])

        phase_a(nc, sb, sb_split, sem, passed, bank_a, bank_b, X, ident, pow_half, adj_rows, x_rows, adj,
                alpha, w, d, fc_w, fc_b, l1_w, l1_blin, l1_b, B, N, D, KT, PAIRS)
        at = sb_split(top, "at", [P, KT, N])
        Y2 = sb(top, "Y2", [P, B, N])
        bn2 = sb(top, "bn2", [P, 2])
        phase_b(nc, sb, sb_split, sem, passed, bank_a, bank_b, X, ident, pow_half, adj_rows, at, Y2, bn2,
                w1, b1, g1, be1, w2, b2, g2, be2, B, N, D, KT, PAIRS, HID)
        phase_c(nc, sb, sb_split, sem, passed, bank_a, bank_b, X, ident, pow_half, at, Y2, bn2,
                wg0, bg0, wg1, bg1, wih, whh, bih, bhh, out_rows, B, N, D, KT, PAIRS, SKIP, GATES)



class Norm:

    def __init__(self, sb, ctx, sem, passed, name, rows, KT):
        self.passed = passed
        self.stats = sb(ctx, name + "_stats", [P, PAIR * KT, 6])
        self.mv = sb(ctx, name + "_mv", [P, PAIR * KT, 2])
        self.var = sb(ctx, name + "_var", [P, PAIR * KT])
        self.rstd = sb(ctx, name + "_rstd", [P, PAIR * KT])
        self.rows = rows
        self.KT = KT
        self.has_stats, self.has_mv, self.has_var = sem(name + "_has_stats"), sem(name + "_has_mv"), sem(name + "_has_var")
        self.has_rstd, self.has_rows = sem(name + "_has_rstd"), sem(name + "_has_rows")

    def dve(self, dve, X, pair, n):
        tiles = [(k, b) for k in range(self.KT) for b in range(PAIR)]
        apart(dve, self.passed)
        for t, (k, b) in enumerate(tiles):
            last = dve.bn_stats(self.stats[:, t, :], X[:, k, bass.ds(pair * PAIR + b, 1), :].rearrange("p a d -> p (a d)"))
        last.then_inc(self.has_stats, 1)
        dve.wait_ge(self.has_stats, n + 1)
        apart(dve, self.passed)
        for t in range(len(tiles)):
            last = dve.bn_aggr(self.mv[:, t, :], self.stats[:, t, :])
        last.then_inc(self.has_mv, 1)
        dve.wait_ge(self.has_mv, n + 1)
        dve.tensor_scalar(self.var[:, :], self.mv[:, :, 1], LN_EPS, None, ALU.add).then_inc(self.has_var, 1)
        dve.wait_ge(self.has_rstd, n + 1)
        for t, (k, b) in enumerate(tiles):
            last = dve.tensor_scalar(self.rows[:, k, b, :], X[:, k, bass.ds(pair * PAIR + b, 1), :].rearrange("p a d -> p (a d)"),
                                     self.mv[:, t, 0:1], self.rstd[:, t:t + 1], ALU.subtract, ALU.mult)
        last.then_inc(self.has_rows, 1)

    def pool(self, pool, pow_half, n):
        pool.wait_ge(self.has_var, n + 1)
        pool.tensor_tensor(self.rstd[:, :], self.var[:, :], pow_half[:, :], ALU.pow).then_inc(self.has_rstd, 1)



def phase_a(nc, sb, sb_split, sem, passed, bank_a, bank_b, X, ident, pow_half, adj_rows, x_rows, adj,
            alpha, w, d, fc_w, fc_b, l1_w, l1_blin, l1_b, B, N, D, KT, PAIRS):
    ctx = ExitStack()
    with ctx:
        m_t = [None] + [sb_split(ctx, f"m{i}_t", [P, KT, N]) for i in (1, 2, 3)]
        R = sb_split(ctx, "R", [P, STEPS + 1, D])
        g_bias = sb(ctx, "g_bias", [P, SPLIT, KT, D])
        w_l1 = sb_split(ctx, "w_l1", [P, D])
        blin_col = sb(ctx, "blin_col", [P, 1])
        b_row = sb(ctx, "b_row", [P, D])

        x_in, adj_in, small_in = sem("x_in"), sem("adj_in"), sem("small_in")

        with ExitStack() as tmp:
            w_raw = sb(tmp, "w_raw", [P, D])
            fc_raw = sb(tmp, "fc_raw", [P, D])
            l1_raw = sb(tmp, "l1_raw", [P, D])
            d_col = sb(tmp, "d_col", [P, 1])
            fcb_col = sb(tmp, "fcb_col", [P, 1])
            alpha_col = sb(tmp, "alpha_col", [P, KT])
            gain = sb(tmp, "gain", [P, KT])
            keep = sb(tmp, "keep", [P, KT])
            w_t = sb(tmp, "w_t", [P, D])
            wd_t = sb(tmp, "wd_t", [P, D])
            b_wide = sb(tmp, "b_wide", [P, D])
            v1 = sb(tmp, "v1", [P, D])
            powers = sb(tmp, "powers", [P, STEPS + 1, 3, D])
            r_sum = sb(tmp, "r_sum", [P, STEPS + 1, D])
            r_bias = sb(tmp, "r_bias", [P, STEPS + 1, D])
            m_rows = sb(tmp, "m_rows", [P, KT, N])
            m_split = sb_split(tmp, "m_split", [P, KT, N])
            ones = sb(tmp, "ones", [P, 2], F32R)
            ones_f = sb(tmp, "ones_f", [P, 2])
            u = sb(tmp, "u", [P, 2, KT])

            has_ident, has_exp = sem("has_ident"), sem("has_exp")
            has_m_rows, m_rows_hi = sem("has_m_rows"), sem("m_rows_hi")
            has_m_split = sem("has_m_split")
            has_const = sem("has_const")
            v_filled, v_drained = sem("v_filled"), sem("v_drained")
            m_filled, m_hi, m_drained = sem("m_filled"), sem("m_hi"), sem("m_drained")
            u_filled, link_s, r_hi = sem("u_filled"), sem("setup_link"), sem("r_hi")
            r_full, w_hi = sem("r_full"), sem("w_l1_hi")
            block = tmp.enter_context(nc.Block())

            @block.sync
            def _(sp):
                with nc.allow_non_contiguous_dma(reason="parameter columns"):
                    sp.dma_start(w_raw[:, :], w).then_inc(small_in, 16)
                    sp.dma_start(d_col[:, :], d.rearrange("(p a) -> p a", a=1)).then_inc(small_in, 16)
                    sp.dma_start(alpha_col[:, :], alpha.rearrange("(k p) -> p k", p=P)).then_inc(small_in, 16)
                    sp.dma_start(adj_rows[:, :, :], adj.rearrange("(k p) n -> p k n", p=P)).then_inc(adj_in, 16)
                    sp.dma_start(fc_raw[:, :], fc_w).then_inc(small_in, 16)
                    sp.dma_start(fcb_col[:, :], fc_b.rearrange("(p a) -> p a", a=1)).then_inc(small_in, 16)
                    sp.dma_start(l1_raw[:, :], l1_w).then_inc(small_in, 16)
                    sp.dma_start(blin_col[:, :], l1_blin.rearrange("(p a) -> p a", a=1)).then_inc(small_in, 16)
                    sp.dma_start(b_row[:, :], l1_b.partition_broadcast(P)).then_inc(small_in, 16)
                with sp.Fori(0, B) as b:
                    sp.dma_start(X[:, :, bass.ds(b, 1), :].rearrange("p k a d -> p k (a d)"),
                                 x_rows[bass.ds(b, 1)].rearrange("a p k d -> p k (a d)")).then_inc(x_in, 16)

            @block.gpsimd
            def _(pool):
                pool.memset(pow_half[:, :], -0.5)
                pool.memset(ident[:, :], 0.0).then_inc(has_ident, 1)
                pool.wait_ge(has_ident, 1)
                pool.affine_select(out=ident[:, :], in_=ident[:, :], compare_op=ALU.not_equal, fill=1.0,
                                   base=0, pattern=[[-1, P]], channel_multiplier=1).then_inc(has_ident, 1)

            @block.scalar
            def _(act):
                act.wait_ge(small_in, 8 * 16)
                act.activation(gain[:, :], alpha_col[:, :], ACT.Exp, scale=-1.0).then_inc(has_exp, 1)
                act.activation(w_l1.hi[:, :], l1_raw[:, :], ACT.Copy).then_inc(w_hi, 1)
                for k in range(KT):
                    act.wait_ge(has_m_rows, k + 1)
                    act.activation(m_split.hi[:, k, :], m_rows[:, k, :], ACT.Copy).then_inc(m_rows_hi, 1)
                for f in range(3 * KT):
                    act.wait_ge(m_filled, f + 1)
                    act.activation(m_t[f // KT + 1].hi[:, f % KT, :], bank_a[f % 4][:, :], ACT.Copy).then_inc(m_hi, 1)
                act.wait_ge(r_full, 1)
                act.activation(R.hi[:, :, :], r_sum[:, :, :], ACT.Copy).then_inc(r_hi, 1)

            @block.tensor
            def _(pe):
                pe.wait_ge(small_in, 8 * 16)
                pe.wait_ge(has_ident, 2)
                pe.transpose(bank_b[2][:, 0:D], w_raw[:, :], ident[:, :]).then_inc(v_filled, 1)
                pe.wait_ge(v_drained, 1)
                pe.matmul(bank_b[3][:, 0:D], wd_t[:, :], w_t[:, :], start=True, stop=True).then_inc(v_filled, 1)

                def v_round(i):
                    pe.wait_ge(v_drained, i + 2)
                    rhs = ident[:, :] if i == 0 else powers[:, i - 1, 0, :]
                    for n, lhs in enumerate((v1, fc_raw, b_wide)):
                        last = pe.matmul(bank_b[i % 2][:, n * D:(n + 1) * D], lhs[:, :], rhs, start=True, stop=True)
                    last.then_inc(v_filled, 1)

                def m_fill(f):
                    power, mt = f // KT + 1, f % KT
                    if f >= 4:
                        pe.wait_ge(m_drained, f - 3)
                    if power == 1:
                        for nt in range(KT):
                            last = pe.transpose(bank_a[f % 4][:, nt * P:(nt + 1) * P],
                                                m_rows[:, nt, mt * P:(mt + 1) * P], ident[:, :])
                    else:
                        pe.wait_ge(m_drained, KT * (power - 1))
                        for kt in range(KT):
                            last = split_matmul(pe, bank_a[f % 4][:, :], m_split[:, kt, mt * P:(mt + 1) * P],
                                                m_t[power - 1][:, kt, :], kt == 0, kt == KT - 1)
                    last.then_inc(m_filled, 1)

                pe.wait_ge(has_m_rows, KT)
                v_round(0)
                for f in range(KT):
                    m_fill(f)
                pe.wait_ge(has_m_split, 1)
                for f in range(KT, 3 * KT):
                    v_round(f - KT + 1)
                    m_fill(f)
                for nt in range(KT):
                    for n, part in enumerate((m_t[2].hi, m_t[2].lo)):
                        for kt in range(KT):
                            last = pe.matmul(bank_b[2][:, 2 * nt:2 * nt + 2], part[:, kt, nt * P:(nt + 1) * P], ones[:, :],
                                             start=(n == 0 and kt == 0), stop=(n == 1 and kt == KT - 1))
                last.then_inc(u_filled, 1)

            @block.vector
            def _(dve):
                done = [0]

                def link(ins):
                    done[0] += 1
                    ins.then_inc(link_s, 1)
                    dve.wait_ge(link_s, done[0])

                link(dve.memset(ones_f[:, :], 1.0))
                dve.tensor_copy(ones[:, :], ones_f[:, :])
                dve.wait_ge(small_in, 8 * 16)
                link(dve.tensor_scalar(d_col[:, :], d_col[:, :], 0.0, 1.0, ALU.max, ALU.min))
                dve.tensor_copy(b_wide[:, :], fcb_col[:, 0:1].to_broadcast([P, D]))
                dve.wait_ge(has_exp, 1)
                link(dve.tensor_scalar(gain[:, :], gain[:, :], 1.0, None, ALU.add))
                link(dve.reciprocal(gain[:, :], gain[:, :]))
                link(dve.tensor_scalar(gain[:, :], gain[:, :], 0.5 * DT, None, ALU.mult))
                link(dve.tensor_scalar(keep[:, :], gain[:, :], -1.0, 1.0 - DT, ALU.mult, ALU.add))
                dve.wait_ge(v_filled, 1)
                dve.tensor_copy(w_t[:, :], bank_b[2][:, 0:D])
                dve.tensor_scalar(wd_t[:, :], bank_b[2][:, 0:D], d_col[:, 0:1], None, ALU.mult).then_inc(v_drained, 1)
                dve.wait_ge(adj_in, 16)
                dve.wait_ge(has_ident, 2)
                for k in range(KT):
                    link(dve.tensor_scalar(m_rows[:, k, :], adj_rows[:, k, :], gain[:, k:k + 1], None, ALU.mult))
                    blk = m_rows[:, k, k * P:(k + 1) * P]
                    dve.scalar_tensor_tensor(blk, ident[:, :], keep[:, k:k + 1], blk, ALU.mult, ALU.add).then_inc(has_m_rows, 1)
                dve.wait_ge(v_filled, 2)
                dve.tensor_scalar(v1[:, :], bank_b[3][:, 0:D], DT, None, ALU.mult).then_inc(v_drained, 1)
                for k in range(KT):
                    dve.wait_ge(m_rows_hi, k + 1)
                    last = dve.tensor_tensor(m_split.lo[:, k, :], m_rows[:, k, :], as_f32(m_split.hi[:, k, :]), ALU.subtract)
                last.then_inc(has_m_split, 1)

                def v_drain(i):
                    dve.wait_ge(v_filled, i + 3)
                    dve.tensor_copy(powers[:, i, :, :], bank_b[i % 2][:, 0:3 * D].rearrange("p (a d) -> p a d", a=3)).then_inc(v_drained, 1)

                def m_drain(f):
                    dve.wait_ge(m_hi, f + 1)
                    dve.tensor_tensor(m_t[f // KT + 1].lo[:, f % KT, :], bank_a[f % 4][:, :],
                                      as_f32(m_t[f // KT + 1].hi[:, f % KT, :]), ALU.subtract).then_inc(m_drained, 1)

                v_drain(0)
                for f in range(KT):
                    m_drain(f)
                for f in range(KT, 3 * KT):
                    v_drain(f - KT + 1)
                    m_drain(f)
                dve.wait_ge(v_drained, STEPS + 3)
                for k in range(STEPS + 1):
                    dve.tensor_scalar(r_bias[:, k, :], powers[:, STEPS - k, 2, :], float(comb(STEPS, k)), None, ALU.mult)
                    ins = dve.tensor_scalar(r_sum[:, k, :], powers[:, STEPS - k, 1, :], float(comb(STEPS, k)), None, ALU.mult)
                    if k == STEPS:
                        ins.then_inc(r_full, 1)
                        break
                    link(ins)
                    for i in range(STEPS - k):
                        v_i = ident[:, :] if i == 0 else powers[:, i - 1, 0, :]
                        link(dve.scalar_tensor_tensor(r_sum[:, k, :], v_i, DT * comb(k + i, k), r_sum[:, k, :], ALU.mult, ALU.add))
                link(dve.tensor_reduce(u[:, 0, :], m_rows[:, :, :], AX.X, ALU.add))
                dve.wait_ge(u_filled, 1)
                link(dve.tensor_copy(u[:, 1, :], bank_b[2][:, 0:2 * KT].rearrange("p (k a) -> p k a", a=2)[:, :, 0]))
                for j in range(SPLIT):
                    for nt in range(KT):
                        dst = g_bias[:, j, nt, :]
                        link(dve.scalar_tensor_tensor(dst, r_bias[:, SPLIT * j + 1, :], u[:, 0, nt:nt + 1],
                                                      r_bias[:, SPLIT * j, :], ALU.mult, ALU.add))
                        link(dve.scalar_tensor_tensor(dst, r_bias[:, SPLIT * j + 2, :], u[:, 1, nt:nt + 1], dst, ALU.mult, ALU.add))
                dve.wait_ge(w_hi, 1)
                dve.tensor_tensor(w_l1.lo[:, :], l1_raw[:, :], as_f32(w_l1.hi[:, :]), ALU.subtract)
                dve.wait_ge(r_hi, 1)
                dve.tensor_tensor(R.lo[:, :, :], r_sum[:, :, :], as_f32(R.hi[:, :, :]), ALU.subtract)

        rows = sb(ctx, "rows", [P, KT, PAIR, D])
        x0 = sb_split(ctx, "x0", [P, KT, PAIR, D])
        x_t = sb_split(ctx, "x_t", [P, SPLIT, PAIR, N])
        g_two = sb_split(ctx, "g_two", [P, KT, PAIR, D])
        g_one = x0
        g_full = sb(ctx, "g_full", [P, KT, PAIR, D])
        hn_t = sb_split(ctx, "hn_t", [P, PAIR, N])
        h_t = sb_split(ctx, "h_t", [P, PAIR, N])
        scores = sb(ctx, "scores", [P, KT, N])
        h_full = scores
        probs = sb(ctx, "probs", [P, KT, N])
        probs_t = sb_split(ctx, "probs_t", [P, KT, N])
        neg_max = sb(ctx, "neg_max", [P, PAIR, KT])
        row_sum = sb(ctx, "row_sum", [P, PAIR, KT])
        inv_sum = sb(ctx, "inv_sum", [P, PAIR, KT])
        h_rows = hn_t.view("p b (k d) -> p b k d", k=KT)

        ln0 = Norm(sb, ctx, sem, passed, "ln0", rows, KT)
        ln1 = Norm(sb, ctx, sem, passed, "ln1", rows, KT)
        x0_hi, x0_lo = sem("x0_hi"), sem("x0_lo")
        a_filled, a_hi, a_drained = sem("a_filled"), sem("a_hi"), sem("a_drained")
        g_hi, g_lo, x1_done = sem("g_hi"), sem("g_lo"), sem("x1_done")
        b_filled, b_hi, b_drained, b_full = sem("b_filled"), sem("b_hi"), sem("b_drained"), sem("b_full")
        has_xb, has_neg, has_mask, has_probs = sem("has_xb"), sem("has_neg"), sem("has_mask"), sem("has_probs")
        has_inv = sem("has_inv")

        A = 12
        C = 24
        SCORES, PROBS, OUT = (6, 15), (10, 19), (14, 23)

        with nc.Block() as block:
            @block.tensor
            def _(pe):
                def a_slot(i, f):
                    pe.wait_ge(a_drained, A * i + f + 1)
                    return bank_a[f % 4]

                def c_slot(j, f):
                    pe.wait_ge(b_drained, C * j + f + 1)
                    return bank_b[f % 4]

                def transposes(i):
                    pe.wait_ge(ln0.has_rows, i + 1)
                    for b in range(PAIR):
                        bank = a_slot(i, b)
                        for k in range(KT):
                            last = pe.transpose(bank[:, k * P:(k + 1) * P], rows[:, k, b, :], ident[:, :])
                        last.then_inc(a_filled, 1)

                def m_powers(i, b):
                    pe.wait_ge(x0_lo, i + 1)
                    for q in (1, 2):
                        f = 2 + 2 * b + q - 1
                        bank = a_slot(i, f)
                        for k in range(KT):
                            last = split_matmul(pe, bank[:, :], x0[:, k, b, :], m_t[q][:, k, :], k == 0, k == KT - 1)
                        last.then_inc(a_filled, 1)

                def g_term(i, j):
                    for half in range(2):
                        f = 6 + 2 * (SPLIT - 1 - j) + half
                        bank = a_slot(i, f)
                        if half == 0 and j == SPLIT - 1:
                            pe.wait_ge(a_drained, A * i + 5 + 5)
                        for n in range(2):
                            nt = 2 * half + n
                            for b in range(PAIR):
                                for q in range(SPLIT):
                                    last = split_matmul(
                                        pe, bank[:, (PAIR * n + b) * D:(PAIR * n + b + 1) * D],
                                        x_t[:, q, b, nt * P:(nt + 1) * P], R[:, SPLIT * j + q, :],
                                        n == 0 and b == 0 and q == 0, j == SPLIT - 1 and q == SPLIT - 1, shared=True)
                        if j < SPLIT - 1:
                            if half == 0:
                                pe.wait_ge(g_lo, 4 * i + 2 * (SPLIT - 1 - j))
                            src = (g_two if j == 1 else g_one).view("p k b d -> p k (b d)")
                            for n in range(2):
                                nt = 2 * half + n
                                for k in range(KT):
                                    last = split_matmul(pe, bank[:, PAIR * n * D:PAIR * (n + 1) * D],
                                                        m_t[3][:, k, nt * P:(nt + 1) * P], src[:, k, :],
                                                        False, k == KT - 1, shared=True)
                        last.then_inc(a_filled, 1)

                def in_transposes(j):
                    pe.wait_ge(ln1.has_rows, j + 1)
                    for b in range(PAIR):
                        bank = c_slot(j, b)
                        for k in range(KT):
                            last = pe.transpose(bank[:, k * P:(k + 1) * P], rows[:, k, b, :], ident[:, :])
                        last.then_inc(b_filled, 1)

                def project(j):
                    for b in range(PAIR):
                        bank = c_slot(j, 2 + b)
                        pe.wait_ge(b_drained, C * j + b + 5)
                        split_matmul(pe, bank[:, :], w_l1, hn_t[:, b, :], True, True).then_inc(b_filled, 1)

                def h_transposes(j):
                    for b in range(PAIR):
                        bank = c_slot(j, 4 + b)
                        pe.wait_ge(b_full, PAIR * j + b + 1)
                        for k in range(KT):
                            last = pe.transpose(bank[:, k * P:(k + 1) * P], h_full[:, b, k * P:(k + 1) * P], ident[:, :])
                        last.then_inc(b_filled, 1)

                def score(j, b):
                    pe.wait_ge(b_drained, C * j + 2 + b + 5)
                    for nt in range(KT):
                        bank = c_slot(j, SCORES[b] + nt)
                        split_matmul(pe, bank[:, :], h_t[:, b, nt * P:(nt + 1) * P], h_t[:, b, :], True, True).then_inc(b_filled, 1)

                def attend(j, b):
                    pe.wait_ge(has_probs, 2 * KT * j + KT * b + KT)
                    for kt in range(KT):
                        bank = c_slot(j, PROBS[b] + kt)
                        for nt in range(KT):
                            last = pe.transpose(bank[:, nt * P:(nt + 1) * P], probs[:, nt, kt * P:(kt + 1) * P], ident[:, :])
                        last.then_inc(b_filled, 1)

                def attend_out(j, b):
                    bank = c_slot(j, OUT[b])
                    pe.wait_ge(b_drained, C * j + PROBS[b] + KT - 1 + 5)
                    for nt in range(KT):
                        for kt in range(KT):
                            last = split_matmul(pe, bank[:, nt * D:(nt + 1) * D], probs_t[:, kt, nt * P:(nt + 1) * P],
                                                h_rows[:, b, kt, :], kt == 0, kt == KT - 1)
                    last.then_inc(b_filled, 1)

                def turn(i, zero, one):
                    j = i - 1
                    if zero:
                        transposes(i)
                        m_powers(i, 0)
                    if one:
                        in_transposes(j)
                    if zero:
                        m_powers(i, 1)
                    if one:
                        project(j)
                    if zero:
                        g_term(i, 2)
                    if one:
                        h_transposes(j)
                        score(j, 0)
                    if zero:
                        g_term(i, 1)
                    if one:
                        attend(j, 0)
                        attend_out(j, 0)
                        score(j, 1)
                    if zero:
                        g_term(i, 0)
                    if one:
                        attend(j, 1)
                        attend_out(j, 1)

                turn(0, True, False)
                with pe.Fori(1, PAIRS) as i:
                    turn(i, True, True)
                turn(PAIRS, False, True)

            @block.scalar
            def _(act):
                def split_x0(i):
                    act.wait_ge(ln0.has_rows, i + 1)
                    if not isinstance(i, int) or i > 0:
                        act.wait_ge(a_filled, A * i)
                    act.activation(x0.hi[:, :, :, :], rows[:, :, :, :], ACT.Relu).then_inc(x0_hi, 1)

                def a_round(i, f):
                    act.wait_ge(a_filled, A * i + f + 1)
                    q, b = (0, f) if f < 2 else ((f - 2) % 2 + 1, (f - 2) // 2)
                    act.activation(x_t.hi[:, q, b, :], bank_a[f % 4][:, :], ACT.Relu if f < 2 else ACT.Copy).then_inc(a_hi, 1)

                def g_round(i, j):
                    for half in range(2):
                        act.wait_ge(a_drained, A * i + 6 + 2 * (SPLIT - 1 - j) + half + 5)
                        dst = g_two if j == 2 else g_one
                        act.activation(dst.hi[:, 2 * half:2 * half + 2, :, :], g_full[:, 2 * half:2 * half + 2, :, :],
                                       ACT.Copy).then_inc(g_hi, 1)

                def c_round(j, f, dst, func=ACT.Copy):
                    act.wait_ge(b_filled, C * j + f + 1)
                    act.activation(dst, bank_b[f % 4][:, :], func).then_inc(b_hi, 1)

                def project(j):
                    for b in range(PAIR):
                        act.wait_ge(b_filled, C * j + 2 + b + 1)
                        act.activation(h_full[:, b, :], bank_b[2 + b][:, :], ACT.Identity, bias=blin_col[:, 0:1]).then_inc(b_full, 1)
                        act.activation(h_t.hi[:, b, :], bank_b[2 + b][:, :], ACT.Identity, bias=blin_col[:, 0:1]).then_inc(b_hi, 1)

                def exponentials(j, b):
                    for nt in range(KT):
                        act.wait_ge(has_neg, 2 * KT * j + KT * b + nt + 1)
                        act.activation(probs[:, nt, :], scores[:, nt, :], ACT.Exp, bias=neg_max[:, b, nt:nt + 1], scale=-1.0,
                                       accum_out=row_sum[:, b, nt:nt + 1]).then_inc(has_probs, 1)

                def round_probs(j, b):
                    for kt in range(KT):
                        c_round(j, PROBS[b] + kt, probs_t.hi[:, kt, :])

                def turn(i, zero, one, ahead):
                    j = i - 1
                    if zero:
                        for f in range(4):
                            a_round(i, f)
                    if one:
                        for b in range(PAIR):
                            c_round(j, b, hn_t.hi[:, b, :], ACT.Relu)
                    if zero:
                        for f in (4, 5):
                            a_round(i, f)
                    if one:
                        project(j)
                    if zero:
                        g_round(i, 2)
                    if one:
                        for b in range(PAIR):
                            c_round(j, 4 + b, hn_t.hi[:, b, :])
                        exponentials(j, 0)
                    if zero:
                        g_round(i, 1)
                    if one:
                        round_probs(j, 0)
                        exponentials(j, 1)
                    if ahead:
                        split_x0(i + 1)
                    if one:
                        round_probs(j, 1)

                split_x0(0)
                turn(0, True, False, True)
                with act.Fori(1, PAIRS - 1) as i:
                    turn(i, True, True, True)
                turn(PAIRS - 1, True, True, False)
                turn(PAIRS, False, True, False)

            @block.gpsimd
            def _(pool):
                def add_b(j):
                    pool.wait_ge(ln1.has_rows, j + 1)
                    for b in range(PAIR):
                        xs = X[:, :, bass.ds(PAIR * j + b, 1), :].rearrange("p k a d -> p k (a d)")
                        last = pool.tensor_tensor(xs, xs, b_row[:, :].unsqueeze(1).to_broadcast([P, KT, D]), ALU.add)
                    last.then_inc(has_xb, 1)

                def g_rest(i, j):
                    dst = g_two if j == 2 else g_one
                    for half in range(2):
                        s = slice(2 * half, 2 * half + 2)
                        pool.wait_ge(g_hi, 4 * i + 2 * (SPLIT - 1 - j) + half + 1)
                        pool.tensor_tensor(dst.lo[:, s, :, :], g_full[:, s, :, :], as_f32(dst.hi[:, s, :, :]),
                                           ALU.subtract).then_inc(g_lo, 1)

                def masks(j, b):
                    for nt in range(KT):
                        pool.wait_ge(b_drained, C * j + SCORES[b] + nt + 5)
                        apart(pool, passed)
                        pool.tensor_scalar(probs[:, nt, :], scores[:, nt, :], 0.0, MASKED, ALU.is_equal, ALU.mult).then_inc(has_mask, 1)

                def residual(i):
                    for half in range(2):
                        pool.wait_ge(a_drained, A * i + 10 + half + 5)
                        s = slice(2 * half, 2 * half + 2)
                        xs = X[:, s, bass.ds(PAIR * i, PAIR), :]
                        pool.tensor_tensor(xs, xs, g_full[:, s, :, :], ALU.add).then_inc(x1_done, 1)

                def turn(i, zero, one, ahead):
                    j = i - 1
                    if one:
                        ln1.pool(pool, pow_half, j)
                        add_b(j)
                    if zero:
                        g_rest(i, 2)
                    if one:
                        masks(j, 0)
                    if ahead:
                        ln0.pool(pool, pow_half, i + 1)
                    if zero:
                        g_rest(i, 1)
                    if one:
                        masks(j, 1)
                    if zero:
                        residual(i)

                ln0.pool(pool, pow_half, 0)
                turn(0, True, False, True)
                with pool.Fori(1, PAIRS - 1) as i:
                    turn(i, True, True, True)
                turn(PAIRS - 1, True, True, False)
                turn(PAIRS, False, True, False)

            @block.vector
            def _(dve):
                def split_x0(i):
                    dve.wait_ge(x0_hi, i + 1)
                    flat = "p k b d -> p (k b d)"
                    dve.scalar_tensor_tensor(x0.lo[:, :, :, :].rearrange(flat), rows[:, :, :, :].rearrange(flat), 0.0,
                                             as_f32(x0.hi[:, :, :, :]).rearrange(flat), ALU.max, ALU.subtract).then_inc(x0_lo, 1)

                def a_rest(i, f):
                    dve.wait_ge(a_hi, 6 * i + f + 1)
                    q, b = (0, f) if f < 2 else ((f - 2) % 2 + 1, (f - 2) // 2)
                    bank = bank_a[f % 4]
                    if f < 2:
                        ins = dve.scalar_tensor_tensor(x_t.lo[:, q, b, :], bank[:, :], 0.0, as_f32(x_t.hi[:, q, b, :]),
                                                       ALU.max, ALU.subtract)
                    else:
                        ins = dve.tensor_tensor(x_t.lo[:, q, b, :], bank[:, :], as_f32(x_t.hi[:, q, b, :]), ALU.subtract)
                    ins.then_inc(a_drained, 1)

                def g_full_of(i, j):
                    stage = SPLIT - 1 - j
                    for half in range(2):
                        f = 6 + 2 * stage + half
                        dve.wait_ge(a_filled, A * i + f + 1)
                        if stage:
                            dve.wait_ge(g_lo, 4 * i + 2 * (stage - 1) + half + 1)
                        else:
                            wait_some(dve, x1_done, 2 * i + half - 1)
                        for n in range(2):
                            nt = 2 * half + n
                            last = dve.tensor_tensor(g_full[:, nt, :, :],
                                                     bank_a[f % 4][:, n * PAIR * D:(n + 1) * PAIR * D].rearrange("p (b d) -> p b d", b=PAIR),
                                                     g_bias[:, j, nt:nt + 1, :].to_broadcast([P, PAIR, D]), ALU.add)
                        last.then_inc(a_drained, 1)

                def c_rest(j, f, n, hi, lo, relu=False):
                    dve.wait_ge(b_hi, 14 * j + n + 1)
                    if relu:
                        ins = dve.scalar_tensor_tensor(lo, bank_b[f % 4][:, :], 0.0, as_f32(hi), ALU.max, ALU.subtract)
                    else:
                        ins = dve.tensor_tensor(lo, bank_b[f % 4][:, :], as_f32(hi), ALU.subtract)
                    ins.then_inc(b_drained, 1)

                def edges(j, b, nt):
                    dve.wait_ge(b_filled, C * j + SCORES[b] + nt + 1)
                    if b == 1:
                        dve.wait_ge(has_probs, 2 * KT * j + nt + 1)
                    dve.tensor_tensor(scores[:, nt, :], bank_b[(SCORES[b] + nt) % 4][:, :], adj_rows[:, nt, :],
                                      ALU.mult).then_inc(b_drained, 1)

                def maximum(j, b, nt):
                    dve.wait_ge(b_drained, C * j + SCORES[b] + nt + 5)
                    dve.wait_ge(has_mask, 2 * KT * j + KT * b + nt + 1)
                    apart(dve, passed)
                    dve.tensor_tensor_reduce(scores[:, nt, :], scores[:, nt, :], probs[:, nt, :], -1.0, 3.0e38,
                                             ALU.add, ALU.min, neg_max[:, b, nt:nt + 1]).then_inc(has_neg, 1)

                def softmax(j, b):
                    edges(j, b, 0)
                    for nt in range(1, KT):
                        edges(j, b, nt)
                        maximum(j, b, nt - 1)
                    maximum(j, b, KT - 1)

                def rest_of_probs(j, b):
                    dve.wait_ge(has_probs, 2 * KT * j + KT * b + KT)
                    dve.reciprocal(inv_sum[:, b, :], row_sum[:, b, :]).then_inc(has_inv, 1)
                    for kt in range(KT):
                        c_rest(j, PROBS[b] + kt, 6 + KT * b + kt, probs_t.hi[:, kt, :], probs_t.lo[:, kt, :])

                def attend_out(j, b):
                    if b == 0:
                        dve.wait_ge(has_xb, j + 1)
                    dve.wait_ge(has_inv, PAIR * j + b + 1)
                    dve.wait_ge(b_filled, C * j + OUT[b] + 1)
                    for nt in range(KT):
                        xs = X[:, nt, bass.ds(PAIR * j + b, 1), :].rearrange("p a d -> p (a d)")
                        last = dve.scalar_tensor_tensor(xs, bank_b[OUT[b] % 4][:, nt * D:(nt + 1) * D], inv_sum[:, b, nt:nt + 1],
                                                        xs, ALU.mult, ALU.add)
                    last.then_inc(b_drained, 1)

                def turn(i, zero, one, ahead):
                    j = i - 1
                    if zero:
                        for f in (0, 1):
                            a_rest(i, f)
                    if one:
                        dve.wait_ge(x1_done, 2 * j + 2)
                        ln1.dve(dve, X, j, j)
                    if zero:
                        for f in (2, 3):
                            a_rest(i, f)
                    if one:
                        for b in range(PAIR):
                            c_rest(j, b, b, hn_t.hi[:, b, :], hn_t.lo[:, b, :], relu=True)
                    if zero:
                        for f in (4, 5):
                            a_rest(i, f)
                    if one:
                        for b in range(PAIR):
                            dve.wait_ge(b_hi, 14 * j + 2 + b + 1)
                            dve.scalar_tensor_tensor(h_t.lo[:, b, :], bank_b[2 + b][:, :], blin_col[:, 0:1],
                                                     as_f32(h_t.hi[:, b, :]), ALU.add, ALU.subtract).then_inc(b_drained, 1)
                    if zero:
                        g_full_of(i, 2)
                    if one:
                        for b in range(PAIR):
                            c_rest(j, 4 + b, 4 + b, hn_t.hi[:, b, :], hn_t.lo[:, b, :])
                        softmax(j, 0)
                    if ahead:
                        ln0.dve(dve, X, i + 1, i + 1)
                    if zero:
                        g_full_of(i, 1)
                    if one:
                        rest_of_probs(j, 0)
                        attend_out(j, 0)
                        softmax(j, 1)
                    if zero:
                        g_full_of(i, 0)
                    if ahead:
                        split_x0(i + 1)
                    if one:
                        rest_of_probs(j, 1)
                        attend_out(j, 1)

                for _ in range(4):
                    dve.engine_nop().then_inc(a_drained, 1)
                    dve.engine_nop().then_inc(b_drained, 1)
                dve.wait_ge(x_in, 16 * B)
                ln0.dve(dve, X, 0, 0)
                split_x0(0)
                turn(0, True, False, True)
                with dve.Fori(1, PAIRS - 1) as i:
                    turn(i, True, True, True)
                turn(PAIRS - 1, True, True, False)
                turn(PAIRS, False, True, False)



def phase_b(nc, sb, sb_split, sem, passed, bank_a, bank_b, X, ident, pow_half, adj_rows, at, Y2, bn2,
            w1, b1, g1, be1, w2, b2, g2, be2, B, N, D, KT, PAIRS, HID):
    ctx = ExitStack()
    with ctx:
        Y1 = sb(ctx, "Y1", [P, HID, B, N])
        ah_t = sb_split(ctx, "ah_t", [P, KT, N])
        w1_t = sb_split(ctx, "w1_t", [P, HID * P])
        w2_t = sb_split(ctx, "w2_t", [P, HID, D])
        b1_col = sb(ctx, "b1_col", [P, HID])
        g1_col = sb(ctx, "g1_col", [P, HID])
        be1_col = sb(ctx, "be1_col", [P, HID])
        out_cols = sb(ctx, "out_cols", [P, 3])
        bn1 = sb(ctx, "bn1", [P, HID, 2])
        stats1 = sb(ctx, "stats1", [P, HID, B, 6])
        stats2 = sb(ctx, "stats2", [P, B, 6])
        mv = sb(ctx, "mv", [P, 3, 2])
        bn_var = sb(ctx, "bn_var", [P, 4])
        bn_rstd = sb(ctx, "bn_rstd", [P, 4])

        with ExitStack() as tmp:
            w1_raw = sb(tmp, "w1_raw", [P, HID, D])
            w2_raw = sb(tmp, "w2_raw", [P, HID * P])
            loops = sb(tmp, "loops", [P, KT, N])
            diag = sb(tmp, "diag", [P, KT])
            junk = sb(tmp, "junk", [P, KT, P])
            deg = sb(tmp, "deg", [P, KT])
            rows_sum = sb(tmp, "rows_sum", [P, KT])
            cols_sum = sb(tmp, "cols_sum", [P, KT])
            dinv = sb(tmp, "dinv", [P, KT])
            params_in = sem("l2_params_in")
            s_filled, s_hi, s_drained = sem("l2s_filled"), sem("l2s_hi"), sem("l2s_drained")
            has_deg, has_dinv, has_loops, link_s = sem("has_deg"), sem("has_dinv"), sem("has_loops"), sem("l2_link")

            with nc.Block() as block:
                @block.sync
                def _(sp):
                    with nc.allow_non_contiguous_dma(reason="parameter columns"):
                        sp.dma_start(w1_raw[:, :, :], w1.rearrange("(a p) d -> p a d", p=P)).then_inc(params_in, 16)
                        sp.dma_start(w2_raw[:, :], w2).then_inc(params_in, 16)
                        for dst, src in ((b1_col, b1), (g1_col, g1), (be1_col, be1)):
                            sp.dma_start(dst[:, :], src.rearrange("(a p) -> p a", p=P)).then_inc(params_in, 16)
                        for n, src in enumerate((b2, g2, be2)):
                            sp.dma_start(out_cols[:, n:n + 1], src.rearrange("(p a) -> p a", a=1)).then_inc(params_in, 16)

                @block.gpsimd
                def _(pool):
                    pool.wait_ge(has_deg, 1)
                    pool.tensor_tensor(dinv[:, :], deg[:, :], pow_half[:, 0:KT], ALU.pow).then_inc(has_dinv, 1)

                @block.tensor
                def _(pe):
                    banks = bank_a + bank_b
                    for f in range(4):
                        for nt in range(KT):
                            last = pe.transpose(banks[f][:, nt * P:(nt + 1) * P], adj_rows[:, nt, f * P:(f + 1) * P], ident[:, :])
                        last.then_inc(s_filled, 1)
                    pe.wait_ge(params_in, 8 * 16)
                    for a in range(HID):
                        last = pe.transpose(banks[4][:, a * P:(a + 1) * P], w1_raw[:, a, :], ident[:, :])
                    last.then_inc(s_filled, 1)
                    for a in range(HID):
                        last = pe.transpose(banks[5][:, a * P:(a + 1) * P], w2_raw[:, a * P:(a + 1) * P], ident[:, :])
                    last.then_inc(s_filled, 1)
                    pe.wait_ge(has_loops, KT)
                    for f in range(6, 10):
                        pe.wait_ge(s_drained, max(f - 7, 1))
                        for nt in range(KT):
                            last = pe.transpose(banks[f % 8][:, nt * P:(nt + 1) * P],
                                                loops[:, nt, (f - 6) * P:(f - 5) * P], ident[:, :])
                        last.then_inc(s_filled, 1)

                @block.scalar
                def _(act):
                    banks = bank_a + bank_b
                    for f in range(4):
                        act.wait_ge(s_filled, f + 1)
                        act.activation(at.hi[:, f, :], banks[f][:, :], ACT.Copy).then_inc(s_hi, 1)
                    act.wait_ge(s_filled, 5)
                    act.activation(w1_t.hi[:, :], banks[4][:, 0:HID * P], ACT.Copy).then_inc(s_hi, 1)
                    act.wait_ge(s_filled, 6)
                    act.activation(w2_t.hi[:, :, :].rearrange("p a d -> p (a d)"), banks[5][:, 0:HID * P], ACT.Copy).then_inc(s_hi, 1)
                    for f in range(6, 10):
                        act.wait_ge(s_filled, f + 1)
                        act.activation(ah_t.hi[:, f - 6, :], banks[f % 8][:, :], ACT.Copy, scale=dinv[:, f - 6:f - 5]).then_inc(s_hi, 1)

                @block.vector
                def _(dve):
                    banks = bank_a + bank_b
                    done = [0]

                    def link(ins):
                        done[0] += 1
                        ins.then_inc(link_s, 1)
                        dve.wait_ge(link_s, done[0])

                    dve.tensor_reduce(rows_sum[:, :], adj_rows[:, :, :], AX.X, ALU.add)
                    for k in range(KT):
                        dve.tensor_tensor_reduce(junk[:, k, :], adj_rows[:, k, k * P:(k + 1) * P], ident[:, :], 1.0, 0.0,
                                                 ALU.mult, ALU.add, diag[:, k:k + 1])
                    for f in range(4):
                        dve.wait_ge(s_hi, f + 1)
                        dve.tensor_reduce(cols_sum[:, f:f + 1], banks[f][:, :], AX.X, ALU.add)
                        dve.tensor_tensor(at.lo[:, f, :], banks[f][:, :], as_f32(at.hi[:, f, :]), ALU.subtract).then_inc(s_drained, 1)
                    dve.wait_ge(s_drained, 4)
                    link(dve.scalar_tensor_tensor(deg[:, :], rows_sum[:, :], 1.0, cols_sum[:, :], ALU.add, ALU.add))
                    dve.tensor_tensor(deg[:, :], deg[:, :], diag[:, :], ALU.subtract).then_inc(has_deg, 1)
                    for f, part, bank in ((4, w1_t, banks[4]), (5, w2_t.view("p a d -> p (a d)"), banks[5])):
                        dve.wait_ge(s_hi, f + 1)
                        dve.tensor_tensor(part.lo[:, :], bank[:, 0:HID * P], as_f32(part.hi[:, :]), ALU.subtract).then_inc(s_drained, 1)
                    link(dve.tensor_copy(loops[:, :, :], adj_rows[:, :, :]))
                    for k in range(KT):
                        blk = loops[:, k, k * P:(k + 1) * P]
                        last = dve.tensor_tensor(blk, blk, ident[:, :], ALU.add)
                    link(last)
                    dve.wait_ge(has_dinv, 1)
                    for k in range(KT):
                        dve.tensor_scalar(loops[:, k, :], loops[:, k, :], dinv[:, k:k + 1], None, ALU.mult).then_inc(has_loops, 1)
                    for f in range(6, 10):
                        dve.wait_ge(s_hi, f + 1)
                        dve.scalar_tensor_tensor(ah_t.lo[:, f - 6, :], banks[f % 8][:, :], dinv[:, f - 6:f - 5],
                                                 as_f32(ah_t.hi[:, f - 6, :]), ALU.mult, ALU.subtract).then_inc(s_drained, 1)

        with ExitStack() as tmp:
            rows = sb(tmp, "rows2", [P, KT, PAIR, D])
            f_in = sb_split(tmp, "f_in", [P, KT, PAIR, D])
            agg_t = sb_split(tmp, "agg_t", [P, PAIR, N])
            ln2 = Norm(sb, tmp, sem, passed, "ln2", rows, KT)
            f_hi, f_lo = sem("f2_hi"), sem("f2_lo")
            agg_filled, agg_hi, agg_drained = sem("agg_filled"), sem("agg_hi"), sem("agg_drained")
            y_filled, y_read, y_stats = sem("y_filled"), sem("y_read"), sem("y_stats")
            has_mv, has_bvar, has_brstd, has_bn, bn_link = sem("bn_mv"), sem("bn_var_s"), sem("bn_rstd_s"), sem("bn_done"), sem("bn_link")
            Y = PAIR * HID

            def columns(dve, turn, first, mvs, stats, scale_shift, gamma, beta, n):
                for a in range(n):
                    last = dve.bn_aggr(mvs[:, a, :], stats[a])
                last.then_inc(has_mv, 1)
                dve.wait_ge(has_mv, turn)
                dve.tensor_scalar(bn_var[:, first:first + n], mvs[:, :, 1], BN_EPS, None, ALU.add).then_inc(has_bvar, 1)
                dve.wait_ge(has_brstd, turn)
                dve.tensor_tensor(scale_shift[:, :, 0], gamma, bn_rstd[:, first:first + n], ALU.mult).then_inc(bn_link, 1)
                dve.wait_ge(bn_link, 2 * turn - 1)
                dve.tensor_tensor(scale_shift[:, :, 1], mvs[:, :, 0], scale_shift[:, :, 0], ALU.mult).then_inc(bn_link, 1)
                dve.wait_ge(bn_link, 2 * turn)
                dve.tensor_tensor(scale_shift[:, :, 1], beta, scale_shift[:, :, 1], ALU.subtract).then_inc(has_bn, 1)

            with nc.Block() as block:
                @block.tensor
                def _(pe):
                    def conv(i):
                        pe.wait_ge(f_lo, i + 1)
                        for b in range(PAIR):
                            wait_some(pe, agg_drained, PAIR * i + b - 1)
                            for k in range(KT):
                                last = split_matmul(pe, bank_a[b][:, :], f_in[:, k, b, :], ah_t[:, k, :], k == 0, k == KT - 1)
                            last.then_inc(agg_filled, 1)
                        for b in range(PAIR):
                            pe.wait_ge(agg_drained, PAIR * i + b + 1)
                            for a in range(HID):
                                n = HID * b + a
                                wait_some(pe, y_read, Y * (i - 1) + n + 1)
                                split_matmul(pe, bank_b[n][:, :], w1_t[:, a * P:(a + 1) * P], agg_t[:, b, :],
                                             True, True).then_inc(y_filled, 1)

                    conv(0)
                    with pe.Fori(1, PAIRS) as i:
                        conv(i)

                @block.scalar
                def _(act):
                    def split_f(i):
                        act.wait_ge(ln2.has_rows, i + 1)
                        wait_some(act, agg_filled, PAIR * i)
                        act.activation(f_in.hi[:, :, :, :], rows[:, :, :, :], ACT.Relu).then_inc(f_hi, 1)

                    def conv(i, ahead):
                        for b in range(PAIR):
                            act.wait_ge(agg_filled, PAIR * i + b + 1)
                            act.activation(agg_t.hi[:, b, :], bank_a[b][:, :], ACT.Copy).then_inc(agg_hi, 1)
                        if ahead:
                            split_f(i + 1)
                        for b in range(PAIR):
                            for a in range(HID):
                                n = HID * b + a
                                act.wait_ge(y_filled, Y * i + n + 1)
                                act.activation(Y1[:, a, bass.ds(PAIR * i + b, 1), :].rearrange("p a n -> p (a n)"), bank_b[n][:, :],
                                               ACT.Identity, bias=b1_col[:, a:a + 1]).then_inc(y_read, 1)

                    split_f(0)
                    with act.Fori(0, PAIRS - 1) as i:
                        conv(i, True)
                    conv(PAIRS - 1, False)
                @block.gpsimd
                def _(pool):
                    with pool.Fori(0, PAIRS) as i:
                        ln2.pool(pool, pow_half, i)
                    pool.wait_ge(has_bvar, 1)
                    pool.tensor_tensor(bn_rstd[:, 0:HID], bn_var[:, 0:HID], pow_half[:, 0:HID], ALU.pow).then_inc(has_brstd, 1)
                @block.vector
                def _(dve):
                    def split_f(i):
                        dve.wait_ge(f_hi, i + 1)
                        flat = "p k b d -> p (k b d)"
                        dve.scalar_tensor_tensor(f_in.lo[:, :, :, :].rearrange(flat), rows[:, :, :, :].rearrange(flat), 0.0,
                                                 as_f32(f_in.hi[:, :, :, :]).rearrange(flat), ALU.max, ALU.subtract).then_inc(f_lo, 1)

                    def conv(i, ahead):
                        if ahead:
                            ln2.dve(dve, X, i + 1, i + 1)
                        for b in range(PAIR):
                            dve.wait_ge(agg_hi, PAIR * i + b + 1)
                            dve.tensor_tensor(agg_t.lo[:, b, :], bank_a[b][:, :], as_f32(agg_t.hi[:, b, :]),
                                              ALU.subtract).then_inc(agg_drained, 1)
                        if ahead:
                            split_f(i + 1)
                        for b in range(PAIR):
                            for a in range(HID):
                                dve.wait_ge(y_read, Y * i + HID * b + a + 1)
                                apart(dve, passed)
                                dve.bn_stats(stats1[:, a, bass.ds(PAIR * i + b, 1), :].rearrange("p a n -> p (a n)"),
                                             Y1[:, a, bass.ds(PAIR * i + b, 1), :].rearrange("p a n -> p (a n)")).then_inc(y_stats, 1)

                    ln2.dve(dve, X, 0, 0)
                    split_f(0)
                    with dve.Fori(0, PAIRS - 1) as i:
                        conv(i, True)
                    conv(PAIRS - 1, False)
                    dve.wait_ge(y_stats, Y * PAIRS)
                    columns(dve, 1, 0, mv[:, 0:HID, :], [stats1[:, a, :, :].rearrange("p b s -> p (b s)") for a in range(HID)],
                            bn1, g1_col[:, :], be1_col[:, :], HID)

        with ExitStack() as tmp:
            z = sb_split(tmp, "z", [P, 2, HID, N])
            has_z, z_hi, z_lo = sem("has_z"), sem("z_hi"), sem("z_lo")
            o_filled, o_read = sem("o_filled"), sem("o_read")

            with nc.Block() as block:
                @block.tensor
                def _(pe):
                    def product(j, s):
                        pe.wait_ge(z_lo, j + 1)
                        wait_some(pe, o_read, j - 1)
                        for a in range(HID):
                            last = split_matmul(pe, bank_a[s][:, :], w2_t[:, a, :], z[:, s, a, :], a == 0, a == HID - 1)
                        last.then_inc(o_filled, 1)

                    product(0, 0)
                    product(1, 1)
                    with pe.Fori(1, B // 2) as t:
                        for s in range(2):
                            product(2 * t + s, s)

                @block.scalar
                def _(act):
                    def norm(j):
                        for a in range(HID):
                            y = Y1[:, a, bass.ds(j, 1), :].rearrange("p a n -> p (a n)")
                            act.activation(y, y, ACT.Relu, bias=bn1[:, a, 1:2], scale=bn1[:, a, 0:1]).then_inc(has_z, 1)

                    def product(j, s):
                        act.wait_ge(o_filled, j + 1)
                        act.activation(Y2[:, bass.ds(j, 1), :].rearrange("p a n -> p (a n)"), bank_a[s][:, :], ACT.Identity,
                                       bias=out_cols[:, 0:1]).then_inc(o_read, 1)

                    norm(0)
                    with act.Fori(0, B // 2 - 1) as t:
                        for s in range(2):
                            norm(2 * t + s + 1)
                            product(2 * t + s, s)
                    norm(B - 1)
                    product(B - 2, 0)
                    product(B - 1, 1)

                @block.gpsimd
                def _(pool):
                    with pool.Fori(0, B // 2) as t:
                        for s in range(2):
                            j = 2 * t + s
                            pool.wait_ge(z_hi, j + 1)
                            for a in range(HID):
                                last = pool.tensor_tensor(z.lo[:, s, a, :], Y1[:, a, bass.ds(j, 1), :].rearrange("p a n -> p (a n)"),
                                                          as_f32(z.hi[:, s, a, :]), ALU.subtract)
                            last.then_inc(z_lo, 1)
                    pool.wait_ge(has_bvar, 2)
                    pool.tensor_tensor(bn_rstd[:, 2:3], bn_var[:, 2:3], pow_half[:, 0:1], ALU.pow).then_inc(has_brstd, 1)

                @block.vector
                def _(dve):
                    def round_z(j, s):
                        dve.wait_ge(has_z, HID * j + HID)
                        wait_some(dve, o_filled, j - 1)
                        for a in range(HID):
                            last = dve.tensor_copy(z.hi[:, s, a, :], Y1[:, a, bass.ds(j, 1), :].rearrange("p a n -> p (a n)"))
                        last.then_inc(z_hi, 1)

                    def product_stats(j):
                        dve.wait_ge(o_read, j + 1)
                        apart(dve, passed)
                        dve.bn_stats(stats2[:, bass.ds(j, 1), :].rearrange("p a s -> p (a s)"),
                                     Y2[:, bass.ds(j, 1), :].rearrange("p a n -> p (a n)")).then_inc(y_stats, 1)

                    round_z(0, 0)
                    round_z(1, 1)
                    with dve.Fori(1, B // 2) as t:
                        for s in range(2):
                            round_z(2 * t + s, s)
                            product_stats(2 * t + s - 2)
                    product_stats(B - 2)
                    product_stats(B - 1)
                    dve.wait_ge(y_stats, Y * PAIRS + B)
                    columns(dve, 2, 2, mv[:, 2:3, :], [stats2[:, :, :].rearrange("p b s -> p (b s)")],
                            bn2[:, :].unsqueeze(1), out_cols[:, 1:2], out_cols[:, 2:3], 1)



def phase_c(nc, sb, sb_split, sem, passed, bank_a, bank_b, X, ident, pow_half, at, Y2, bn2,
            wg0, bg0, wg1, bg1, wih, whh, bih, bhh, out_rows, B, N, D, KT, PAIRS, SKIP, GATES):
    STREAMS = 2
    GROUPS = PAIRS // STREAMS
    INPUT, FORGET, CELL, OUTPUT = range(GATES)
    UNITS = [(1, 0, 0, 1), (1, 0, 1, 2)] + [(p, t, 0, PAIR) for p in range(2, SKIP + 1) for t in range(p)]
    gates_of = lambda t: (INPUT, CELL, OUTPUT) if t == 0 else (INPUT, CELL, FORGET, OUTPUT)
    before = [sum(len(gates_of(u[1])) for u in UNITS[:n]) for n in range(len(UNITS) + 1)]
    READS = before[-1]
    CONV = 10
    wrapped = ExitStack()
    with wrapped as ctx:
        wih_t = sb_split(ctx, "wih_t", [P, SKIP, GATES * P])
        whh_t = sb_split(ctx, "whh_t", [P, SKIP - 1, GATES * P])
        wg = sb_split(ctx, "wg", [P, 2, D])
        gate_bias = sb(ctx, "gate_bias", [P, SKIP, GATES])
        bias0 = sb(ctx, "bias0", [P, KT, D])
        bias1 = sb(ctx, "bias1", [P, N])

        with ExitStack() as tmp:
            raw = sb(tmp, "lstm_raw", [P, 2 * SKIP - 1, GATES, D])
            wg_raw = sb(tmp, "wg_raw", [P, 2, D])
            bg_raw = sb(tmp, "bg_raw", [P, 2, D])
            bg = sb_split(tmp, "bg", [P, 2, D])
            bih_col = sb(tmp, "bih_col", [P, SKIP, GATES])
            bhh_col = sb(tmp, "bhh_col", [P, SKIP, GATES])
            params_in, small_hi = sem("l3_params_in"), sem("l3_small_hi")
            s_filled, s_hi, s_drained = sem("l3s_filled"), sem("l3s_hi"), sem("l3s_drained")
            has_bg = sem("has_bg")
            LOADS = 6 + 2 * SKIP
            with nc.Block() as block:
                @block.sync
                def _(sp):
                    with nc.allow_non_contiguous_dma(reason="parameter columns"):
                        sp.dma_start(raw[:, 0:SKIP, :, :], wih.rearrange("l (g p) h -> p l g h", p=P)).then_inc(params_in, 16)
                        sp.dma_start(raw[:, SKIP:2 * SKIP - 1, :, :],
                                     whh[1:SKIP].rearrange("l (g p) h -> p l g h", p=P)).then_inc(params_in, 16)
                        sp.dma_start(wg_raw[:, 0, :], wg0).then_inc(params_in, 16)
                        sp.dma_start(wg_raw[:, 1, :], wg1).then_inc(params_in, 16)
                        sp.dma_start(bg_raw[:, 0, :], bg0.partition_broadcast(P)).then_inc(params_in, 16)
                        sp.dma_start(bg_raw[:, 1, :], bg1.partition_broadcast(P)).then_inc(params_in, 16)
                        for l in range(SKIP):
                            sp.dma_start(bih_col[:, l, :], bih[l].rearrange("(g p) -> p g", p=P)).then_inc(params_in, 16)
                            sp.dma_start(bhh_col[:, l, :], bhh[l].rearrange("(g p) -> p g", p=P)).then_inc(params_in, 16)

                W = 2 * SKIP - 1

                def weights(f):
                    return (wih_t[:, f, :] if f < SKIP else whh_t[:, f - SKIP, :])

                @block.tensor
                def _(pe):
                    pe.wait_ge(params_in, 16 * LOADS)
                    for f in range(W):
                        if f >= 4:
                            pe.wait_ge(s_drained, f - 3)
                        for g in range(GATES):
                            last = pe.transpose(bank_a[f % 4][:, g * P:(g + 1) * P], raw[:, f, g, :], ident[:, :])
                        last.then_inc(s_filled, 1)
                    pe.wait_ge(has_bg, 1)
                    for nt in range(KT):
                        for k in range(KT):
                            last = split_matmul(pe, bank_b[0][:, nt * D:(nt + 1) * D], at[:, k, nt * P:(nt + 1) * P], bg[:, 0, :],
                                                k == 0, k == KT - 1)
                    last.then_inc(s_filled, 1)
                    for k in range(KT):
                        last = split_matmul(pe, bank_b[1][:, :], bg[:, 1, :], at[:, k, :], k == 0, k == KT - 1)
                    last.then_inc(s_filled, 1)

                @block.scalar
                def _(act):
                    act.wait_ge(params_in, 16 * LOADS)
                    act.activation(wg.hi[:, :, :], wg_raw[:, :, :], ACT.Copy).then_inc(small_hi, 1)
                    act.activation(bg.hi[:, :, :], bg_raw[:, :, :], ACT.Copy).then_inc(small_hi, 1)
                    for f in range(W):
                        act.wait_ge(s_filled, f + 1)
                        act.activation(weights(f).hi, bank_a[f % 4][:, :], ACT.Copy).then_inc(s_hi, 1)

                @block.vector
                def _(dve):
                    dve.wait_ge(small_hi, 2)
                    dve.tensor_tensor(wg.lo[:, :, :], wg_raw[:, :, :], as_f32(wg.hi[:, :, :]), ALU.subtract)
                    dve.tensor_tensor(bg.lo[:, :, :], bg_raw[:, :, :], as_f32(bg.hi[:, :, :]), ALU.subtract).then_inc(has_bg, 1)
                    dve.tensor_tensor(gate_bias[:, :, :], bih_col[:, :, :], bhh_col[:, :, :], ALU.add)
                    for f in range(W):
                        dve.wait_ge(s_hi, f + 1)
                        dve.tensor_tensor(weights(f).lo, bank_a[f % 4][:, :], as_f32(weights(f).hi), ALU.subtract).then_inc(s_drained, 1)
                    dve.wait_ge(s_filled, W + 1)
                    dve.tensor_copy(bias0[:, :, :].rearrange("p k d -> p (k d)"), bank_b[0][:, :])
                    dve.wait_ge(s_filled, W + 2)
                    dve.tensor_copy(bias1[:, :], bank_b[1][:, :])

        class Stream:
            def __init__(self, s):
                n = f"s{s}_"
                self.number = s
                self.banks = (bank_a, bank_b)[s]
                self.rows = sb(ctx, n + "rows", [P, KT, PAIR, D])
                self.y = self.rows[:, :, :, :].rearrange("p k b d -> p (k b d)").rearrange("p (b n) -> p b n", b=PAIR)
                self.h = sb_split(ctx, n + "h", [P, PAIR, N])
                self.f = self.h.view("p b n -> p (b n)").view("p (k b d) -> p k b d", k=KT, b=PAIR)
                self.agg = sb_split(ctx, n + "agg", [P, PAIR, N])
                self.h1 = sb_split(ctx, n + "h1", [P, PAIR, KT, D])
                self.step = self.h1.view("p b k d -> p (b k d)")
                self.gates = sb(ctx, n + "gates", [P, GATES, N])
                self.full = self.gates[:, 0:2, :]
                self.c = sb(ctx, n + "c", [P, N])
                self.tc = sb(ctx, n + "tc", [P, N])
                self.h_full = self.rows[:, :, :, :].rearrange("p k b d -> p (k b d)")
                self.ln = Norm(sb, ctx, sem, passed, n + "ln3", self.rows, KT)
                self.has_y = sem(n + "has_y")
                self.filled = sem(n + "filled")
                self.hi = sem(n + "hi")
                self.drained = sem(n + "drained")
                self.x2_done = sem(n + "x2_done")
                self.f_hi = sem(n + "f_hi")
                self.f_lo = sem(n + "f_lo")
                self.has_full = sem(n + "has_full")
                self.relu_hi = sem(n + "relu_hi")
                self.relu_lo = sem(n + "relu_lo")
                self.gates_full = sem(n + "gates_full")
                self.gates_read = sem(n + "gates_read")
                self.kept = sem(n + "kept")
                self.added = sem(n + "added")
                self.has_c = sem(n + "has_c")
                self.has_tc = sem(n + "has_tc")
                self.has_h = sem(n + "has_h")
                self.h_hi = sem(n + "h_hi")
                self.h_lo = sem(n + "h_lo")
                self.has_h_full = sem(n + "has_h_full")
                self.out_filled = sem(n + "out_filled")
                self.x_done = sem(n + "x_done")
                self.stored = sem(n + "stored")

        streams = [Stream(s) for s in range(STREAMS)]

        def columns(unit, q=None):
            p, t, b0, b1 = unit
            n = N // p
            return n, b1 - b0, slice(b0, b1), slice(t, t + (n - 1) * p + 1, p)

        def windows(part, unit):
            _, _, bs, ts = columns(unit)
            return part[:, bs, ts]

        def by_batch(ap, unit):
            n, nb, _, _ = columns(unit)
            return ap[:, 0:nb * n].rearrange("p (b n) -> p b n", b=nb)

        UN = len(UNITS)
        later = [n for n, unit in enumerate(UNITS) if unit[1] > 0]
        with nc.Block() as block:
            @block.scalar
            def _(act):
                def normalise(s, u):
                    act.wait_ge(s.x_done, PAIR * u + 1)
                    for b in range(PAIR):
                        y = Y2[:, bass.ds(PAIR * (STREAMS * u + s.number) + b, 1), :].rearrange("p a n -> p (a n)")
                        act.activation(s.y[:, b, :], y, ACT.Identity, bias=bn2[:, 1:2], scale=bn2[:, 0:1]).then_inc(s.has_y, 1)

                def split_input(s, u):
                    act.wait_ge(s.ln.has_rows, u + 1)
                    act.activation(s.f.hi, s.rows[:, :, :, :], ACT.Relu).then_inc(s.f_hi, 1)

                def agg(s, u, first, n):
                    for b in range(PAIR):
                        act.wait_ge(s.filled, CONV * u + first + b + 1)
                        act.activation(s.agg.hi[:, b, :], s.banks[(first + b) % 4][:, :], ACT.Copy).then_inc(s.hi, 1)

                def relu(s, u, n, dst):
                    for b in range(PAIR):
                        act.wait_ge(s.has_full, 2 * PAIR * u + PAIR * n + b + 1)
                        act.activation(dst[:, b, :], s.full[:, b, :], ACT.Relu).then_inc(s.relu_hi, 1)

                def lstm_step(s, u, n):
                    p, t, _, _ = UNITS[n]
                    width = columns(UNITS[n])[0] * columns(UNITS[n])[1]
                    if n == 0:
                        act.wait_ge(s.relu_lo, 2 * PAIR * u + 2 * PAIR)
                    else:
                        act.wait_ge(s.has_h, UN * u + n)
                    for m, g in enumerate(gates_of(t)):
                        act.wait_ge(s.gates_full, READS * u + before[n] + m + 1)
                        act.activation(s.gates[:, g, 0:width], s.banks[g][:, 0:width], ACT.Tanh if g == CELL else ACT.Sigmoid,
                                       bias=gate_bias[:, p - 1, g:g + 1]).then_inc(s.gates_read, 1)
                    if t == 0:
                        act.wait_ge(s.added, UN * u + n + 1)
                    else:
                        act.wait_ge(s.has_c, len(later) * u + later.index(n) + 1)
                    if n == 1:
                        act.wait_ge(s.h_lo, UN * u + n)
                    act.activation(s.tc[:, 0:width], s.c[:, 0:width], ACT.Tanh).then_inc(s.has_tc, 1)

                with act.Fori(0, GROUPS) as u:
                    for s in streams:
                        normalise(s, u)
                    for s in streams:
                        split_input(s, u)
                    for s in streams:
                        agg(s, u, 2, 0)
                    for s in streams:
                        relu(s, u, 0, s.h1.hi[:, :, :, :].rearrange("p b k d -> p b (k d)"))
                    for s in streams:
                        agg(s, u, 6, 1)
                    for s in streams:
                        relu(s, u, 1, s.h.hi)
                    for n in range(UN):
                        for s in streams:
                            lstm_step(s, u, n)

            @block.gpsimd
            def _(pool):
                def lstm_product(s, u, n):
                    p, t, _, _ = UNITS[n]
                    width = columns(UNITS[n])[0] * columns(UNITS[n])[1]
                    pool.wait_ge(s.gates_read, READS * u + before[n] + 2)
                    if t == 0:
                        if n > 0:
                            pool.wait_ge(s.has_tc, UN * u + n)
                        pool.tensor_tensor(s.c[:, 0:width], s.gates[:, INPUT, 0:width], s.gates[:, CELL, 0:width],
                                           ALU.mult).then_inc(s.added, 1)
                    else:
                        pool.tensor_tensor(s.gates[:, CELL, 0:width], s.gates[:, INPUT, 0:width], s.gates[:, CELL, 0:width],
                                           ALU.mult).then_inc(s.added, 1)

                def lstm_rest(s, u, n):
                    p, t, _, _ = UNITS[n]
                    unit = UNITS[n]
                    width = columns(unit)[0] * columns(unit)[1]
                    pool.wait_ge(s.h_hi, UN * u + n + 1)
                    if t == p - 1:
                        pool.tensor_tensor(windows(s.h.lo, unit), by_batch(s.tc, unit), as_f32(windows(s.h.hi, unit)), ALU.subtract)\
                            .then_inc(s.h_lo, 1)
                    else:
                        pool.tensor_tensor(s.step.lo[:, 0:width], s.tc[:, 0:width], as_f32(s.step.hi[:, 0:width]), ALU.subtract)\
                            .then_inc(s.h_lo, 1)

                with pool.Fori(0, GROUPS) as u:
                    for s in streams:
                        s.ln.pool(pool, pow_half, u)
                    for n in range(UN):
                        for s in streams:
                            lstm_product(s, u, n)
                            lstm_rest(s, u, n)

            @block.tensor
            def _(pe):
                def y_rows(s, u):
                    pe.wait_ge(s.x_done, PAIR * u + 1)
                    for b in range(PAIR):
                        pe.wait_ge(s.has_y, PAIR * u + b + 1)
                        for k in range(KT):
                            last = pe.transpose(s.banks[b][:, k * P:(k + 1) * P], s.y[:, b, k * P:(k + 1) * P], ident[:, :])
                        last.then_inc(s.filled, 1)

                def convolve(s, u, first, src):
                    for b in range(PAIR):
                        if first == 6:
                            pe.wait_ge(s.drained, 4 * u + b + 1)
                        for k in range(KT):
                            last = split_matmul(pe, s.banks[(first + b) % 4][:, :], src(k, b), at[:, k, :], k == 0, k == KT - 1)
                        last.then_inc(s.filled, 1)

                def by_rows(s, u):
                    for b in range(PAIR):
                        pe.wait_ge(s.drained, 4 * u + b + 1)
                        for nt in range(KT):
                            last = split_matmul(pe, s.banks[b][:, nt * D:(nt + 1) * D], s.agg[:, b, nt * P:(nt + 1) * P], wg[:, 0, :],
                                                True, True)
                        last.then_inc(s.filled, 1)

                def by_features(s, u):
                    for b in range(PAIR):
                        pe.wait_ge(s.drained, 4 * u + PAIR + b + 1)
                        split_matmul(pe, s.banks[b][:, :], wg[:, 1, :], s.agg[:, b, :], True, True).then_inc(s.filled, 1)

                def lstm_step(s, u, n):
                    unit = UNITS[n]
                    p, t, _, _ = unit
                    width = columns(unit)[0] * columns(unit)[1]
                    x = Split(windows(s.h.hi, unit), windows(s.h.lo, unit))
                    for m, g in enumerate(gates_of(t)):
                        users = [k for k in range(n) if g in gates_of(UNITS[k][1])]
                        if users:
                            pe.wait_ge(s.gates_read, READS * u + before[users[-1]] + gates_of(UNITS[users[-1]][1]).index(g) + 1)
                        last = split_matmul(pe, by_batch(s.banks[g], unit), wih_t[:, p - 1, g * P:(g + 1) * P], x, True, t == 0)
                        if t == 0:
                            last.then_inc(s.gates_full, 1)
                    if t > 0:
                        pe.wait_ge(s.h_lo, UN * u + n)
                        h = s.step[:, 0:width]
                        for g in gates_of(t):
                            split_matmul(pe, s.banks[g][:, 0:width], whh_t[:, p - 2, g * P:(g + 1) * P], h, False, True)\
                                .then_inc(s.gates_full, 1)

                def out_rows_of(s, u):
                    pe.wait_ge(s.gates_read, READS * (u + 1))
                    pe.wait_ge(s.has_h_full, u + 1)
                    for b in range(PAIR):
                        for k in range(KT):
                            c = b * N + k * P
                            last = pe.transpose(s.banks[b][:, k * P:(k + 1) * P], s.h_full[:, c:c + P], ident[:, :])
                        last.then_inc(s.out_filled, 1)

                with pe.Fori(0, GROUPS) as u:
                    for s in streams:
                        y_rows(s, u)
                    for s in streams:
                        pe.wait_ge(s.f_lo, u + 1)
                        convolve(s, u, 2, lambda k, b, s=s: s.f[:, k, b, :])
                    for s in streams:
                        pe.wait_ge(s.x2_done, PAIR * (u + 1))
                        by_rows(s, u)
                    for s in streams:
                        pe.wait_ge(s.relu_lo, 2 * PAIR * u + PAIR)
                        convolve(s, u, 6, lambda k, b, s=s: s.h1[:, b, k, :])
                    for s in streams:
                        by_features(s, u)
                    for n in range(UN):
                        for s in streams:
                            if n == 0:
                                pe.wait_ge(s.relu_lo, 2 * PAIR * (u + 1))
                            elif UNITS[n][1] == 0 and n > 1:
                                pe.wait_ge(s.h_lo, UN * u + n)
                            lstm_step(s, u, n)
                    for s in streams:
                        out_rows_of(s, u)

            @block.vector
            def _(dve):
                def x2(s, u):
                    for b in range(PAIR):
                        dve.wait_ge(s.filled, CONV * u + b + 1)
                        xs = X[:, :, bass.ds(PAIR * (STREAMS * u + s.number) + b, 1), :].rearrange("p k a d -> p k (a d)")
                        dve.tensor_tensor(xs, s.banks[b][:, :].rearrange("p (k d) -> p k d", k=KT), xs, ALU.add).then_inc(s.x2_done, 1)
                    dve.wait_ge(s.x2_done, PAIR * (u + 1))
                    s.ln.dve(dve, X, STREAMS * u + s.number, u)

                def split_input(s, u):
                    dve.wait_ge(s.f_hi, u + 1)
                    flat = "p k b d -> p (k b d)"
                    dve.scalar_tensor_tensor(s.h.lo[:, :, :].rearrange("p b n -> p (b n)"), s.rows[:, :, :, :].rearrange(flat), 0.0,
                                             as_f32(s.h.hi[:, :, :]).rearrange("p b n -> p (b n)"), ALU.max, ALU.subtract)\
                        .then_inc(s.f_lo, 1)

                def agg(s, u, first, n):
                    for b in range(PAIR):
                        dve.wait_ge(s.hi, 2 * PAIR * u + PAIR * n + b + 1)
                        dve.tensor_tensor(s.agg.lo[:, b, :], s.banks[(first + b) % 4][:, :], as_f32(s.agg.hi[:, b, :]),
                                          ALU.subtract).then_inc(s.drained, 1)

                def with_bias(s, u, first, bias):
                    for b in range(PAIR):
                        dve.wait_ge(s.filled, CONV * u + first + b + 1)
                        dve.tensor_tensor(s.full[:, b, :], s.banks[b][:, :], bias, ALU.add).then_inc(s.has_full, 1)

                def relu_rest(s, u, n, hi, lo):
                    for b in range(PAIR):
                        dve.wait_ge(s.relu_hi, 2 * PAIR * u + PAIR * n + b + 1)
                        dve.scalar_tensor_tensor(lo[:, b, :], s.full[:, b, :], 0.0, as_f32(hi[:, b, :]), ALU.max, ALU.subtract)\
                            .then_inc(s.relu_lo, 1)

                def lstm_cell(s, u, n):
                    width = columns(UNITS[n])[0] * columns(UNITS[n])[1]
                    t = UNITS[n][1]
                    if t == 0:
                        return
                    dve.wait_ge(s.gates_read, READS * u + before[n] + 3)
                    dve.tensor_tensor(s.c[:, 0:width], s.c[:, 0:width], s.gates[:, FORGET, 0:width], ALU.mult).then_inc(s.kept, 1)
                    dve.wait_ge(s.kept, len(later) * u + later.index(n) + 1)
                    dve.wait_ge(s.added, UN * u + n + 1)
                    dve.tensor_tensor(s.c[:, 0:width], s.c[:, 0:width], s.gates[:, CELL, 0:width], ALU.add).then_inc(s.has_c, 1)

                def lstm_h(s, u, n):
                    unit = UNITS[n]
                    p, t, _, _ = unit
                    width = columns(unit)[0] * columns(unit)[1]
                    dve.wait_ge(s.has_tc, UN * u + n + 1)
                    dve.tensor_tensor(s.tc[:, 0:width], s.tc[:, 0:width], s.gates[:, OUTPUT, 0:width], ALU.mult).then_inc(s.has_h, 1)
                    dve.wait_ge(s.has_h, UN * u + n + 1)
                    if t == p - 1:
                        dve.tensor_copy(windows(s.h.hi, unit), by_batch(s.tc, unit)).then_inc(s.h_hi, 1)
                    else:
                        dve.tensor_copy(s.step.hi[:, 0:width], s.tc[:, 0:width]).then_inc(s.h_hi, 1)

                def whole_h(s, u):
                    dve.wait_ge(s.h_lo, UN * (u + 1))
                    dve.tensor_tensor(s.h_full, as_f32(s.h.hi[:, :, :]).rearrange("p b n -> p (b n)"),
                                      as_f32(s.h.lo[:, :, :]).rearrange("p b n -> p (b n)"), ALU.add).then_inc(s.has_h_full, 1)

                def x3(s, u):
                    for b in range(PAIR):
                        dve.wait_ge(s.out_filled, PAIR * u + b + 1)
                        xs = X[:, :, bass.ds(PAIR * (STREAMS * u + s.number) + b, 1), :].rearrange("p k a d -> p k (a d)")
                        dve.tensor_tensor(xs, s.banks[b][:, :].rearrange("p (k d) -> p k d", k=KT), xs, ALU.add).then_inc(s.x_done, 1)

                for s in streams:
                    dve.engine_nop().then_inc(s.x_done, 1)
                with dve.Fori(0, GROUPS) as u:
                    for s in streams:
                        x2(s, u)
                    for s in streams:
                        split_input(s, u)
                    for s in streams:
                        agg(s, u, 2, 0)
                    for s in streams:
                        with_bias(s, u, 4, bias0[:, :, :].rearrange("p k d -> p (k d)"))
                        relu_rest(s, u, 0, s.h1.hi[:, :, :, :].rearrange("p b k d -> p b (k d)"),
                                  s.h1.lo[:, :, :, :].rearrange("p b k d -> p b (k d)"))
                    for s in streams:
                        agg(s, u, 6, 1)
                    for s in streams:
                        with_bias(s, u, 8, bias1[:, :])
                        relu_rest(s, u, 1, s.h.hi, s.h.lo)
                    for n in range(UN):
                        for s in streams:
                            lstm_cell(s, u, n)
                            lstm_h(s, u, n)
                    for s in streams:
                        whole_h(s, u)
                    for s in streams:
                        x3(s, u)

            @block.sync
            def _(sp):
                with sp.Fori(0, GROUPS) as u:
                    for s in streams:
                        for b in range(PAIR):
                            sp.wait_ge(s.x_done, PAIR * u + b + 2)
                            at_b = PAIR * (STREAMS * u + s.number) + b
                            sp.dma_start(out_rows[bass.ds(at_b, 1)].rearrange("a p k d -> p k (a d)"),
                                         X[:, :, bass.ds(at_b, 1), :].rearrange("p k a d -> p k (a d)")).then_inc(s.stored, 16)
                for s in streams:
                    sp.wait_ge(s.stored, 16 * PAIR * GROUPS)


_INS = ['x', 'adj', 'L0_gnn_alpha_train', 'L0_gnn_w', 'L0_gnn_d', 'L0_gnn_fc_in_w', 'L0_gnn_fc_in_b',
        'L1_gnn_W', 'L1_gnn_b_lin', 'L1_gnn_b',
        'L2_gnn_W1', 'L2_gnn_b1', 'L2_gnn_g1', 'L2_gnn_be1', 'L2_gnn_W2', 'L2_gnn_b2', 'L2_gnn_g2', 'L2_gnn_be2',
        'L3_gnn_Wg0', 'L3_gnn_bg0', 'L3_gnn_Wg1', 'L3_gnn_bg1', 'L3_gnn_Wih', 'L3_gnn_Whh', 'L3_gnn_bih', 'L3_gnn_bhh']
_OUTS = [((16, 512, 128), 'float32')]


def kernel(**inputs):
    import numpy as _np
    import concourse.bacc as _bacc
    from concourse import mybir as _mybir
    from concourse.bass_utils import run_bass_kernel_spmd as _run

    nc = _bacc.Bacc("TRN2", target_bir_lowering=False, num_devices=1)
    arrays, args = {}, []
    for name in _INS:
        a = _np.ascontiguousarray(inputs[name])
        arrays[f"in_{name}_dram"] = a
        args.append(nc.dram_tensor(f"in_{name}_dram", a.shape, _mybir.dt.from_np(a.dtype), kind="ExternalInput").ap())
    for i, (shape, dtype) in enumerate(_OUTS):
        dt = _mybir.dt.from_np(_np.dtype(dtype))
        args.append(nc.dram_tensor(f"out_{i}_dram", shape, dt, kind="ExternalOutput").ap())
    build(nc, *args)
    r = _run(nc, [arrays], core_ids=[0])
    got = tuple(r.results[0][f"out_{i}_dram"] for i in range(len(_OUTS)))
    return got[0]
```

```python
from contextlib import ExitStack
from math import comb

import concourse.bass as bass
from concourse import mybir
from concourse.alu_op_type import AluOpType as ALU

ACT = mybir.ActivationFunctionType
AX = mybir.AxisListType
F32 = mybir.dt.float32
F32R = mybir.dt.float32r

P = 128
STEPS = 8
DT = 1.0 / STEPS
LN_EPS = 1e-5
BN_EPS = 1e-5
MASKED = -1e16
SPLIT = 3
PAIR = 2


class Split:

    def __init__(self, hi, lo):
        self.hi, self.lo = hi, lo

    def __getitem__(self, key):
        return Split(self.hi[key], self.lo[key])

    def view(self, pattern, **sizes):
        return Split(self.hi.rearrange(pattern, **sizes), self.lo.rearrange(pattern, **sizes))


def as_f32(ap):
    return ap.bitcast(F32)


def split_matmul(pe, out, w, x, start, stop, shared=False):
    pe.matmul(out, w.hi, x.hi, start=start, stop=False, skip_group_check=shared)
    pe.matmul(out, w.hi, x.lo, start=False, stop=False, skip_group_check=shared)
    return pe.matmul(out, w.lo, x.hi, start=False, stop=stop, skip_group_check=shared)


def wait_some(eng, sem, value):
    if not isinstance(value, int) or value > 0:
        eng.wait_ge(sem, value)


def apart(eng, passed):
    eng.sem_inc(passed)


def build(nc, x, adj, alpha, w, d, fc_w, fc_b, l1_w, l1_blin, l1_b, w1, b1, g1, be1, w2, b2, g2, be2,
          wg0, bg0, wg1, bg1, wih, whh, bih, bhh, out):
    B, N, D = x.shape
    KT = N // P
    PAIRS = B // PAIR
    HID = w1.shape[0] // P
    SKIP = wih.shape[0]
    GATES = 4
    assert D == P and PAIR == 2 and KT == 4 and HID == 2 and SKIP == 4

    x_rows = x.rearrange("b (k p) d -> b p k d", p=P)
    out_rows = out.rearrange("b (k p) d -> b p k d", p=P)

    top = ExitStack()
    with top:
        def sb(ctx, name, shape, dt=F32):
            return ctx.enter_context(nc.sbuf_tensor(name, shape, dt))[:]

        def sb_split(ctx, name, shape):
            return Split(sb(ctx, name + "_hi", shape, F32R), sb(ctx, name + "_lo", shape, F32R))

        def sem(name):
            return top.enter_context(nc.semaphore(name))

        bank_a = [top.enter_context(nc.psum_tensor(f"bank_a{i}", [P, 512], F32))[:] for i in range(4)]
        bank_b = [top.enter_context(nc.psum_tensor(f"bank_b{i}", [P, 512], F32))[:] for i in range(4)]

        X = sb(top, "X", [P, KT, B, D])
        ident = sb(top, "ident", [P, P])
        pow_half = sb(top, "pow_half", [P, 8])
        passed = sem("passed")
        adj_rows = sb(top, "adj_rows", [P, KT, N])

        phase_a(nc, sb, sb_split, sem, passed, bank_a, bank_b, X, ident, pow_half, adj_rows, x_rows, adj,
                alpha, w, d, fc_w, fc_b, l1_w, l1_blin, l1_b, B, N, D, KT, PAIRS)
        at = sb_split(top, "at", [P, KT, N])
        Y2 = sb(top, "Y2", [P, B, N])
        bn2 = sb(top, "bn2", [P, 2])
        phase_b(nc, sb, sb_split, sem, passed, bank_a, bank_b, X, ident, pow_half, adj_rows, at, Y2, bn2,
                w1, b1, g1, be1, w2, b2, g2, be2, B, N, D, KT, PAIRS, HID)
        phase_c(nc, sb, sb_split, sem, passed, bank_a, bank_b, X, ident, pow_half, at, Y2, bn2,
                wg0, bg0, wg1, bg1, wih, whh, bih, bhh, out_rows, B, N, D, KT, PAIRS, SKIP, GATES)



class Norm:

    def __init__(self, sb, ctx, sem, passed, name, rows, KT):
        self.passed = passed
        self.stats = sb(ctx, name + "_stats", [P, PAIR * KT, 6])
        self.mv = sb(ctx, name + "_mv", [P, PAIR * KT, 2])
        self.var = sb(ctx, name + "_var", [P, PAIR * KT])
        self.neg_mean = sb(ctx, name + "_neg_mean", [P, PAIR * KT])
        self.rstd = sb(ctx, name + "_rstd", [P, PAIR * KT])
        self.shift = sb(ctx, name + "_shift", [P, PAIR * KT])
        self.rows = rows
        self.tiles = [(k, b) for k in range(KT) for b in range(PAIR)]
        self.has_stats, self.has_mv, self.has_var = sem(name + "_has_stats"), sem(name + "_has_mv"), sem(name + "_has_var")
        self.has_rstd, self.has_shift, self.has_rows = sem(name + "_has_rstd"), sem(name + "_has_shift"), sem(name + "_has_rows")

    def tile(self, X, pair, k, b):
        return X[:, k, bass.ds(pair * PAIR + b, 1), :].rearrange("p a d -> p (a d)")

    def statistics(self, dve, X, pair, n):
        apart(dve, self.passed)
        for t, (k, b) in enumerate(self.tiles):
            last = dve.bn_stats(self.stats[:, t, :], self.tile(X, pair, k, b))
        last.then_inc(self.has_stats, 1)
        dve.wait_ge(self.has_stats, n + 1)
        apart(dve, self.passed)
        for t in range(len(self.tiles)):
            last = dve.bn_aggr(self.mv[:, t, :], self.stats[:, t, :])
        last.then_inc(self.has_mv, 1)
        dve.wait_ge(self.has_mv, n + 1)
        dve.tensor_scalar(self.neg_mean[:, :], self.mv[:, :, 0], -1.0, None, ALU.mult)
        dve.tensor_scalar(self.var[:, :], self.mv[:, :, 1], LN_EPS, None, ALU.add).then_inc(self.has_var, 1)

    def scales(self, pool, pow_half, n):
        pool.wait_ge(self.has_var, n + 1)
        pool.tensor_tensor(self.rstd[:, :], self.var[:, :], pow_half[:, :], ALU.pow).then_inc(self.has_rstd, 1)
        pool.wait_ge(self.has_rstd, n + 1)
        pool.tensor_tensor(self.shift[:, :], self.neg_mean[:, :], self.rstd[:, :], ALU.mult).then_inc(self.has_shift, 1)

    def normalise(self, act, X, pair, n):
        act.wait_ge(self.has_shift, n + 1)
        for t, (k, b) in enumerate(self.tiles):
            last = act.activation(self.rows[:, k, b, :], self.tile(X, pair, k, b), ACT.Identity,
                                  bias=self.shift[:, t:t + 1], scale=self.rstd[:, t:t + 1])
        last.then_inc(self.has_rows, 1)

    def normalise_dve(self, dve, X, pair, n):
        dve.wait_ge(self.has_shift, n + 1)
        for t, (k, b) in enumerate(self.tiles):
            last = dve.tensor_scalar(self.rows[:, k, b, :], self.tile(X, pair, k, b),
                                     self.rstd[:, t:t + 1], self.shift[:, t:t + 1], ALU.mult, ALU.add)
        last.then_inc(self.has_rows, 1)



def phase_a(nc, sb, sb_split, sem, passed, bank_a, bank_b, X, ident, pow_half, adj_rows, x_rows, adj,
            alpha, w, d, fc_w, fc_b, l1_w, l1_blin, l1_b, B, N, D, KT, PAIRS):
    ctx = ExitStack()
    with ctx:
        m_t = [None] + [sb_split(ctx, f"m{i}_t", [P, KT, N]) for i in (1, 2, 3)]
        R = sb_split(ctx, "R", [P, STEPS + 1, D])
        g_bias = sb(ctx, "g_bias", [P, SPLIT, N])
        w_l1 = sb_split(ctx, "w_l1", [P, D])
        blin_col = sb(ctx, "blin_col", [P, 1])
        b_row = sb(ctx, "b_row", [P, D])

        rows = sb(ctx, "rows", [P, KT, PAIR, D])
        x0 = sb_split(ctx, "x0", [P, KT, PAIR, D])
        ln0 = Norm(sb, ctx, sem, passed, "ln0", rows, KT)

        x_in, x_first_in, adj_in, small_in = sem("x_in"), sem("x_first_in"), sem("adj_in"), sem("small_in")
        x0_hi, x0_lo = sem("x0_hi"), sem("x0_lo")

        def round_x0(act, i):
            act.wait_ge(ln0.has_rows, i + 1)
            act.activation(x0.hi[:, :, :, :], rows[:, :, :, :], ACT.Relu).then_inc(x0_hi, 1)

        def rest_of_x0(dve, i):
            dve.wait_ge(x0_hi, i + 1)
            flat = "p k b d -> p (k b d)"
            dve.scalar_tensor_tensor(x0.lo[:, :, :, :].rearrange(flat), rows[:, :, :, :].rearrange(flat), 0.0,
                                     as_f32(x0.hi[:, :, :, :]).rearrange(flat), ALU.max, ALU.subtract).then_inc(x0_lo, 1)

        with ExitStack() as tmp:
            w_raw = sb(tmp, "w_raw", [P, D])
            fc_raw = sb(tmp, "fc_raw", [P, D])
            l1_raw = sb(tmp, "l1_raw", [P, D])
            d_col = sb(tmp, "d_col", [P, 1])
            fcb_col = sb(tmp, "fcb_col", [P, 1])
            alpha_col = sb(tmp, "alpha_col", [P, KT])
            gain = sb(tmp, "gain", [P, KT])
            keep = sb(tmp, "keep", [P, KT])
            w_t = sb(tmp, "w_t", [P, D])
            wd_t = sb(tmp, "wd_t", [P, D])
            v1 = sb(tmp, "v1", [P, D])
            powers = sb(tmp, "powers", [P, STEPS + 1, 2 * D + 1])
            r_sum = sb(tmp, "r_sum", [P, STEPS + 1, D])
            r_bias = sb(tmp, "r_bias", [P, STEPS + 1])
            m_rows = sb(tmp, "m_rows", [P, KT, N])
            m_split = sb_split(tmp, "m_split", [P, KT, N])
            ones = sb(tmp, "ones", [P, P], F32R)
            ones_f = sb(tmp, "ones_f", [P, P])

            has_ident, has_exp = sem("has_ident"), sem("has_exp")
            has_m_rows, m_rows_hi = sem("has_m_rows"), sem("m_rows_hi")
            has_m_split = sem("has_m_split")
            has_ones = sem("has_ones")
            v_filled, v_drained = sem("v_filled"), sem("v_drained")
            m_filled, m_hi, m_drained = sem("m_filled"), sem("m_hi"), sem("m_drained")
            u_filled, link_s, r_hi = sem("u_filled"), sem("setup_link"), sem("r_hi")
            r_full, w_hi = sem("r_full"), sem("w_l1_hi")

            def v_rounds(f):
                i = 2 * (f - KT) + 1
                return [r for r in (i, i + 1) if 1 <= r <= STEPS]

            block = tmp.enter_context(nc.Block())

            @block.sync
            def _(sp):
                with nc.allow_non_contiguous_dma(reason="parameter columns"):
                    sp.dma_start(w_raw[:, :], w).then_inc(small_in, 16)
                    sp.dma_start(d_col[:, :], d.rearrange("(p a) -> p a", a=1)).then_inc(small_in, 16)
                    sp.dma_start(alpha_col[:, :], alpha.rearrange("(k p) -> p k", p=P)).then_inc(small_in, 16)
                    sp.dma_start(adj_rows[:, :, :], adj.rearrange("(k p) n -> p k n", p=P)).then_inc(adj_in, 16)
                    sp.dma_start(fc_raw[:, :], fc_w).then_inc(small_in, 16)
                    sp.dma_start(fcb_col[:, :], fc_b.rearrange("(p a) -> p a", a=1)).then_inc(small_in, 16)
                    sp.dma_start(l1_raw[:, :], l1_w).then_inc(small_in, 16)
                    sp.dma_start(blin_col[:, :], l1_blin.rearrange("(p a) -> p a", a=1)).then_inc(small_in, 16)
                    sp.dma_start(b_row[:, :], l1_b.partition_broadcast(P)).then_inc(small_in, 16)
                for b in range(PAIR):
                    sp.dma_start(X[:, :, b, :], x_rows[b]).then_inc(x_first_in, 16)
                with sp.Fori(PAIR, B) as b:
                    sp.dma_start(X[:, :, bass.ds(b, 1), :].rearrange("p k a d -> p k (a d)"),
                                 x_rows[bass.ds(b, 1)].rearrange("a p k d -> p k (a d)")).then_inc(x_in, 16)

            @block.gpsimd
            def _(pool):
                pool.memset(pow_half[:, :], -0.5)
                pool.memset(ident[:, :], 0.0).then_inc(has_ident, 1)
                pool.wait_ge(has_ident, 1)
                pool.affine_select(out=ident[:, :], in_=ident[:, :], compare_op=ALU.not_equal, fill=1.0,
                                   base=0, pattern=[[-1, P]], channel_multiplier=1).then_inc(has_ident, 1)
                ln0.scales(pool, pow_half, 0)

            @block.scalar
            def _(act):
                act.wait_ge(small_in, 8 * 16)
                act.activation(gain[:, :], alpha_col[:, :], ACT.Exp, scale=-1.0).then_inc(has_exp, 1)
                act.activation(w_l1.hi[:, :], l1_raw[:, :], ACT.Copy).then_inc(w_hi, 1)
                for k in range(KT):
                    act.wait_ge(has_m_rows, k + 1)
                    act.activation(m_split.hi[:, k, :], m_rows[:, k, :], ACT.Copy).then_inc(m_rows_hi, 1)
                for f in range(3 * KT):
                    act.wait_ge(m_filled, f + 1)
                    act.activation(m_t[f // KT + 1].hi[:, f % KT, :], bank_a[f % 4][:, :], ACT.Copy).then_inc(m_hi, 1)
                    if f == KT + 2:
                        ln0.normalise(act, X, 0, 0)
                    if f == KT + 3:
                        round_x0(act, 0)
                    if f == 2 * KT:
                        act.wait_ge(r_full, 1)
                        act.activation(R.hi[:, :, :], r_sum[:, :, :], ACT.Copy).then_inc(r_hi, 1)

            @block.tensor
            def _(pe):
                pe.wait_ge(small_in, 8 * 16)
                pe.wait_ge(has_ident, 2)
                pe.transpose(bank_b[2][:, 0:D], w_raw[:, :], ident[:, :]).then_inc(v_filled, 1)
                pe.wait_ge(v_drained, 1)
                pe.matmul(bank_b[3][:, 0:D], wd_t[:, :], w_t[:, :], start=True, stop=True).then_inc(v_filled, 1)

                def v_round(i):
                    pe.wait_ge(v_drained, i + 2)
                    v_i = ident[:, :] if i == 0 else powers[:, i - 1, 0:D]
                    bank = bank_b[i % 2]
                    pe.matmul(bank[:, 0:D], v1[:, :], v_i, start=True, stop=True)
                    pe.matmul(bank[:, D:2 * D], fc_raw[:, :], v_i, start=True, stop=True)
                    pe.matmul(bank[:, 2 * D:2 * D + 1], v_i, fcb_col[:, :], start=True, stop=True).then_inc(v_filled, 1)

                def m_fill(f):
                    power, mt = f // KT + 1, f % KT
                    rounds = v_rounds(f)
                    for i in rounds[:1]:
                        v_round(i)
                    if f >= 4:
                        pe.wait_ge(m_drained, f - 3)
                    if power == 1:
                        for nt in range(KT):
                            last = pe.transpose(bank_a[f % 4][:, nt * P:(nt + 1) * P],
                                                m_rows[:, nt, mt * P:(mt + 1) * P], ident[:, :])
                    else:
                        pe.wait_ge(m_drained, KT * (power - 1))
                        for kt in range(KT):
                            last = split_matmul(pe, bank_a[f % 4][:, :], m_split[:, kt, mt * P:(mt + 1) * P],
                                                m_t[power - 1][:, kt, :], kt == 0, kt == KT - 1)
                            if kt == 1:
                                for i in rounds[1:]:
                                    v_round(i)
                    last.then_inc(m_filled, 1)

                pe.wait_ge(has_m_rows, KT)
                v_round(0)
                for f in range(KT):
                    m_fill(f)
                pe.wait_ge(has_m_split, 1)
                for f in range(KT, 3 * KT):
                    m_fill(f)
                    if f == 2 * KT:
                        pe.wait_ge(has_ones, 1)
                        for q in (1, 2):
                            for n, part in enumerate((m_t[q].hi, m_t[q].lo)):
                                for kt in range(KT):
                                    last = pe.matmul(bank_b[q + 1][:, :], ones[:, :], part[:, kt, :],
                                                     start=(n == 0 and kt == 0), stop=(n == 1 and kt == KT - 1))
                        last.then_inc(u_filled, 1)

            @block.vector
            def _(dve):
                done = [0]

                def link(ins):
                    done[0] += 1
                    ins.then_inc(link_s, 1)
                    dve.wait_ge(link_s, done[0])

                link(dve.memset(ones_f[:, :], 1.0))
                dve.tensor_copy(ones[:, :], ones_f[:, :]).then_inc(has_ones, 1)
                dve.wait_ge(small_in, 8 * 16)
                link(dve.tensor_scalar(d_col[:, :], d_col[:, :], 0.0, 1.0, ALU.max, ALU.min))
                dve.wait_ge(has_exp, 1)
                link(dve.tensor_scalar(gain[:, :], gain[:, :], 1.0, None, ALU.add))
                link(dve.reciprocal(gain[:, :], gain[:, :]))
                link(dve.tensor_scalar(gain[:, :], gain[:, :], 0.5 * DT, None, ALU.mult))
                link(dve.tensor_scalar(keep[:, :], gain[:, :], -1.0, 1.0 - DT, ALU.mult, ALU.add))
                dve.wait_ge(v_filled, 1)
                dve.tensor_copy(w_t[:, :], bank_b[2][:, 0:D])
                dve.tensor_scalar(wd_t[:, :], bank_b[2][:, 0:D], d_col[:, 0:1], None, ALU.mult).then_inc(v_drained, 1)
                dve.wait_ge(adj_in, 16)
                dve.wait_ge(has_ident, 2)
                for k in range(KT):
                    link(dve.tensor_scalar(m_rows[:, k, :], adj_rows[:, k, :], gain[:, k:k + 1], None, ALU.mult))
                    blk = m_rows[:, k, k * P:(k + 1) * P]
                    dve.scalar_tensor_tensor(blk, ident[:, :], keep[:, k:k + 1], blk, ALU.mult, ALU.add).then_inc(has_m_rows, 1)
                dve.wait_ge(v_filled, 2)
                dve.tensor_scalar(v1[:, :], bank_b[3][:, 0:D], DT, None, ALU.mult).then_inc(v_drained, 1)
                dve.wait_ge(w_hi, 1)
                dve.tensor_tensor(w_l1.lo[:, :], l1_raw[:, :], as_f32(w_l1.hi[:, :]), ALU.subtract)
                for k in range(KT):
                    dve.wait_ge(m_rows_hi, k + 1)
                    last = dve.tensor_tensor(m_split.lo[:, k, :], m_rows[:, k, :], as_f32(m_split.hi[:, k, :]), ALU.subtract)
                last.then_inc(has_m_split, 1)

                def v_drain(i):
                    dve.wait_ge(v_filled, i + 3)
                    dve.tensor_copy(powers[:, i, :], bank_b[i % 2][:, 0:2 * D + 1]).then_inc(v_drained, 1)

                def m_drain(f):
                    dve.wait_ge(m_hi, f + 1)
                    dve.tensor_tensor(m_t[f // KT + 1].lo[:, f % KT, :], bank_a[f % 4][:, :],
                                      as_f32(m_t[f // KT + 1].hi[:, f % KT, :]), ALU.subtract).then_inc(m_drained, 1)

                def add_power(i):
                    dve.wait_ge(v_drained, i + 3)
                    k = STEPS - i
                    c = float(comb(STEPS, k))
                    dve.tensor_scalar(r_bias[:, k:k + 1], powers[:, i, 2 * D:2 * D + 1], c, None, ALU.mult)
                    v_i = ident[:, :] if i == 0 else powers[:, i - 1, 0:D]
                    f_v = powers[:, i, D:2 * D]
                    if i == 0:
                        link(dve.tensor_scalar(r_sum[:, k, :], f_v, c, None, ALU.mult))
                        for k in range(STEPS):
                            last = dve.tensor_scalar(r_sum[:, k, :], v_i, DT, None, ALU.mult)
                    else:
                        last = dve.scalar_tensor_tensor(r_sum[:, k, :], f_v, c, r_sum[:, k, :], ALU.mult, ALU.add)
                        for k in range(STEPS - i):
                            last = dve.scalar_tensor_tensor(r_sum[:, k, :], v_i, DT * comb(k + i, k), r_sum[:, k, :],
                                                            ALU.mult, ALU.add)
                    link(last)

                v_drain(0)
                for f in range(KT):
                    m_drain(f)
                for f in range(KT, 3 * KT):
                    rounds = v_rounds(f)
                    for i in rounds[:1]:
                        v_drain(i)
                    if f == KT:
                        add_power(0)
                    if f == KT + 1:
                        dve.wait_ge(x_first_in, 16 * PAIR)
                        ln0.statistics(dve, X, 0, 0)
                    if f in (KT + 2, KT + 3):
                        add_power(f - KT - 1)
                    for i in rounds[1:]:
                        v_drain(i)
                    m_drain(f)
                    if f == 2 * KT - 1:
                        for i in range(3, STEPS + 1):
                            add_power(i)
                        dve.engine_nop().then_inc(r_full, 1)
                    if f == 2 * KT:
                        dve.wait_ge(u_filled, 1)
                        for j in range(SPLIT):
                            k = SPLIT * j
                            last = dve.tensor_scalar(g_bias[:, j, :], bank_b[2][:, :], r_bias[:, k + 1:k + 2], r_bias[:, k:k + 1],
                                                     ALU.mult, ALU.add)
                        link(last)
                        for j in range(SPLIT):
                            k = SPLIT * j
                            dve.scalar_tensor_tensor(g_bias[:, j, :], bank_b[3][:, :], r_bias[:, k + 2:k + 3], g_bias[:, j, :],
                                                     ALU.mult, ALU.add)
                    if f == 2 * KT + 1:
                        dve.wait_ge(r_hi, 1)
                        dve.tensor_tensor(R.lo[:, :, :], r_sum[:, :, :], as_f32(R.hi[:, :, :]), ALU.subtract)
                    if f == 2 * KT + 2:
                        rest_of_x0(dve, 0)

        x_t = sb_split(ctx, "x_t", [P, SPLIT, PAIR, N])
        g_full = sb(ctx, "g_full", [P, PAIR, N])
        g_rows = sb_split(ctx, "g_rows", [P, PAIR, KT, D])
        hn_t = sb_split(ctx, "hn_t", [P, PAIR, N])
        h_t = sb_split(ctx, "h_t", [P, PAIR, N])
        scores = sb(ctx, "scores", [P, KT, N])
        h_full = scores
        probs = sb(ctx, "probs", [P, KT, N])
        probs_t = sb_split(ctx, "probs_t", [P, KT, N])
        out_t = sb(ctx, "out_t", [P, N])
        neg_max = sb(ctx, "neg_max", [P, PAIR, KT])
        row_sum = sb(ctx, "row_sum", [P, PAIR, KT])
        inv_sum = sb(ctx, "inv_sum", [P, PAIR, KT])
        h_rows = hn_t.view("p b (k d) -> p b k d", k=KT)

        ln1 = Norm(sb, ctx, sem, passed, "ln1", rows, KT)
        a_filled, a_hi, a_drained = sem("a_filled"), sem("a_hi"), sem("a_drained")
        b_filled, b_hi, b_drained, b_full = sem("b_filled"), sem("b_hi"), sem("b_drained"), sem("b_full")
        has_xb, has_neg, has_mask, has_probs = sem("has_xb"), sem("has_neg"), sem("has_mask"), sem("has_probs")
        has_inv, o_filled, o_drained = sem("has_inv"), sem("out_filled"), sem("out_drained")

        A, A_BANKS, A_SPLITS = 18, 3, 10
        C, C_BANKS, C_SPLITS = 24, 4, 14
        banks_0, banks_1, bank_out = bank_a[:3], [bank_a[3]] + bank_b[:3], bank_b[3]
        SCORES, PROBS, OUT = (6, 14), (10, 19), (18, 23)

        def power_of(f):
            return (0, f) if f < 2 else ((f - 2) % 2 + 1, (f - 2) // 2)

        with nc.Block() as block:
            @block.tensor
            def _(pe):
                def a_slot(i, f):
                    pe.wait_ge(a_drained, A * i + f + 1)
                    return banks_0[f % A_BANKS]

                def c_slot(j, f):
                    pe.wait_ge(b_drained, C * j + f + 1)
                    return banks_1[f % C_BANKS]

                def transpose_tiles(bank, tiles):
                    for k, tile in enumerate(tiles):
                        last = pe.transpose(bank[:, k * P:(k + 1) * P], tile, ident[:, :])
                    return last

                def x0_transposes(i):
                    pe.wait_ge(ln0.has_rows, i + 1)
                    for b in range(PAIR):
                        transpose_tiles(a_slot(i, b), [rows[:, k, b, :] for k in range(KT)]).then_inc(a_filled, 1)

                def m_powers(i, b):
                    pe.wait_ge(x0_lo, i + 1)
                    for q in (1, 2):
                        bank = a_slot(i, 2 + 2 * b + q - 1)
                        for k in range(KT):
                            last = split_matmul(pe, bank[:, :], x0[:, k, b, :], m_t[q][:, k, :], k == 0, k == KT - 1)
                        last.then_inc(a_filled, 1)

                def g_term(i, j):
                    stage = SPLIT - 1 - j
                    for b in range(PAIR):
                        f = 6 + 4 * stage + b
                        bank = a_slot(i, f)
                        if stage == 0:
                            pe.wait_ge(a_drained, A * i + 3 + 2 * b + A_BANKS + 1)
                        for q in range(SPLIT):
                            last = split_matmul(pe, bank[:, :], R[:, SPLIT * j + q, :], x_t[:, q, b, :],
                                                q == 0, stage == 0 and q == SPLIT - 1)
                        if stage:
                            pe.wait_ge(a_drained, A * i + f - 2 + A_BANKS + 1)
                            for k in range(KT):
                                last = split_matmul(pe, bank[:, :], g_rows[:, b, k, :], m_t[3][:, k, :], False, k == KT - 1)
                        last.then_inc(a_filled, 1)

                def g_transposes(i, j):
                    for b in range(PAIR):
                        f = 8 + 4 * (SPLIT - 1 - j) + b
                        bank = a_slot(i, f)
                        pe.wait_ge(a_drained, A * i + f - 2 + A_BANKS + 1)
                        transpose_tiles(bank, [g_full[:, b, k * P:(k + 1) * P] for k in range(KT)]).then_inc(a_filled, 1)

                def in_transposes(j):
                    pe.wait_ge(ln1.has_rows, j + 1)
                    for b in range(PAIR):
                        transpose_tiles(c_slot(j, b), [rows[:, k, b, :] for k in range(KT)]).then_inc(b_filled, 1)

                def project(j):
                    for b in range(PAIR):
                        bank = c_slot(j, 2 + b)
                        pe.wait_ge(b_drained, C * j + b + C_BANKS + 1)
                        split_matmul(pe, bank[:, :], w_l1, hn_t[:, b, :], True, True).then_inc(b_filled, 1)

                def h_transposes(j):
                    for b in range(PAIR):
                        bank = c_slot(j, 4 + b)
                        pe.wait_ge(b_full, PAIR * j + b + 1)
                        transpose_tiles(bank, [h_full[:, b, k * P:(k + 1) * P] for k in range(KT)]).then_inc(b_filled, 1)

                def score(j, b):
                    pe.wait_ge(b_drained, C * j + 2 + b + C_BANKS + 1)
                    for nt in range(KT):
                        bank = c_slot(j, SCORES[b] + nt)
                        split_matmul(pe, bank[:, :], h_t[:, b, nt * P:(nt + 1) * P], h_t[:, b, :], True, True).then_inc(b_filled, 1)

                def probs_transposes(j, b):
                    pe.wait_ge(has_probs, 2 * KT * j + KT * b + KT)
                    for kt in range(KT):
                        transpose_tiles(c_slot(j, PROBS[b] + kt),
                                        [probs[:, nt, kt * P:(kt + 1) * P] for nt in range(KT)]).then_inc(b_filled, 1)

                def attend(j, b):
                    bank = c_slot(j, OUT[b])
                    for kt in range(KT):
                        pe.wait_ge(b_drained, C * j + PROBS[b] + kt + C_BANKS + 1)
                        last = split_matmul(pe, bank[:, :], h_rows[:, b, kt, :], probs_t[:, kt, :], kt == 0, kt == KT - 1)
                    last.then_inc(b_filled, 1)

                def out_transposes(j, b):
                    pe.wait_ge(b_drained, C * j + OUT[b] + C_BANKS + 1)
                    pe.wait_ge(o_drained, PAIR * j + b + 1)
                    transpose_tiles(bank_out, [out_t[:, k * P:(k + 1) * P] for k in range(KT)]).then_inc(o_filled, 1)

                def turn(i, zero, one):
                    j = i - 1
                    if zero:
                        x0_transposes(i)
                        m_powers(i, 0)
                    if one:
                        in_transposes(j)
                    if zero:
                        m_powers(i, 1)
                    if one:
                        project(j)
                    if zero:
                        g_term(i, 2)
                    if one:
                        h_transposes(j)
                    if zero:
                        g_transposes(i, 2)
                    if one:
                        score(j, 0)
                    if zero:
                        g_term(i, 1)
                    if one:
                        probs_transposes(j, 0)
                    if zero:
                        g_transposes(i, 1)
                    if one:
                        score(j, 1)
                        attend(j, 0)
                    if zero:
                        g_term(i, 0)
                    if one:
                        out_transposes(j, 0)
                        probs_transposes(j, 1)
                    if zero:
                        g_transposes(i, 0)
                    if one:
                        attend(j, 1)
                        out_transposes(j, 1)

                turn(0, True, False)
                with pe.Fori(1, PAIRS) as i:
                    turn(i, True, True)
                turn(PAIRS, False, True)

            @block.scalar
            def _(act):
                def a_round(i, f, n, dst, func=ACT.Copy):
                    act.wait_ge(a_filled, A * i + f + 1)
                    act.activation(dst, banks_0[f % A_BANKS][:, :], func).then_inc(a_hi, 1)

                def power_round(i, f):
                    q, b = power_of(f)
                    a_round(i, f, f, x_t.hi[:, q, b, :], ACT.Relu if q == 0 else ACT.Copy)

                def g_round(i, j):
                    for b in range(PAIR):
                        a_round(i, 8 + 4 * (SPLIT - 1 - j) + b, 0, g_rows.hi[:, b, :, :].rearrange("p k d -> p (k d)"))

                def c_round(j, f, dst, func=ACT.Copy):
                    act.wait_ge(b_filled, C * j + f + 1)
                    act.activation(dst, banks_1[f % C_BANKS][:, :], func).then_inc(b_hi, 1)

                def project(j):
                    for b in range(PAIR):
                        act.wait_ge(b_filled, C * j + 2 + b + 1)
                        bank = banks_1[2 + b]
                        act.activation(h_full[:, b, :], bank[:, :], ACT.Identity, bias=blin_col[:, 0:1]).then_inc(b_full, 1)
                        act.activation(h_t.hi[:, b, :], bank[:, :], ACT.Identity, bias=blin_col[:, 0:1]).then_inc(b_hi, 1)

                def exponentials(j, b):
                    for nt in range(KT):
                        act.wait_ge(has_neg, 2 * KT * j + KT * b + nt + 1)
                        act.activation(probs[:, nt, :], scores[:, nt, :], ACT.Exp, bias=neg_max[:, b, nt:nt + 1], scale=-1.0,
                                       accum_out=row_sum[:, b, nt:nt + 1]).then_inc(has_probs, 1)

                def round_probs(j, b):
                    for kt in range(KT):
                        c_round(j, PROBS[b] + kt, probs_t.hi[:, kt, :])

                def turn(i, zero, one, ahead):
                    j = i - 1
                    if zero:
                        power_round(i, 0)
                        power_round(i, 1)
                    if one:
                        if zero:
                            act.wait_ge(x0_lo, i + 1)
                        ln1.normalise(act, X, j, j)
                    if zero:
                        power_round(i, 2)
                        power_round(i, 3)
                    if one:
                        for b in range(PAIR):
                            c_round(j, b, hn_t.hi[:, b, :], ACT.Relu)
                    if zero:
                        power_round(i, 4)
                        power_round(i, 5)
                    if one:
                        project(j)
                        for b in range(PAIR):
                            c_round(j, 4 + b, hn_t.hi[:, b, :])
                    if zero:
                        g_round(i, 2)
                    if one:
                        exponentials(j, 0)
                    if ahead:
                        ln0.normalise(act, X, i + 1, i + 1)
                        act.wait_ge(a_filled, A * i + 6)
                        round_x0(act, i + 1)
                    if one:
                        round_probs(j, 0)
                    if zero:
                        g_round(i, 1)
                    if one:
                        exponentials(j, 1)
                        round_probs(j, 1)

                turn(0, True, False, True)
                with act.Fori(1, PAIRS - 1) as i:
                    turn(i, True, True, True)
                turn(PAIRS - 1, True, True, False)
                turn(PAIRS, False, True, False)

            @block.gpsimd
            def _(pool):
                def add_b(j):
                    pool.wait_ge(ln1.has_rows, j + 1)
                    for b in range(PAIR):
                        xs = X[:, :, bass.ds(PAIR * j + b, 1), :].rearrange("p k a d -> p k (a d)")
                        last = pool.tensor_tensor(xs, xs, b_row[:, :].unsqueeze(1).to_broadcast([P, KT, D]), ALU.add)
                    last.then_inc(has_xb, 1)

                def turn(i, one, ahead):
                    if one:
                        ln1.scales(pool, pow_half, i - 1)
                        add_b(i - 1)
                    if ahead:
                        ln0.scales(pool, pow_half, i + 1)

                turn(0, False, True)
                with pool.Fori(1, PAIRS - 1) as i:
                    turn(i, True, True)
                turn(PAIRS - 1, True, False)
                turn(PAIRS, True, False)

            @block.vector
            def _(dve):
                def power_rest(i, f):
                    dve.wait_ge(a_hi, A_SPLITS * i + f + 1)
                    q, b = power_of(f)
                    bank = banks_0[f % A_BANKS]
                    if q == 0:
                        ins = dve.scalar_tensor_tensor(x_t.lo[:, q, b, :], bank[:, :], 0.0, as_f32(x_t.hi[:, q, b, :]),
                                                       ALU.max, ALU.subtract)
                    else:
                        ins = dve.tensor_tensor(x_t.lo[:, q, b, :], bank[:, :], as_f32(x_t.hi[:, q, b, :]), ALU.subtract)
                    ins.then_inc(a_drained, 1)

                def g_full_of(i, j):
                    for b in range(PAIR):
                        f = 6 + 4 * (SPLIT - 1 - j) + b
                        dve.wait_ge(a_filled, A * i + f + 1)
                        dve.tensor_tensor(g_full[:, b, :], banks_0[f % A_BANKS][:, :], g_bias[:, j, :], ALU.add).then_inc(a_drained, 1)

                def g_rest(i, j):
                    stage = SPLIT - 1 - j
                    for b in range(PAIR):
                        f = 8 + 4 * stage + b
                        dve.wait_ge(a_hi, A_SPLITS * i + 6 + 2 * stage + b + 1)
                        flat = "p k d -> p (k d)"
                        dve.tensor_tensor(g_rows.lo[:, b, :, :].rearrange(flat), banks_0[f % A_BANKS][:, :],
                                          as_f32(g_rows.hi[:, b, :, :]).rearrange(flat), ALU.subtract).then_inc(a_drained, 1)

                def residual(i):
                    for b in range(PAIR):
                        dve.wait_ge(a_filled, A * i + 16 + b + 1)
                        xs = X[:, :, bass.ds(PAIR * i + b, 1), :].rearrange("p k a d -> p k (a d)")
                        dve.tensor_tensor(xs, banks_0[(16 + b) % A_BANKS][:, :].rearrange("p (k d) -> p k d", k=KT), xs,
                                          ALU.add).then_inc(a_drained, 1)

                def c_rest(j, f, n, hi, lo, relu=False):
                    dve.wait_ge(b_hi, C_SPLITS * j + n + 1)
                    bank = banks_1[f % C_BANKS]
                    if relu:
                        ins = dve.scalar_tensor_tensor(lo, bank[:, :], 0.0, as_f32(hi), ALU.max, ALU.subtract)
                    else:
                        ins = dve.tensor_tensor(lo, bank[:, :], as_f32(hi), ALU.subtract)
                    ins.then_inc(b_drained, 1)

                def edges(j, b, nt):
                    dve.wait_ge(b_filled, C * j + SCORES[b] + nt + 1)
                    if b == 1:
                        dve.wait_ge(has_probs, 2 * KT * j + nt + 1)
                    dve.tensor_tensor(scores[:, nt, :], banks_1[(SCORES[b] + nt) % C_BANKS][:, :], adj_rows[:, nt, :],
                                      ALU.mult).then_inc(b_drained, 1)

                def mask(j, b, nt):
                    dve.wait_ge(b_drained, C * j + SCORES[b] + nt + C_BANKS + 1)
                    dve.tensor_scalar(probs[:, nt, :], scores[:, nt, :], 0.0, MASKED, ALU.is_equal, ALU.mult).then_inc(has_mask, 1)

                def maximum(j, b, nt):
                    dve.wait_ge(has_mask, 2 * KT * j + KT * b + nt + 1)
                    apart(dve, passed)
                    dve.tensor_tensor_reduce(scores[:, nt, :], scores[:, nt, :], probs[:, nt, :], -1.0, 3.0e38,
                                             ALU.add, ALU.min, neg_max[:, b, nt:nt + 1]).then_inc(has_neg, 1)

                def softmax(j, b):
                    for step in range(KT + 2):
                        if step < KT:
                            edges(j, b, step)
                        if 0 <= step - 1 < KT:
                            mask(j, b, step - 1)
                        if 0 <= step - 2 < KT:
                            maximum(j, b, step - 2)

                def rest_of_probs(j, b):
                    dve.wait_ge(has_probs, 2 * KT * j + KT * b + KT)
                    dve.reciprocal(inv_sum[:, b, :], row_sum[:, b, :]).then_inc(has_inv, 1)
                    for kt in range(KT):
                        c_rest(j, PROBS[b] + kt, 6 + KT * b + kt, probs_t.hi[:, kt, :], probs_t.lo[:, kt, :])

                def attention(j, b):
                    dve.wait_ge(b_filled, C * j + OUT[b] + 1)
                    dve.tensor_copy(out_t[:, :], banks_1[OUT[b] % C_BANKS][:, :]).then_inc(b_drained, 1)

                def attention_rows(j, b):
                    if b == 0:
                        dve.wait_ge(has_xb, j + 1)
                    dve.wait_ge(has_inv, PAIR * j + b + 1)
                    dve.wait_ge(o_filled, PAIR * j + b + 1)
                    for nt in range(KT):
                        xs = X[:, nt, bass.ds(PAIR * j + b, 1), :].rearrange("p a d -> p (a d)")
                        last = dve.scalar_tensor_tensor(xs, bank_out[:, nt * D:(nt + 1) * D], inv_sum[:, b, nt:nt + 1],
                                                        xs, ALU.mult, ALU.add)
                    last.then_inc(o_drained, 1)

                def turn(i, zero, one, ahead):
                    j = i - 1
                    if one:
                        dve.wait_ge(a_drained, A * i + A_BANKS)
                        ln1.statistics(dve, X, j, j)
                    if zero:
                        for f in range(4):
                            power_rest(i, f)
                    if one:
                        for b in range(PAIR):
                            c_rest(j, b, b, hn_t.hi[:, b, :], hn_t.lo[:, b, :], relu=True)
                    if zero:
                        for f in (4, 5):
                            power_rest(i, f)
                    if one:
                        for b in range(PAIR):
                            dve.wait_ge(b_hi, C_SPLITS * j + 2 + b + 1)
                            dve.scalar_tensor_tensor(h_t.lo[:, b, :], banks_1[2 + b][:, :], blin_col[:, 0:1],
                                                     as_f32(h_t.hi[:, b, :]), ALU.add, ALU.subtract).then_inc(b_drained, 1)
                    if zero:
                        g_full_of(i, 2)
                    if one:
                        for b in range(PAIR):
                            c_rest(j, 4 + b, 4 + b, hn_t.hi[:, b, :], hn_t.lo[:, b, :])
                    if zero:
                        g_rest(i, 2)
                    if ahead:
                        ln0.statistics(dve, X, i + 1, i + 1)
                    if one:
                        softmax(j, 0)
                    if zero:
                        g_full_of(i, 1)
                    if one:
                        rest_of_probs(j, 0)
                    if zero:
                        g_rest(i, 1)
                    if one:
                        softmax(j, 1)
                        attention(j, 0)
                    if ahead:
                        rest_of_x0(dve, i + 1)
                    if zero:
                        g_full_of(i, 0)
                    if one:
                        attention_rows(j, 0)
                        rest_of_probs(j, 1)
                    if zero:
                        residual(i)
                    if one:
                        attention(j, 1)
                        attention_rows(j, 1)

                for _ in range(A_BANKS):
                    dve.engine_nop().then_inc(a_drained, 1)
                for _ in range(C_BANKS):
                    dve.engine_nop().then_inc(b_drained, 1)
                dve.engine_nop().then_inc(o_drained, 1)
                dve.wait_ge(x_in, 16 * (B - PAIR))
                turn(0, True, False, True)
                with dve.Fori(1, PAIRS - 1) as i:
                    turn(i, True, True, True)
                turn(PAIRS - 1, True, True, False)
                turn(PAIRS, False, True, False)



def phase_b(nc, sb, sb_split, sem, passed, bank_a, bank_b, X, ident, pow_half, adj_rows, at, Y2, bn2,
            w1, b1, g1, be1, w2, b2, g2, be2, B, N, D, KT, PAIRS, HID):
    ctx = ExitStack()
    with ctx:
        Y1 = sb(ctx, "Y1", [P, HID, B, N])
        ah_t = sb_split(ctx, "ah_t", [P, KT, N])
        w1_t = sb_split(ctx, "w1_t", [P, HID * P])
        w2_t = sb_split(ctx, "w2_t", [P, HID, D])
        b1_col = sb(ctx, "b1_col", [P, HID])
        g1_col = sb(ctx, "g1_col", [P, HID])
        be1_col = sb(ctx, "be1_col", [P, HID])
        out_cols = sb(ctx, "out_cols", [P, 3])
        bn1 = sb(ctx, "bn1", [P, HID, 2])
        stats1 = sb(ctx, "stats1", [P, HID, B, 6])
        stats2 = sb(ctx, "stats2", [P, B, 6])
        mv = sb(ctx, "mv", [P, 3, 2])
        bn_var = sb(ctx, "bn_var", [P, 4])
        bn_rstd = sb(ctx, "bn_rstd", [P, 4])

        with ExitStack() as tmp:
            w1_raw = sb(tmp, "w1_raw", [P, HID, D])
            w2_raw = sb(tmp, "w2_raw", [P, HID * P])
            loops = sb(tmp, "loops", [P, KT, N])
            diag = sb(tmp, "diag", [P, KT])
            junk = sb(tmp, "junk", [P, KT, P])
            deg = sb(tmp, "deg", [P, KT])
            rows_sum = sb(tmp, "rows_sum", [P, KT])
            cols_sum = sb(tmp, "cols_sum", [P, KT])
            dinv = sb(tmp, "dinv", [P, KT])
            params_in = sem("l2_params_in")
            s_filled, s_hi, s_drained = sem("l2s_filled"), sem("l2s_hi"), sem("l2s_drained")
            has_deg, has_dinv, has_loops, link_s = sem("has_deg"), sem("has_dinv"), sem("has_loops"), sem("l2_link")

            with nc.Block() as block:
                @block.sync
                def _(sp):
                    with nc.allow_non_contiguous_dma(reason="parameter columns"):
                        sp.dma_start(w1_raw[:, :, :], w1.rearrange("(a p) d -> p a d", p=P)).then_inc(params_in, 16)
                        sp.dma_start(w2_raw[:, :], w2).then_inc(params_in, 16)
                        for dst, src in ((b1_col, b1), (g1_col, g1), (be1_col, be1)):
                            sp.dma_start(dst[:, :], src.rearrange("(a p) -> p a", p=P)).then_inc(params_in, 16)
                        for n, src in enumerate((b2, g2, be2)):
                            sp.dma_start(out_cols[:, n:n + 1], src.rearrange("(p a) -> p a", a=1)).then_inc(params_in, 16)

                @block.gpsimd
                def _(pool):
                    pool.wait_ge(has_deg, 1)
                    pool.tensor_tensor(dinv[:, :], deg[:, :], pow_half[:, 0:KT], ALU.pow).then_inc(has_dinv, 1)

                @block.tensor
                def _(pe):
                    banks = bank_a + bank_b
                    for f in range(4):
                        for nt in range(KT):
                            last = pe.transpose(banks[f][:, nt * P:(nt + 1) * P], adj_rows[:, nt, f * P:(f + 1) * P], ident[:, :])
                        last.then_inc(s_filled, 1)
                    pe.wait_ge(params_in, 8 * 16)
                    for a in range(HID):
                        last = pe.transpose(banks[4][:, a * P:(a + 1) * P], w1_raw[:, a, :], ident[:, :])
                    last.then_inc(s_filled, 1)
                    for a in range(HID):
                        last = pe.transpose(banks[5][:, a * P:(a + 1) * P], w2_raw[:, a * P:(a + 1) * P], ident[:, :])
                    last.then_inc(s_filled, 1)
                    pe.wait_ge(has_loops, KT)
                    for f in range(6, 10):
                        pe.wait_ge(s_drained, max(f - 7, 1))
                        for nt in range(KT):
                            last = pe.transpose(banks[f % 8][:, nt * P:(nt + 1) * P],
                                                loops[:, nt, (f - 6) * P:(f - 5) * P], ident[:, :])
                        last.then_inc(s_filled, 1)

                @block.scalar
                def _(act):
                    banks = bank_a + bank_b
                    for f in range(4):
                        act.wait_ge(s_filled, f + 1)
                        act.activation(at.hi[:, f, :], banks[f][:, :], ACT.Copy).then_inc(s_hi, 1)
                    act.wait_ge(s_filled, 5)
                    act.activation(w1_t.hi[:, :], banks[4][:, 0:HID * P], ACT.Copy).then_inc(s_hi, 1)
                    act.wait_ge(s_filled, 6)
                    act.activation(w2_t.hi[:, :, :].rearrange("p a d -> p (a d)"), banks[5][:, 0:HID * P], ACT.Copy).then_inc(s_hi, 1)
                    for f in range(6, 10):
                        act.wait_ge(s_filled, f + 1)
                        act.activation(ah_t.hi[:, f - 6, :], banks[f % 8][:, :], ACT.Copy, scale=dinv[:, f - 6:f - 5]).then_inc(s_hi, 1)

                @block.vector
                def _(dve):
                    banks = bank_a + bank_b
                    done = [0]

                    def link(ins):
                        done[0] += 1
                        ins.then_inc(link_s, 1)
                        dve.wait_ge(link_s, done[0])

                    dve.tensor_reduce(rows_sum[:, :], adj_rows[:, :, :], AX.X, ALU.add)
                    for k in range(KT):
                        dve.tensor_tensor_reduce(junk[:, k, :], adj_rows[:, k, k * P:(k + 1) * P], ident[:, :], 1.0, 0.0,
                                                 ALU.mult, ALU.add, diag[:, k:k + 1])
                    for f in range(4):
                        dve.wait_ge(s_hi, f + 1)
                        dve.tensor_reduce(cols_sum[:, f:f + 1], banks[f][:, :], AX.X, ALU.add)
                        dve.tensor_tensor(at.lo[:, f, :], banks[f][:, :], as_f32(at.hi[:, f, :]), ALU.subtract).then_inc(s_drained, 1)
                    dve.wait_ge(s_drained, 4)
                    link(dve.scalar_tensor_tensor(deg[:, :], rows_sum[:, :], 1.0, cols_sum[:, :], ALU.add, ALU.add))
                    dve.tensor_tensor(deg[:, :], deg[:, :], diag[:, :], ALU.subtract).then_inc(has_deg, 1)
                    for f, part, bank in ((4, w1_t, banks[4]), (5, w2_t.view("p a d -> p (a d)"), banks[5])):
                        dve.wait_ge(s_hi, f + 1)
                        dve.tensor_tensor(part.lo[:, :], bank[:, 0:HID * P], as_f32(part.hi[:, :]), ALU.subtract).then_inc(s_drained, 1)
                    link(dve.tensor_copy(loops[:, :, :], adj_rows[:, :, :]))
                    for k in range(KT):
                        blk = loops[:, k, k * P:(k + 1) * P]
                        last = dve.tensor_tensor(blk, blk, ident[:, :], ALU.add)
                    link(last)
                    dve.wait_ge(has_dinv, 1)
                    for k in range(KT):
                        dve.tensor_scalar(loops[:, k, :], loops[:, k, :], dinv[:, k:k + 1], None, ALU.mult).then_inc(has_loops, 1)
                    for f in range(6, 10):
                        dve.wait_ge(s_hi, f + 1)
                        dve.scalar_tensor_tensor(ah_t.lo[:, f - 6, :], banks[f % 8][:, :], dinv[:, f - 6:f - 5],
                                                 as_f32(ah_t.hi[:, f - 6, :]), ALU.mult, ALU.subtract).then_inc(s_drained, 1)

        with ExitStack() as tmp:
            rows = sb(tmp, "rows2", [P, KT, PAIR, D])
            f_in = sb_split(tmp, "f_in", [P, 2, KT, PAIR, D])
            agg_t = sb_split(tmp, "agg_t", [P, PAIR, N])
            ln2 = Norm(sb, tmp, sem, passed, "ln2", rows, KT)
            f_hi, f_lo = sem("f2_hi"), sem("f2_lo")
            agg_filled, agg_hi, agg_drained = sem("agg_filled"), sem("agg_hi"), sem("agg_drained")
            y_filled, y_read, y_stats = sem("y_filled"), sem("y_read"), sem("y_stats")
            has_mv, has_bvar, has_brstd, has_bn, bn_link = sem("bn_mv"), sem("bn_var_s"), sem("bn_rstd_s"), sem("bn_done"), sem("bn_link")
            Y = PAIR * HID

            def columns(dve, turn, first, mvs, stats, scale_shift, gamma, beta, n):
                for a in range(n):
                    last = dve.bn_aggr(mvs[:, a, :], stats[a])
                last.then_inc(has_mv, 1)
                dve.wait_ge(has_mv, turn)
                dve.tensor_scalar(bn_var[:, first:first + n], mvs[:, :, 1], BN_EPS, None, ALU.add).then_inc(has_bvar, 1)
                dve.wait_ge(has_brstd, turn)
                dve.tensor_tensor(scale_shift[:, :, 0], gamma, bn_rstd[:, first:first + n], ALU.mult).then_inc(bn_link, 1)
                dve.wait_ge(bn_link, 2 * turn - 1)
                dve.tensor_tensor(scale_shift[:, :, 1], mvs[:, :, 0], scale_shift[:, :, 0], ALU.mult).then_inc(bn_link, 1)
                dve.wait_ge(bn_link, 2 * turn)
                dve.tensor_tensor(scale_shift[:, :, 1], beta, scale_shift[:, :, 1], ALU.subtract).then_inc(has_bn, 1)

            with nc.Block() as block:
                @block.tensor
                def _(pe):
                    def conv(i, s):
                        pe.wait_ge(f_lo, i + 1)
                        for b in range(PAIR):
                            for k in range(KT):
                                last = split_matmul(pe, bank_a[PAIR * s + b][:, :], f_in[:, s, k, b, :], ah_t[:, k, :],
                                                    k == 0, k == KT - 1)
                            last.then_inc(agg_filled, 1)

                    def product(i):
                        for b in range(PAIR):
                            pe.wait_ge(agg_drained, PAIR * i + b + 1)
                            for a in range(HID):
                                n = HID * b + a
                                wait_some(pe, y_read, Y * (i - 1) + n + 1)
                                split_matmul(pe, bank_b[n][:, :], w1_t[:, a * P:(a + 1) * P], agg_t[:, b, :],
                                             True, True).then_inc(y_filled, 1)

                    conv(0, 0)
                    conv(1, 1)
                    product(0)
                    with pe.Fori(1, PAIRS // 2) as t:
                        for s in range(2):
                            conv(2 * t + s, s)
                            product(2 * t + s - 1)
                    product(PAIRS - 1)

                @block.scalar
                def _(act):
                    def split_f(i, s):
                        wait_some(act, f_lo, i)
                        ln2.normalise(act, X, i, i)
                        act.wait_ge(ln2.has_rows, i + 1)
                        act.activation(f_in.hi[:, s, :, :, :], rows[:, :, :, :], ACT.Relu).then_inc(f_hi, 1)

                    def turn(i, s, ahead):
                        for b in range(PAIR):
                            act.wait_ge(agg_filled, PAIR * i + b + 1)
                            act.activation(agg_t.hi[:, b, :], bank_a[PAIR * s + b][:, :], ACT.Copy).then_inc(agg_hi, 1)
                        if ahead:
                            split_f(i + 2, s)
                        for b in range(PAIR):
                            for a in range(HID):
                                n = HID * b + a
                                act.wait_ge(y_filled, Y * i + n + 1)
                                act.activation(Y1[:, a, bass.ds(PAIR * i + b, 1), :].rearrange("p a n -> p (a n)"), bank_b[n][:, :],
                                               ACT.Identity, bias=b1_col[:, a:a + 1]).then_inc(y_read, 1)

                    split_f(0, 0)
                    split_f(1, 1)
                    with act.Fori(0, PAIRS // 2 - 1) as t:
                        for s in range(2):
                            turn(2 * t + s, s, True)
                    for s in range(2):
                        turn(PAIRS - 2 + s, s, False)

                @block.gpsimd
                def _(pool):
                    with pool.Fori(0, PAIRS) as i:
                        ln2.scales(pool, pow_half, i)
                    pool.wait_ge(has_bvar, 1)
                    pool.tensor_tensor(bn_rstd[:, 0:HID], bn_var[:, 0:HID], pow_half[:, 0:HID], ALU.pow).then_inc(has_brstd, 1)

                @block.vector
                def _(dve):
                    def split_f(i, s):
                        dve.wait_ge(f_hi, i + 1)
                        flat = "p k b d -> p (k b d)"
                        dve.scalar_tensor_tensor(f_in.lo[:, s, :, :, :].rearrange(flat), rows[:, :, :, :].rearrange(flat), 0.0,
                                                 as_f32(f_in.hi[:, s, :, :, :]).rearrange(flat), ALU.max, ALU.subtract).then_inc(f_lo, 1)

                    def turn(i, s, ahead, further):
                        for b in range(PAIR):
                            dve.wait_ge(agg_hi, PAIR * i + b + 1)
                            dve.tensor_tensor(agg_t.lo[:, b, :], bank_a[PAIR * s + b][:, :], as_f32(agg_t.hi[:, b, :]),
                                              ALU.subtract).then_inc(agg_drained, 1)
                        if ahead:
                            split_f(i + 2, s)
                        if further:
                            ln2.statistics(dve, X, i + 3, i + 3)
                        for b in range(PAIR):
                            for a in range(HID):
                                dve.wait_ge(y_read, Y * i + HID * b + a + 1)
                                apart(dve, passed)
                                dve.bn_stats(stats1[:, a, bass.ds(PAIR * i + b, 1), :].rearrange("p a n -> p (a n)"),
                                             Y1[:, a, bass.ds(PAIR * i + b, 1), :].rearrange("p a n -> p (a n)")).then_inc(y_stats, 1)

                    ln2.statistics(dve, X, 0, 0)
                    split_f(0, 0)
                    ln2.statistics(dve, X, 1, 1)
                    split_f(1, 1)
                    ln2.statistics(dve, X, 2, 2)
                    with dve.Fori(0, PAIRS // 2 - 2) as t:
                        for s in range(2):
                            turn(2 * t + s, s, True, True)
                    for i in range(PAIRS - 4, PAIRS):
                        turn(i, i % 2, i + 2 < PAIRS, i + 3 < PAIRS)
                    dve.wait_ge(y_stats, Y * PAIRS)
                    columns(dve, 1, 0, mv[:, 0:HID, :], [stats1[:, a, :, :].rearrange("p b s -> p (b s)") for a in range(HID)],
                            bn1, g1_col[:, :], be1_col[:, :], HID)

        with ExitStack() as tmp:
            RING = 4
            AHEAD = 2
            z = sb_split(tmp, "z", [P, RING, HID, N])
            has_z, z_hi_0, z_hi_1 = sem("has_z"), sem("z_hi_0"), sem("z_hi_1")
            z_lo_0, z_lo_1 = sem("z_lo_0"), sem("z_lo_1")
            o_filled, o_read = sem("o_filled"), sem("o_read")

            def hidden(j, a):
                return Y1[:, a, bass.ds(j, 1), :].rearrange("p a n -> p (a n)")

            with nc.Block() as block:
                @block.tensor
                def _(pe):
                    def product(j, s):
                        pe.wait_ge(z_lo_0, j + 1)
                        pe.wait_ge(z_lo_1, j + 1)
                        wait_some(pe, o_read, j + 1 - RING)
                        for a in range(HID):
                            last = split_matmul(pe, bank_a[s][:, :], w2_t[:, a, :], z[:, s, a, :], a == 0, a == HID - 1)
                        last.then_inc(o_filled, 1)

                    for s in range(RING):
                        product(s, s)
                    with pe.Fori(1, B // RING) as t:
                        for s in range(RING):
                            product(RING * t + s, s)

                @block.scalar
                def _(act):
                    def norm(j):
                        for a in range(HID):
                            act.activation(hidden(j, a), hidden(j, a), ACT.Relu, bias=bn1[:, a, 1:2], scale=bn1[:, a, 0:1]).then_inc(has_z, 1)

                    def product(j, s):
                        act.wait_ge(o_filled, j + 1)
                        act.activation(Y2[:, bass.ds(j, 1), :].rearrange("p a n -> p (a n)"), bank_a[s][:, :], ACT.Identity,
                                       bias=out_cols[:, 0:1]).then_inc(o_read, 1)

                    for j in range(AHEAD):
                        norm(j)
                    with act.Fori(0, B // RING - 1) as t:
                        for s in range(RING):
                            norm(RING * t + s + AHEAD)
                            product(RING * t + s, s)
                    for s in range(RING):
                        j = B - RING + s
                        if j + AHEAD < B:
                            norm(j + AHEAD)
                        product(j, s)

                @block.gpsimd
                def _(pool):
                    with pool.Fori(0, B // RING) as t:
                        for s in range(RING):
                            j = RING * t + s
                            pool.wait_ge(z_hi_1, j + 1)
                            pool.tensor_tensor(z.lo[:, s, 1, :], hidden(j, 1), as_f32(z.hi[:, s, 1, :]), ALU.subtract).then_inc(z_lo_1, 1)
                    pool.wait_ge(has_bvar, 2)
                    pool.tensor_tensor(bn_rstd[:, 2:3], bn_var[:, 2:3], pow_half[:, 0:1], ALU.pow).then_inc(has_brstd, 1)

                @block.vector
                def _(dve):
                    def split_z(j, s):
                        dve.wait_ge(has_z, HID * j + HID)
                        wait_some(dve, o_filled, j + 1 - RING)
                        for a in reversed(range(HID)):
                            last = dve.tensor_copy(z.hi[:, s, a, :], hidden(j, a))
                            if a == 1:
                                last.then_inc(z_hi_1, 1)
                        last.then_inc(z_hi_0, 1)
                        dve.wait_ge(z_hi_0, j + 1)
                        dve.tensor_tensor(z.lo[:, s, 0, :], hidden(j, 0), as_f32(z.hi[:, s, 0, :]), ALU.subtract).then_inc(z_lo_0, 1)

                    def product_stats(j):
                        dve.wait_ge(o_read, j + 1)
                        apart(dve, passed)
                        dve.bn_stats(stats2[:, bass.ds(j, 1), :].rearrange("p a s -> p (a s)"),
                                     Y2[:, bass.ds(j, 1), :].rearrange("p a n -> p (a n)")).then_inc(y_stats, 1)

                    LAG = 2
                    for s in range(RING):
                        split_z(s, s)
                        if s >= LAG:
                            product_stats(s - LAG)
                    with dve.Fori(1, B // RING) as t:
                        for s in range(RING):
                            split_z(RING * t + s, s)
                            product_stats(RING * t + s - LAG)
                    for j in range(B - LAG, B):
                        product_stats(j)
                    dve.wait_ge(y_stats, Y * PAIRS + B)
                    columns(dve, 2, 2, mv[:, 2:3, :], [stats2[:, :, :].rearrange("p b s -> p (b s)")],
                            bn2[:, :].unsqueeze(1), out_cols[:, 1:2], out_cols[:, 2:3], 1)



def phase_c(nc, sb, sb_split, sem, passed, bank_a, bank_b, X, ident, pow_half, at, Y2, bn2,
            wg0, bg0, wg1, bg1, wih, whh, bih, bhh, out_rows, B, N, D, KT, PAIRS, SKIP, GATES):
    STREAMS = 2
    GROUPS = PAIRS // STREAMS
    INPUT, FORGET, CELL, OUTPUT = range(GATES)
    UNITS = [(1, 0, 0, 1), (1, 0, 1, 2)] + [(p, t, 0, PAIR) for p in range(2, SKIP + 1) for t in range(p)]
    gates_of = lambda t: (INPUT, CELL, OUTPUT) if t == 0 else (INPUT, CELL, FORGET, OUTPUT)
    before = [sum(len(gates_of(u[1])) for u in UNITS[:n]) for n in range(len(UNITS) + 1)]
    READS = before[-1]
    CONV = 8
    AGG_0, ROWS, AGG_1, FEATURES = 0, 2, 4, 6
    HI_FIRST = 3
    NORMALISE_AT, SPLIT_AT = 2, 4
    wrapped = ExitStack()
    with wrapped as ctx:
        wih_t = sb_split(ctx, "wih_t", [P, SKIP, GATES * P])
        whh_t = sb_split(ctx, "whh_t", [P, SKIP - 1, GATES * P])
        wg = sb_split(ctx, "wg", [P, 2, D])
        bg = sb_split(ctx, "bg", [P, 2, D])
        gate_bias = sb(ctx, "gate_bias", [P, SKIP, GATES])
        bias0 = sb(ctx, "bias0", [P, KT, D])
        bias1 = sb(ctx, "bias1", [P, N])

        with ExitStack() as tmp:
            raw = sb(tmp, "lstm_raw", [P, 2 * SKIP - 1, GATES, D])
            wg_raw = sb(tmp, "wg_raw", [P, 2, D])
            bg_raw = sb(tmp, "bg_raw", [P, 2, D])
            bih_col = sb(tmp, "bih_col", [P, SKIP, GATES])
            bhh_col = sb(tmp, "bhh_col", [P, SKIP, GATES])
            params_in, small_hi = sem("l3_params_in"), sem("l3_small_hi")
            s_filled, s_hi, s_drained = sem("l3s_filled"), sem("l3s_hi"), sem("l3s_drained")
            has_y, y_filled, x2_done = sem("has_y"), sem("yt_filled"), sem("x2_done")
            LOADS = 6 + 2 * SKIP

            RING = 4
            y_norm = sb(tmp, "y_norm", [P, RING, N])

            with nc.Block() as block:
                @block.sync
                def _(sp):
                    with nc.allow_non_contiguous_dma(reason="parameter columns"):
                        sp.dma_start(raw[:, 0:SKIP, :, :], wih.rearrange("l (g p) h -> p l g h", p=P)).then_inc(params_in, 16)
                        sp.dma_start(raw[:, SKIP:2 * SKIP - 1, :, :],
                                     whh[1:SKIP].rearrange("l (g p) h -> p l g h", p=P)).then_inc(params_in, 16)
                        sp.dma_start(wg_raw[:, 0, :], wg0).then_inc(params_in, 16)
                        sp.dma_start(wg_raw[:, 1, :], wg1).then_inc(params_in, 16)
                        sp.dma_start(bg_raw[:, 0, :], bg0.partition_broadcast(P)).then_inc(params_in, 16)
                        sp.dma_start(bg_raw[:, 1, :], bg1.partition_broadcast(P)).then_inc(params_in, 16)
                        for l in range(SKIP):
                            sp.dma_start(bih_col[:, l, :], bih[l].rearrange("(g p) -> p g", p=P)).then_inc(params_in, 16)
                            sp.dma_start(bhh_col[:, l, :], bhh[l].rearrange("(g p) -> p g", p=P)).then_inc(params_in, 16)

                W = 2 * SKIP - 1

                def weights(f):
                    return (wih_t[:, f, :] if f < SKIP else whh_t[:, f - SKIP, :])

                @block.tensor
                def _(pe):
                    with pe.Fori(0, B // RING) as t:
                        for r in range(RING):
                            pe.wait_ge(has_y, RING * t + r + 1)
                            pe.wait_ge(x2_done, RING * t + r + 1)
                            for k in range(KT):
                                last = pe.transpose(bank_b[r][:, k * P:(k + 1) * P], y_norm[:, r, k * P:(k + 1) * P], ident[:, :])
                            last.then_inc(y_filled, 1)
                    pe.wait_ge(params_in, 16 * LOADS)
                    for f in range(W):
                        if f >= 4:
                            pe.wait_ge(s_drained, f - 3)
                        for g in range(GATES):
                            last = pe.transpose(bank_a[f % 4][:, g * P:(g + 1) * P], raw[:, f, g, :], ident[:, :])
                        last.then_inc(s_filled, 1)

                @block.scalar
                def _(act):
                    with act.Fori(0, B // RING) as t:
                        for r in range(RING):
                            act.wait_ge(x2_done, RING * t + r + 1)
                            act.activation(y_norm[:, r, :], Y2[:, bass.ds(RING * t + r, 1), :].rearrange("p a n -> p (a n)"),
                                           ACT.Identity, bias=bn2[:, 1:2], scale=bn2[:, 0:1]).then_inc(has_y, 1)
                    act.wait_ge(params_in, 16 * LOADS)
                    act.activation(wg.hi[:, :, :], wg_raw[:, :, :], ACT.Copy).then_inc(small_hi, 1)
                    act.activation(bg.hi[:, :, :], bg_raw[:, :, :], ACT.Copy).then_inc(small_hi, 1)
                    for f in range(W):
                        act.wait_ge(s_filled, f + 1)
                        act.activation(weights(f).hi, bank_a[f % 4][:, :], ACT.Copy).then_inc(s_hi, 1)

                @block.vector
                def _(dve):
                    for _ in range(RING):
                        dve.engine_nop().then_inc(x2_done, 1)
                    with dve.Fori(0, B // RING) as t:
                        for r in range(RING):
                            dve.wait_ge(y_filled, RING * t + r + 1)
                            xs = X[:, :, bass.ds(RING * t + r, 1), :].rearrange("p k a d -> p k (a d)")
                            dve.tensor_tensor(xs, bank_b[r][:, :].rearrange("p (k d) -> p k d", k=KT), xs, ALU.add).then_inc(x2_done, 1)
                    dve.wait_ge(small_hi, 2)
                    dve.tensor_tensor(wg.lo[:, :, :], wg_raw[:, :, :], as_f32(wg.hi[:, :, :]), ALU.subtract)
                    dve.tensor_tensor(bg.lo[:, :, :], bg_raw[:, :, :], as_f32(bg.hi[:, :, :]), ALU.subtract)
                    dve.tensor_tensor(gate_bias[:, :, :], bih_col[:, :, :], bhh_col[:, :, :], ALU.add)
                    for f in range(W):
                        dve.wait_ge(s_hi, f + 1)
                        dve.tensor_tensor(weights(f).lo, bank_a[f % 4][:, :], as_f32(weights(f).hi), ALU.subtract).then_inc(s_drained, 1)

        class Stream:
            def __init__(self, s):
                n = f"s{s}_"
                self.number = s
                self.banks = (bank_a, bank_b)[s]
                self.rows = sb(ctx, n + "rows", [P, PAIR, KT, D])
                self.h = sb_split(ctx, n + "h", [P, PAIR, N])
                self.agg = sb_split(ctx, n + "agg", [P, PAIR, N])
                self.f = self.agg.view("p b (k d) -> p b k d", k=KT)
                self.h1 = sb_split(ctx, n + "h1", [P, PAIR, KT, D])
                self.step = self.h1.view("p b k d -> p (b k d)")
                self.gates = sb(ctx, n + "gates", [P, GATES, N])
                self.full = self.gates[:, 0:2, :]
                self.c = sb(ctx, n + "c", [P, N])
                self.tc = sb(ctx, n + "tc", [P, N])
                self.h_full = self.rows[:, :, :, :].rearrange("p b k d -> p (b k d)")
                self.ln = Norm(sb, ctx, sem, passed, n + "ln3", self.rows[:, :, :, :].rearrange("p b k d -> p k b d"), KT)
                self.filled = sem(n + "filled")
                self.hi = sem(n + "hi")
                self.drained = sem(n + "drained")
                self.f_hi = sem(n + "f_hi")
                self.f_lo = sem(n + "f_lo")
                self.has_full = sem(n + "has_full")
                self.relu_hi = sem(n + "relu_hi")
                self.relu_lo = sem(n + "relu_lo")
                self.gates_full = sem(n + "gates_full")
                self.gates_read = sem(n + "gates_read")
                self.kept = sem(n + "kept")
                self.added = sem(n + "added")
                self.has_c = sem(n + "has_c")
                self.has_tc = sem(n + "has_tc")
                self.has_h = sem(n + "has_h")
                self.h_hi = sem(n + "h_hi")
                self.h_lo = sem(n + "h_lo")
                self.has_h_full = sem(n + "has_h_full")
                self.out_filled = sem(n + "out_filled")
                self.x_done = sem(n + "x_done")
                self.stored = sem(n + "stored")

        streams = [Stream(s) for s in range(STREAMS)]

        def columns(unit, q=None):
            p, t, b0, b1 = unit
            n = N // p
            return n, b1 - b0, slice(b0, b1), slice(t, t + (n - 1) * p + 1, p)

        def windows(part, unit):
            _, _, bs, ts = columns(unit)
            return part[:, bs, ts]

        def by_batch(ap, unit):
            n, nb, _, _ = columns(unit)
            return ap[:, 0:nb * n].rearrange("p (b n) -> p b n", b=nb)

        UN = len(UNITS)
        ORDER = [(s, n) for s in streams for n in range(2)] + [(s, n) for n in range(2, UN) for s in streams]
        later = [n for n, unit in enumerate(UNITS) if unit[1] > 0]

        def bank_of(s, f):
            return s.banks[(f + 2) % 4]

        bias_filled = sem("l3_bias_filled")
        with nc.Block() as block:
            @block.scalar
            def _(act):
                def split_input(s, u):
                    act.wait_ge(s.ln.has_rows, u + 1)
                    act.activation(s.f.hi, s.rows[:, :, :, :], ACT.Relu).then_inc(s.f_hi, 1)

                def agg(s, u, first, n, batches=range(PAIR)):
                    for b in batches:
                        act.wait_ge(s.filled, CONV * u + first + b + 1)
                        act.activation(s.agg.hi[:, b, :], bank_of(s, first + b)[:, :], ACT.Copy).then_inc(s.hi, 1)

                def relu(s, u, n, dst):
                    for b in range(PAIR):
                        act.wait_ge(s.has_full, 2 * PAIR * u + PAIR * n + b + 1)
                        act.activation(dst[:, b, :], s.full[:, b, :], ACT.Relu).then_inc(s.relu_hi, 1)

                def lstm_step(s, u, n):
                    p, t, _, _ = UNITS[n]
                    width = columns(UNITS[n])[0] * columns(UNITS[n])[1]
                    if n == 0:
                        act.wait_ge(s.relu_lo, 2 * PAIR * u + 2 * PAIR)
                    else:
                        act.wait_ge(s.has_h, UN * u + n)
                    for m, g in enumerate(gates_of(t)):
                        act.wait_ge(s.gates_full, READS * u + before[n] + m + 1)
                        act.activation(s.gates[:, g, 0:width], s.banks[g][:, 0:width], ACT.Tanh if g == CELL else ACT.Sigmoid,
                                       bias=gate_bias[:, p - 1, g:g + 1]).then_inc(s.gates_read, 1)
                    act.wait_ge(s.has_c, UN * u + n + 1)
                    act.activation(s.tc[:, 0:width], s.c[:, 0:width], ACT.Tanh).then_inc(s.has_tc, 1)

                def turn(u, ahead):
                    for s in streams:
                        relu(s, u, 0, s.h1.hi[:, :, :, :].rearrange("p b k d -> p b (k d)"))
                    s0, s1 = streams
                    agg(s0, u, AGG_1, 1)
                    agg(s1, u, AGG_1, 1, (0,))
                    relu(s0, u, 1, s0.h.hi)
                    agg(s1, u, AGG_1, 1, (1,))
                    for s, n in ORDER:
                        if (s, n) == ORDER[1]:
                            relu(s1, u, 1, s1.h.hi)
                        lstm_step(s, u, n)
                        if ahead and n == NORMALISE_AT:
                            s.ln.normalise(act, X, STREAMS * (u + 1) + s.number, u + 1)
                        if ahead and n == SPLIT_AT:
                            split_input(s, u + 1)
                    if ahead:
                        for s in streams:
                            agg(s, u + 1, AGG_0, 0)

                for s in streams:
                    split_input(s, 0)
                for s in streams:
                    agg(s, 0, AGG_0, 0)
                with act.Fori(0, GROUPS - 1) as u:
                    turn(u, True)
                turn(GROUPS - 1, False)

            @block.gpsimd
            def _(pool):
                def lstm_product(s, u, n):
                    width = columns(UNITS[n])[0] * columns(UNITS[n])[1]
                    pool.wait_ge(s.gates_read, READS * u + before[n] + 2)
                    pool.tensor_tensor(s.gates[:, CELL, 0:width], s.gates[:, INPUT, 0:width], s.gates[:, CELL, 0:width],
                                       ALU.mult).then_inc(s.added, 1)

                def turn(u, ahead):
                    if ahead:
                        for s in streams:
                            s.ln.scales(pool, pow_half, u + 1)
                    for s, n in ORDER:
                        if n in later:
                            lstm_product(s, u, n)

                for s in streams:
                    s.ln.scales(pool, pow_half, 0)
                with pool.Fori(0, GROUPS - 1) as u:
                    turn(u, True)
                turn(GROUPS - 1, False)

            @block.tensor
            def _(pe):
                def convolve(s, first, src, b):
                    for k in range(KT):
                        last = split_matmul(pe, bank_of(s, first + b)[:, :], src[:, b, k, :], at[:, k, :], k == 0, k == KT - 1)
                    last.then_inc(s.filled, 1)

                def conv_input(s, u):
                    pe.wait_ge(s.f_lo, u + 1)
                    for b in range(PAIR):
                        convolve(s, AGG_0, s.f, b)

                def by_rows(s, u):
                    pe.wait_ge(s.x_done, PAIR * u + 1)
                    for b in range(PAIR):
                        pe.wait_ge(s.drained, 4 * u + b + 1)
                        for nt in range(KT):
                            last = split_matmul(pe, bank_of(s, ROWS + b)[:, nt * D:(nt + 1) * D], s.agg[:, b, nt * P:(nt + 1) * P],
                                                wg[:, 0, :], True, True)
                        last.then_inc(s.filled, 1)

                def conv_h1(s, u, batches=range(PAIR)):
                    for b in batches:
                        pe.wait_ge(s.relu_lo, 2 * PAIR * u + b + 1)
                        convolve(s, AGG_1, s.h1, b)

                def by_features(s, u):
                    for b in range(PAIR):
                        pe.wait_ge(s.drained, 4 * u + PAIR + b + 1)
                        split_matmul(pe, bank_of(s, FEATURES + b)[:, :], wg[:, 1, :], s.agg[:, b, :], True, True).then_inc(s.filled, 1)

                def lstm_product(s, u, n, gates, out, w, x, start):
                    pe.wait_ge(s.h_hi, UN * u + n)
                    for g in gates[:HI_FIRST]:
                        pe.matmul(out(g), w(g).hi, x.hi, start=start, stop=False)
                        pe.matmul(out(g), w(g).lo, x.hi, start=False, stop=False)
                    pe.wait_ge(s.h_lo, UN * u + n)
                    for g in gates[:HI_FIRST]:
                        pe.matmul(out(g), w(g).hi, x.lo, start=False, stop=True).then_inc(s.gates_full, 1)
                    for g in gates[HI_FIRST:]:
                        split_matmul(pe, out(g), w(g), x, start, True).then_inc(s.gates_full, 1)

                def lstm_step(s, u, n):
                    unit = UNITS[n]
                    p, t, b0, b1 = unit
                    width = columns(unit)[0] * columns(unit)[1]
                    x = Split(windows(s.h.hi, unit), windows(s.h.lo, unit))
                    w_x = lambda g: wih_t[:, p - 1, g * P:(g + 1) * P]
                    w_h = lambda g: whh_t[:, p - 2, g * P:(g + 1) * P]
                    out_x = lambda g: by_batch(s.banks[g], unit)
                    out_h = lambda g: s.banks[g][:, 0:width]
                    if p == 1:
                        pe.wait_ge(s.relu_lo, 2 * PAIR * u + PAIR + b1)
                    for g in gates_of(t):
                        users = [k for k in range(n) if g in gates_of(UNITS[k][1])]
                        if users:
                            pe.wait_ge(s.gates_read, READS * u + before[users[-1]] + gates_of(UNITS[users[-1]][1]).index(g) + 1)
                        if p == 1:
                            split_matmul(pe, out_x(g), w_x(g), x, True, True).then_inc(s.gates_full, 1)
                        elif t > 0:
                            split_matmul(pe, out_x(g), w_x(g), x, True, False)
                    if p > 1 and t == 0:
                        lstm_product(s, u, n, gates_of(t), out_x, w_x, x, True)
                    if t > 0:
                        lstm_product(s, u, n, gates_of(t), out_h, w_h, s.step[:, 0:width], False)

                def out_rows_of(s, u):
                    pe.wait_ge(s.has_h_full, u + 1)
                    for b in range(PAIR):
                        for k in range(KT):
                            c = b * N + k * P
                            last = pe.transpose(s.banks[b][:, k * P:(k + 1) * P], s.h_full[:, c:c + P], ident[:, :])
                        last.then_inc(s.out_filled, 1)

                def turn(u, ahead):
                    for s in streams:
                        by_rows(s, u)
                    s0, s1 = streams
                    conv_h1(s0, u)
                    conv_h1(s1, u, (0,))
                    by_features(s0, u)
                    conv_h1(s1, u, (1,))
                    for s, n in ORDER:
                        if (s, n) == ORDER[1]:
                            by_features(s1, u)
                        lstm_step(s, u, n)
                    for s in streams:
                        pe.wait_ge(s.gates_read, READS * (u + 1))
                        if ahead:
                            conv_input(s, u + 1)
                        out_rows_of(s, u)

                for nt in range(KT):
                    for k in range(KT):
                        last = split_matmul(pe, bank_a[0][:, nt * D:(nt + 1) * D], at[:, k, nt * P:(nt + 1) * P], bg[:, 0, :],
                                            k == 0, k == KT - 1)
                last.then_inc(bias_filled, 1)
                for k in range(KT):
                    last = split_matmul(pe, bank_b[0][:, :], bg[:, 1, :], at[:, k, :], k == 0, k == KT - 1)
                last.then_inc(bias_filled, 1)
                for s in streams:
                    conv_input(s, 0)
                with pe.Fori(0, GROUPS - 1) as u:
                    turn(u, True)
                turn(GROUPS - 1, False)

            @block.vector
            def _(dve):
                def pair_of(s, u):
                    return STREAMS * u + s.number

                def split_input(s, u):
                    dve.wait_ge(s.f_hi, u + 1)
                    flat = "p b k d -> p (b k d)"
                    dve.scalar_tensor_tensor(s.f.lo.rearrange(flat), s.rows[:, :, :, :].rearrange(flat), 0.0,
                                             as_f32(s.f.hi).rearrange(flat), ALU.max, ALU.subtract).then_inc(s.f_lo, 1)

                def agg(s, u, first, n, batches=range(PAIR)):
                    for b in batches:
                        dve.wait_ge(s.hi, 2 * PAIR * u + PAIR * n + b + 1)
                        dve.tensor_tensor(s.agg.lo[:, b, :], bank_of(s, first + b)[:, :], as_f32(s.agg.hi[:, b, :]),
                                          ALU.subtract).then_inc(s.drained, 1)

                def with_bias(s, u, first, bias):
                    for b in range(PAIR):
                        dve.wait_ge(s.filled, CONV * u + first + b + 1)
                        dve.tensor_tensor(s.full[:, b, :], bank_of(s, first + b)[:, :], bias, ALU.add).then_inc(s.has_full, 1)

                def relu_rest(s, u, n, hi, lo):
                    for b in range(PAIR):
                        dve.wait_ge(s.relu_hi, 2 * PAIR * u + PAIR * n + b + 1)
                        dve.scalar_tensor_tensor(lo[:, b, :], s.full[:, b, :], 0.0, as_f32(hi[:, b, :]), ALU.max, ALU.subtract)\
                            .then_inc(s.relu_lo, 1)

                def lstm_cell(s, u, n):
                    width = columns(UNITS[n])[0] * columns(UNITS[n])[1]
                    t = UNITS[n][1]
                    c = s.c[:, 0:width]
                    if t == 0:
                        dve.wait_ge(s.gates_read, READS * u + before[n] + 2)
                        dve.tensor_tensor(c, s.gates[:, INPUT, 0:width], s.gates[:, CELL, 0:width], ALU.mult).then_inc(s.has_c, 1)
                        return
                    dve.wait_ge(s.gates_read, READS * u + before[n] + 3)
                    dve.tensor_tensor(c, c, s.gates[:, FORGET, 0:width], ALU.mult).then_inc(s.kept, 1)
                    dve.wait_ge(s.kept, len(later) * u + later.index(n) + 1)
                    dve.wait_ge(s.added, len(later) * u + later.index(n) + 1)
                    dve.tensor_tensor(c, c, s.gates[:, CELL, 0:width], ALU.add).then_inc(s.has_c, 1)

                def lstm_h(s, u, n):
                    unit = UNITS[n]
                    p, t, _, _ = unit
                    width = columns(unit)[0] * columns(unit)[1]
                    tc, o = s.tc[:, 0:width], s.gates[:, OUTPUT, 0:width]
                    if t == p - 1:
                        tc_w, o_w = by_batch(s.tc, unit), by_batch(s.gates[:, OUTPUT, :], unit)
                        hi, lo = windows(s.h.hi, unit), windows(s.h.lo, unit)
                    else:
                        tc_w, o_w, hi, lo = tc, o, s.step.hi[:, 0:width], s.step.lo[:, 0:width]
                    dve.wait_ge(s.has_tc, UN * u + n + 1)
                    dve.tensor_tensor(hi, tc_w, o_w, ALU.mult).then_inc(s.h_hi, 1)
                    dve.wait_ge(s.h_hi, UN * u + n + 1)
                    dve.tensor_tensor(tc, tc, o, ALU.mult).then_inc(s.has_h, 1)
                    dve.wait_ge(s.has_h, UN * u + n + 1)
                    dve.tensor_tensor(lo, tc_w, as_f32(hi), ALU.subtract).then_inc(s.h_lo, 1)

                def whole_h(s, u):
                    dve.wait_ge(s.h_lo, UN * (u + 1))
                    dve.tensor_tensor(s.h_full, as_f32(s.h.hi[:, :, :]).rearrange("p b n -> p (b n)"),
                                      as_f32(s.h.lo[:, :, :]).rearrange("p b n -> p (b n)"), ALU.add).then_inc(s.has_h_full, 1)

                def x3(s, u):
                    for b in range(PAIR):
                        dve.wait_ge(s.out_filled, PAIR * u + b + 1)
                        xs = X[:, :, bass.ds(PAIR * pair_of(s, u) + b, 1), :].rearrange("p k a d -> p k (a d)")
                        dve.tensor_tensor(xs, s.banks[b][:, :].rearrange("p (k d) -> p k d", k=KT), xs, ALU.add).then_inc(s.x_done, 1)

                def turn(u, ahead):
                    for s in streams:
                        with_bias(s, u, ROWS, bias0[:, :, :].rearrange("p k d -> p (k d)"))
                        relu_rest(s, u, 0, s.h1.hi[:, :, :, :].rearrange("p b k d -> p b (k d)"),
                                  s.h1.lo[:, :, :, :].rearrange("p b k d -> p b (k d)"))
                    s0, s1 = streams
                    if ahead:
                        s0.ln.statistics(dve, X, pair_of(s0, u + 1), u + 1)
                    agg(s0, u, AGG_1, 1)
                    if ahead:
                        s1.ln.statistics(dve, X, pair_of(s1, u + 1), u + 1)
                    agg(s1, u, AGG_1, 1, (0,))
                    with_bias(s0, u, FEATURES, bias1[:, :])
                    relu_rest(s0, u, 1, s0.h.hi, s0.h.lo)
                    agg(s1, u, AGG_1, 1, (1,))
                    for s, n in ORDER:
                        if (s, n) == ORDER[1]:
                            with_bias(s1, u, FEATURES, bias1[:, :])
                            relu_rest(s1, u, 1, s1.h.hi, s1.h.lo)
                        lstm_cell(s, u, n)
                        lstm_h(s, u, n)
                        if ahead and n == SPLIT_AT:
                            split_input(s, u + 1)
                        if n == UN - 1:
                            whole_h(s, u)
                    for s in streams:
                        if ahead:
                            agg(s, u + 1, AGG_0, 0)
                        x3(s, u)

                for s in streams:
                    s.ln.statistics(dve, X, pair_of(s, 0), 0)
                for s in streams:
                    s.ln.normalise_dve(dve, X, pair_of(s, 0), 0)
                for s in streams:
                    split_input(s, 0)
                dve.wait_ge(bias_filled, 2)
                dve.tensor_copy(bias0[:, :, :].rearrange("p k d -> p (k d)"), bank_a[0][:, :])
                dve.tensor_copy(bias1[:, :], bank_b[0][:, :])
                for s in streams:
                    dve.engine_nop().then_inc(s.x_done, 1)
                for s in streams:
                    agg(s, 0, AGG_0, 0)
                with dve.Fori(0, GROUPS - 1) as u:
                    turn(u, True)
                turn(GROUPS - 1, False)

            @block.sync
            def _(sp):
                with sp.Fori(0, GROUPS) as u:
                    for s in streams:
                        for b in range(PAIR):
                            sp.wait_ge(s.x_done, PAIR * u + b + 2)
                            at_b = PAIR * (STREAMS * u + s.number) + b
                            sp.dma_start(out_rows[bass.ds(at_b, 1)].rearrange("a p k d -> p k (a d)"),
                                         X[:, :, bass.ds(at_b, 1), :].rearrange("p k a d -> p k (a d)")).then_inc(s.stored, 16)
                for s in streams:
                    sp.wait_ge(s.stored, 16 * PAIR * GROUPS)


_INS = ['x', 'adj', 'L0_gnn_alpha_train', 'L0_gnn_w', 'L0_gnn_d', 'L0_gnn_fc_in_w', 'L0_gnn_fc_in_b',
        'L1_gnn_W', 'L1_gnn_b_lin', 'L1_gnn_b',
        'L2_gnn_W1', 'L2_gnn_b1', 'L2_gnn_g1', 'L2_gnn_be1', 'L2_gnn_W2', 'L2_gnn_b2', 'L2_gnn_g2', 'L2_gnn_be2',
        'L3_gnn_Wg0', 'L3_gnn_bg0', 'L3_gnn_Wg1', 'L3_gnn_bg1', 'L3_gnn_Wih', 'L3_gnn_Whh', 'L3_gnn_bih', 'L3_gnn_bhh']
_OUTS = [((16, 512, 128), 'float32')]


def kernel(**inputs):
    import numpy as _np
    import concourse.bacc as _bacc
    from concourse import mybir as _mybir
    from concourse.bass_utils import run_bass_kernel_spmd as _run

    nc = _bacc.Bacc("TRN2", target_bir_lowering=False, num_devices=1)
    arrays, args = {}, []
    for name in _INS:
        a = _np.ascontiguousarray(inputs[name])
        arrays[f"in_{name}_dram"] = a
        args.append(nc.dram_tensor(f"in_{name}_dram", a.shape, _mybir.dt.from_np(a.dtype), kind="ExternalInput").ap())
    for i, (shape, dtype) in enumerate(_OUTS):
        dt = _mybir.dt.from_np(_np.dtype(dtype))
        args.append(nc.dram_tensor(f"out_{i}_dram", shape, dt, kind="ExternalOutput").ap())
    build(nc, *args)
    r = _run(nc, [arrays], core_ids=[0])
    got = tuple(r.results[0][f"out_{i}_dram"] for i in range(len(_OUTS)))
    return got[0]
```

```python
from contextlib import ExitStack
from math import comb

import concourse.bass as bass
from concourse import mybir
from concourse.alu_op_type import AluOpType as ALU

ACT = mybir.ActivationFunctionType
AX = mybir.AxisListType
F32 = mybir.dt.float32
F32R = mybir.dt.float32r

P = 128
STEPS = 8
DT = 1.0 / STEPS
LN_EPS = 1e-5
BN_EPS = 1e-5
MASKED = -1e16
SPLIT = 3
PAIR = 2


class Split:

    def __init__(self, hi, lo):
        self.hi, self.lo = hi, lo

    def __getitem__(self, key):
        return Split(self.hi[key], self.lo[key])

    def view(self, pattern, **sizes):
        return Split(self.hi.rearrange(pattern, **sizes), self.lo.rearrange(pattern, **sizes))


def as_f32(ap):
    return ap.bitcast(F32)


def split_matmul(pe, out, w, x, start, stop, shared=False):
    pe.matmul(out, w.hi, x.hi, start=start, stop=False, skip_group_check=shared)
    pe.matmul(out, w.hi, x.lo, start=False, stop=False, skip_group_check=shared)
    return pe.matmul(out, w.lo, x.hi, start=False, stop=stop, skip_group_check=shared)


def keep_warm(pe, bank, ident, count):
    for _ in range(count):
        pe.matmul(bank[:, 0:P], ident[:, :], ident[:, :], start=True, stop=True)


def wait_some(eng, sem, value):
    if not isinstance(value, int) or value > 0:
        eng.wait_ge(sem, value)


def apart(eng, passed):
    eng.sem_inc(passed)


def build(nc, x, adj, alpha, w, d, fc_w, fc_b, l1_w, l1_blin, l1_b, w1, b1, g1, be1, w2, b2, g2, be2,
          wg0, bg0, wg1, bg1, wih, whh, bih, bhh, out):
    B, N, D = x.shape
    KT = N // P
    PAIRS = B // PAIR
    HID = w1.shape[0] // P
    SKIP = wih.shape[0]
    GATES = 4
    assert D == P and PAIR == 2 and KT == 4 and HID == 2 and SKIP == 4

    x_rows = x.rearrange("b (k p) d -> b p k d", p=P)
    out_rows = out.rearrange("b (k p) d -> b p k d", p=P)

    top = ExitStack()
    with top:
        def sb(ctx, name, shape, dt=F32):
            return ctx.enter_context(nc.sbuf_tensor(name, shape, dt))[:]

        def sb_split(ctx, name, shape):
            return Split(sb(ctx, name + "_hi", shape, F32R), sb(ctx, name + "_lo", shape, F32R))

        def sem(name):
            return top.enter_context(nc.semaphore(name))

        bank_a = [top.enter_context(nc.psum_tensor(f"bank_a{i}", [P, 512], F32))[:] for i in range(4)]
        bank_b = [top.enter_context(nc.psum_tensor(f"bank_b{i}", [P, 512], F32))[:] for i in range(4)]

        X = sb(top, "X", [P, KT, B, D])
        ident = sb(top, "ident", [P, P])
        pow_half = sb(top, "pow_half", [P, 8])
        bn2 = sb(top, "bn2", [P, 2])
        rows_sum = sb(top, "rows_sum", [P, KT])
        passed = sem("passed")
        at = sb_split(top, "at", [P, KT, N])
        Y2 = sb(top, "Y2", [P, B, N])
        with ExitStack() as middle:
            ah_t = sb_split(middle, "ah_t", [P, KT, N])
            m1 = sb_split(middle, "m1", [P, KT, N])
            layer2 = dict(w1_t=m1[:, 2, 0:2 * P], w2_t=m1[:, 3, 0:2 * D].view("p (a d) -> p a d", a=2), agg_t=m1[:, 0:PAIR, :],
                          b1_col=sb(middle, "b1_col", [P, HID]), g1_col=sb(middle, "g1_col", [P, HID]),
                          be1_col=sb(middle, "be1_col", [P, HID]), out_cols=sb(middle, "out_cols", [P, 3]))
            ln2 = Norm(sb, middle, sem, passed, "ln2", None, KT, PAIRS)
            phase_a(nc, sb, sb_split, sem, passed, bank_a, bank_b, X, ident, pow_half, [None, m1, ah_t, at], Y2, rows_sum, ln2, layer2,
                    x_rows, adj, alpha, w, d, fc_w, fc_b, l1_w, l1_blin, l1_b, w1, b1, g1, be1, w2, b2, g2, be2,
                    B, N, D, KT, PAIRS, HID)
            phase_b(nc, sb, sb_split, sem, passed, bank_a, bank_b, X, ident, pow_half, ah_t, Y2, bn2, ln2, layer2,
                    B, N, D, KT, PAIRS, HID)
        phase_c(nc, sb, sb_split, sem, passed, bank_a, bank_b, X, ident, pow_half, at, Y2, bn2, rows_sum,
                wg0, bg0, wg1, bg1, wih, whh, bih, bhh, out_rows, B, N, D, KT, PAIRS, SKIP, GATES)



class Norm:

    def __init__(self, sb, ctx, sem, passed, name, rows, KT, kept=1):
        self.passed = passed
        self.kept = kept
        self.width = PAIR * KT
        self.stats = sb(ctx, name + "_stats", [P, self.width, 6])
        self.mv = sb(ctx, name + "_mv", [P, self.width, 2])
        self.var = sb(ctx, name + "_var", [P, self.width])
        self.neg_mean = sb(ctx, name + "_neg_mean", [P, self.width])
        self.rstd = sb(ctx, name + "_rstd", [P, kept * self.width])
        self.shift = sb(ctx, name + "_shift", [P, kept * self.width])
        self.rows = rows
        self.tiles = [(k, b) for k in range(KT) for b in range(PAIR)]
        self.has_stats, self.has_mv, self.has_var = sem(name + "_has_stats"), sem(name + "_has_mv"), sem(name + "_has_var")
        self.has_rstd, self.has_shift, self.has_rows = sem(name + "_has_rstd"), sem(name + "_has_shift"), sem(name + "_has_rows")

    def tile(self, X, pair, k, b):
        return X[:, k, bass.ds(pair * PAIR + b, 1), :].rearrange("p a d -> p (a d)")

    def of_turn(self, part, n):
        return part[:, :] if self.kept == 1 else part[:, bass.ds(n * self.width, self.width)]

    def of_tile(self, part, n, t):
        return part[:, t:t + 1] if self.kept == 1 else part[:, bass.ds(n * self.width + t, 1)]

    def statistics(self, dve, X, pair, n):
        apart(dve, self.passed)
        for t, (k, b) in enumerate(self.tiles):
            last = dve.bn_stats(self.stats[:, t, :], self.tile(X, pair, k, b))
        last.then_inc(self.has_stats, 1)
        dve.wait_ge(self.has_stats, n + 1)
        apart(dve, self.passed)
        for t in range(self.width):
            last = dve.bn_aggr(self.mv[:, t, :], self.stats[:, t, :])
        last.then_inc(self.has_mv, 1)
        dve.wait_ge(self.has_mv, n + 1)
        dve.tensor_scalar(self.neg_mean[:, :], self.mv[:, :, 0], -1.0, None, ALU.mult)
        dve.tensor_scalar(self.var[:, :], self.mv[:, :, 1], LN_EPS, None, ALU.add).then_inc(self.has_var, 1)

    def scales(self, pool, pow_half, n):
        rstd = self.of_turn(self.rstd, n)
        pool.wait_ge(self.has_var, n + 1)
        pool.tensor_tensor(rstd, self.var[:, :], pow_half[:, :], ALU.pow).then_inc(self.has_rstd, 1)
        pool.wait_ge(self.has_rstd, n + 1)
        pool.tensor_tensor(self.of_turn(self.shift, n), self.neg_mean[:, :], rstd, ALU.mult).then_inc(self.has_shift, 1)

    def normalise(self, act, X, pair, n):
        act.wait_ge(self.has_shift, n + 1)
        for t, (k, b) in enumerate(self.tiles):
            last = act.activation(self.rows[:, k, b, :], self.tile(X, pair, k, b), ACT.Identity,
                                  bias=self.of_tile(self.shift, n, t), scale=self.of_tile(self.rstd, n, t))
        last.then_inc(self.has_rows, 1)

    def normalise_dve(self, dve, X, pair, n, rows=None):
        rows = self.rows if rows is None else rows
        dve.wait_ge(self.has_shift, n + 1)
        for t, (k, b) in enumerate(self.tiles):
            last = dve.tensor_scalar(rows[:, k, b, :], self.tile(X, pair, k, b),
                                     self.of_tile(self.rstd, n, t), self.of_tile(self.shift, n, t), ALU.mult, ALU.add)
        last.then_inc(self.has_rows, 1)



def phase_a(nc, sb, sb_split, sem, passed, bank_a, bank_b, X, ident, pow_half, m_t, scratch, rows_sum, ln2, layer2,
            x_rows, adj, alpha, w, d, fc_w, fc_b, l1_w, l1_blin, l1_b, w1, b1, g1, be1, w2, b2, g2, be2,
            B, N, D, KT, PAIRS, HID):
    ctx = ExitStack()
    with ctx:
        m1, ah_t, at = m_t[1:]
        w1_t, w2_t = layer2["w1_t"], layer2["w2_t"]
        adj_rows = sb(ctx, "adj_rows", [P, KT, N])
        scores = scratch[:, 0:KT, :]
        probs = scratch[:, KT:2 * KT, :]
        g_full = scratch[:, 8:8 + PAIR, :]
        rows = scratch[:, 10:12, :].rearrange("p a n -> p (a n)").rearrange("p (k b d) -> p k b d", k=KT, b=PAIR)
        g_bias = scratch[:, 12:12 + SPLIT, :]
        out_t = scratch[:, 15, :]
        R = sb_split(ctx, "R", [P, STEPS + 1, D])
        w_l1 = sb_split(ctx, "w_l1", [P, D])
        blin_col = sb(ctx, "blin_col", [P, 1])
        b_row = sb(ctx, "b_row", [P, D])

        x0 = sb_split(ctx, "x0", [P, KT, PAIR, D])
        ln0 = Norm(sb, ctx, sem, passed, "ln0", rows, KT)

        x_in, x_first_in, adj_in, small_in = sem("x_in"), sem("x_first_in"), sem("adj_in"), sem("small_in")
        alpha_in, w_in = sem("alpha_in"), sem("w_in")
        x0_hi, x0_lo = sem("x0_hi"), sem("x0_lo")

        def round_x0(act, i):
            act.wait_ge(ln0.has_rows, i + 1)
            act.activation(x0.hi[:, :, :, :], rows[:, :, :, :], ACT.Relu).then_inc(x0_hi, 1)

        def rest_of_x0(dve, i):
            dve.wait_ge(x0_hi, i + 1)
            flat = "p k b d -> p (k b d)"
            dve.scalar_tensor_tensor(x0.lo[:, :, :, :].rearrange(flat), rows[:, :, :, :].rearrange(flat), 0.0,
                                     as_f32(x0.hi[:, :, :, :]).rearrange(flat), ALU.max, ALU.subtract).then_inc(x0_lo, 1)

        with ExitStack() as tmp:
            w_raw = sb(tmp, "w_raw", [P, D])
            fc_raw = sb(tmp, "fc_raw", [P, D])
            l1_raw = sb(tmp, "l1_raw", [P, D])
            d_col = sb(tmp, "d_col", [P, 1])
            fcb_col = sb(tmp, "fcb_col", [P, 1])
            alpha_col = sb(tmp, "alpha_col", [P, KT])
            gain = sb(tmp, "gain", [P, KT])
            keep = sb(tmp, "keep", [P, KT])
            w_t = sb(tmp, "w_t", [P, D])
            wd_t = sb(tmp, "wd_t", [P, D])
            v1 = sb(tmp, "v1", [P, D])
            powers = sb(tmp, "powers", [P, STEPS + 1, 2 * D + 1])
            r_sum = sb(tmp, "r_sum", [P, STEPS + 1, D])
            r_bias = sb(tmp, "r_bias", [P, STEPS + 1])
            m_rows = sb(tmp, "m_rows", [P, KT, N])
            m_split = sb_split(tmp, "m_split", [P, KT, N])
            ones = sb(tmp, "ones", [P, P], F32R)
            ones_f = sb(tmp, "ones_f", [P, P])

            has_ident, has_exp = sem("has_ident"), sem("has_exp")
            has_m_rows, m_rows_hi = sem("has_m_rows"), sem("m_rows_hi")
            has_m_split = sem("has_m_split")
            has_ones = sem("has_ones")
            v_filled, v_drained = sem("v_filled"), sem("v_drained")
            m_filled, m_hi, m_drained = sem("m_filled"), sem("m_hi"), sem("m_drained")
            u_filled, link_s, r_hi = sem("u_filled"), sem("setup_link"), sem("r_hi")
            r_full, w_hi = sem("r_full"), sem("w_l1_hi")

            SMALL = 5 * 16

            def v_rounds(f):
                i = 2 * (f - KT) + 1
                return [r for r in (i, i + 1) if 1 <= r <= STEPS]

            block = tmp.enter_context(nc.Block())

            @block.sync
            def _(sp):
                with nc.allow_non_contiguous_dma(reason="parameter columns"):
                    sp.dma_start(alpha_col[:, :], alpha.rearrange("(k p) -> p k", p=P)).then_inc(alpha_in, 16)
                    sp.dma_start(adj_rows[:, :, :], adj.rearrange("(k p) n -> p k n", p=P)).then_inc(adj_in, 16)
                    sp.dma_start(w_raw[:, :], w).then_inc(w_in, 16)
                    sp.dma_start(d_col[:, :], d.rearrange("(p a) -> p a", a=1)).then_inc(w_in, 16)
                    sp.dma_start(fc_raw[:, :], fc_w).then_inc(small_in, 16)
                    sp.dma_start(fcb_col[:, :], fc_b.rearrange("(p a) -> p a", a=1)).then_inc(small_in, 16)
                    sp.dma_start(l1_raw[:, :], l1_w).then_inc(small_in, 16)
                    sp.dma_start(blin_col[:, :], l1_blin.rearrange("(p a) -> p a", a=1)).then_inc(small_in, 16)
                    sp.dma_start(b_row[:, :], l1_b.partition_broadcast(P)).then_inc(small_in, 16)
                for b in range(PAIR):
                    sp.dma_start(X[:, :, b, :], x_rows[b]).then_inc(x_first_in, 16)
                with sp.Fori(PAIR, B) as b:
                    sp.dma_start(X[:, :, bass.ds(b, 1), :].rearrange("p k a d -> p k (a d)"),
                                 x_rows[bass.ds(b, 1)].rearrange("a p k d -> p k (a d)")).then_inc(x_in, 16)

            @block.gpsimd
            def _(pool):
                pool.memset(pow_half[:, :], -0.5)
                pool.memset(ident[:, :], 0.0).then_inc(has_ident, 1)
                pool.wait_ge(has_ident, 1)
                pool.affine_select(out=ident[:, :], in_=ident[:, :], compare_op=ALU.not_equal, fill=1.0,
                                   base=0, pattern=[[-1, P]], channel_multiplier=1).then_inc(has_ident, 1)
                ln0.scales(pool, pow_half, 0)

            @block.scalar
            def _(act):
                act.wait_ge(alpha_in, 16)
                act.activation(gain[:, :], alpha_col[:, :], ACT.Exp, scale=-1.0).then_inc(has_exp, 1)
                for k in range(KT):
                    act.wait_ge(has_m_rows, k + 1)
                    act.activation(m_split.hi[:, k, :], m_rows[:, k, :], ACT.Copy).then_inc(m_rows_hi, 1)
                act.wait_ge(small_in, SMALL)
                act.activation(w_l1.hi[:, :], l1_raw[:, :], ACT.Copy).then_inc(w_hi, 1)
                for f in range(3 * KT):
                    act.wait_ge(m_filled, f + 1)
                    act.activation(m_t[f // KT + 1].hi[:, f % KT, :], bank_a[f % 4][:, :], ACT.Copy).then_inc(m_hi, 1)
                    if f == KT + 2:
                        ln0.normalise(act, X, 0, 0)
                    if f == KT + 3:
                        round_x0(act, 0)
                    if f == 2 * KT:
                        act.wait_ge(r_full, 1)
                        act.activation(R.hi[:, :, :], r_sum[:, :, :], ACT.Copy).then_inc(r_hi, 1)

            @block.tensor
            def _(pe):
                pe.wait_ge(w_in, 2 * 16)
                pe.wait_ge(has_ident, 2)
                pe.transpose(bank_b[2][:, 0:D], w_raw[:, :], ident[:, :]).then_inc(v_filled, 1)
                pe.wait_ge(v_drained, 1)
                pe.matmul(bank_b[3][:, 0:D], wd_t[:, :], w_t[:, :], start=True, stop=True).then_inc(v_filled, 1)

                def v_round(i):
                    pe.wait_ge(v_drained, i + 2)
                    v_i = ident[:, :] if i == 0 else powers[:, i - 1, 0:D]
                    bank = bank_b[i % 2]
                    pe.matmul(bank[:, 0:D], v1[:, :], v_i, start=True, stop=True)
                    pe.matmul(bank[:, D:2 * D], fc_raw[:, :], v_i, start=True, stop=True)
                    pe.matmul(bank[:, 2 * D:2 * D + 1], v_i, fcb_col[:, :], start=True, stop=True).then_inc(v_filled, 1)

                def m_fill(f):
                    power, mt = f // KT + 1, f % KT
                    rounds = v_rounds(f)
                    for i in rounds[:1]:
                        v_round(i)
                    if f >= 4:
                        pe.wait_ge(m_drained, f - 3)
                    if power == 1:
                        for nt in range(KT):
                            last = pe.transpose(bank_a[f % 4][:, nt * P:(nt + 1) * P],
                                                m_rows[:, nt, mt * P:(mt + 1) * P], ident[:, :])
                    else:
                        pe.wait_ge(m_drained, KT * (power - 1))
                        for kt in range(KT):
                            last = split_matmul(pe, bank_a[f % 4][:, :], m_split[:, kt, mt * P:(mt + 1) * P],
                                                m_t[power - 1][:, kt, :], kt == 0, kt == KT - 1)
                            if kt == 1:
                                for i in rounds[1:]:
                                    v_round(i)
                    last.then_inc(m_filled, 1)

                pe.wait_ge(small_in, SMALL)
                v_round(0)
                pe.wait_ge(has_m_rows, KT)
                for f in range(KT):
                    m_fill(f)
                pe.wait_ge(has_m_split, 1)
                for f in range(KT, 3 * KT):
                    m_fill(f)
                    if f == 2 * KT:
                        pe.wait_ge(has_ones, 1)
                        for q in (1, 2):
                            for n, part in enumerate((m_t[q].hi, m_t[q].lo)):
                                for kt in range(KT):
                                    last = pe.matmul(bank_b[q + 1][:, :], ones[:, :], part[:, kt, :],
                                                     start=(n == 0 and kt == 0), stop=(n == 1 and kt == KT - 1))
                        last.then_inc(u_filled, 1)

            @block.vector
            def _(dve):
                done = [0]

                def link(ins):
                    done[0] += 1
                    ins.then_inc(link_s, 1)
                    dve.wait_ge(link_s, done[0])

                link(dve.memset(ones_f[:, :], 1.0))
                dve.tensor_copy(ones[:, :], ones_f[:, :]).then_inc(has_ones, 1)
                dve.wait_ge(has_exp, 1)
                link(dve.tensor_scalar(gain[:, :], gain[:, :], 1.0, None, ALU.add))
                link(dve.reciprocal(gain[:, :], gain[:, :]))
                link(dve.tensor_scalar(gain[:, :], gain[:, :], 0.5 * DT, None, ALU.mult))
                link(dve.tensor_scalar(keep[:, :], gain[:, :], -1.0, 1.0 - DT, ALU.mult, ALU.add))
                dve.wait_ge(adj_in, 16)
                dve.wait_ge(has_ident, 2)
                for k in range(KT):
                    link(dve.tensor_scalar(m_rows[:, k, :], adj_rows[:, k, :], gain[:, k:k + 1], None, ALU.mult))
                    blk = m_rows[:, k, k * P:(k + 1) * P]
                    dve.scalar_tensor_tensor(blk, ident[:, :], keep[:, k:k + 1], blk, ALU.mult, ALU.add).then_inc(has_m_rows, 1)
                    if k == 0:
                        dve.wait_ge(w_in, 2 * 16)
                        link(dve.tensor_scalar(d_col[:, :], d_col[:, :], 0.0, 1.0, ALU.max, ALU.min))
                        dve.wait_ge(v_filled, 1)
                        dve.tensor_copy(w_t[:, :], bank_b[2][:, 0:D])
                        dve.tensor_scalar(wd_t[:, :], bank_b[2][:, 0:D], d_col[:, 0:1], None, ALU.mult).then_inc(v_drained, 1)
                dve.wait_ge(v_filled, 2)
                dve.tensor_scalar(v1[:, :], bank_b[3][:, 0:D], DT, None, ALU.mult).then_inc(v_drained, 1)
                for k in range(KT):
                    dve.wait_ge(m_rows_hi, k + 1)
                    last = dve.tensor_tensor(m_split.lo[:, k, :], m_rows[:, k, :], as_f32(m_split.hi[:, k, :]), ALU.subtract)
                last.then_inc(has_m_split, 1)
                dve.wait_ge(w_hi, 1)
                dve.tensor_tensor(w_l1.lo[:, :], l1_raw[:, :], as_f32(w_l1.hi[:, :]), ALU.subtract)

                def v_drain(i):
                    dve.wait_ge(v_filled, i + 3)
                    dve.tensor_copy(powers[:, i, :], bank_b[i % 2][:, 0:2 * D + 1]).then_inc(v_drained, 1)

                def m_drain(f):
                    dve.wait_ge(m_hi, f + 1)
                    dve.tensor_tensor(m_t[f // KT + 1].lo[:, f % KT, :], bank_a[f % 4][:, :],
                                      as_f32(m_t[f // KT + 1].hi[:, f % KT, :]), ALU.subtract).then_inc(m_drained, 1)

                def add_power(i):
                    dve.wait_ge(v_drained, i + 3)
                    k = STEPS - i
                    c = float(comb(STEPS, k))
                    dve.tensor_scalar(r_bias[:, k:k + 1], powers[:, i, 2 * D:2 * D + 1], c, None, ALU.mult)
                    v_i = ident[:, :] if i == 0 else powers[:, i - 1, 0:D]
                    f_v = powers[:, i, D:2 * D]
                    if i == 0:
                        link(dve.tensor_scalar(r_sum[:, k, :], f_v, c, None, ALU.mult))
                        for k in range(STEPS):
                            last = dve.tensor_scalar(r_sum[:, k, :], v_i, DT, None, ALU.mult)
                    else:
                        last = dve.scalar_tensor_tensor(r_sum[:, k, :], f_v, c, r_sum[:, k, :], ALU.mult, ALU.add)
                        for k in range(STEPS - i):
                            last = dve.scalar_tensor_tensor(r_sum[:, k, :], v_i, DT * comb(k + i, k), r_sum[:, k, :],
                                                            ALU.mult, ALU.add)
                    link(last)

                v_drain(0)
                for f in range(KT):
                    m_drain(f)
                for f in range(KT, 3 * KT):
                    rounds = v_rounds(f)
                    for i in rounds[:1]:
                        v_drain(i)
                    if f == KT:
                        add_power(0)
                    if f == KT + 1:
                        dve.wait_ge(x_first_in, 16 * PAIR)
                        ln0.statistics(dve, X, 0, 0)
                    if f in (KT + 2, KT + 3):
                        add_power(f - KT - 1)
                    for i in rounds[1:]:
                        v_drain(i)
                    m_drain(f)
                    if f == 2 * KT - 1:
                        for i in range(3, STEPS + 1):
                            add_power(i)
                        dve.engine_nop().then_inc(r_full, 1)
                    if f == 2 * KT:
                        dve.wait_ge(u_filled, 1)
                        for j in range(SPLIT):
                            k = SPLIT * j
                            last = dve.tensor_scalar(g_bias[:, j, :], bank_b[2][:, :], r_bias[:, k + 1:k + 2], r_bias[:, k:k + 1],
                                                     ALU.mult, ALU.add)
                        link(last)
                        for j in range(SPLIT):
                            k = SPLIT * j
                            dve.scalar_tensor_tensor(g_bias[:, j, :], bank_b[3][:, :], r_bias[:, k + 2:k + 3], g_bias[:, j, :],
                                                     ALU.mult, ALU.add)
                    if f == 2 * KT + 1:
                        dve.wait_ge(r_hi, 1)
                        dve.tensor_tensor(R.lo[:, :, :], r_sum[:, :, :], as_f32(R.hi[:, :, :]), ALU.subtract)
                    if f == 2 * KT + 2:
                        rest_of_x0(dve, 0)

        x_t = sb_split(ctx, "x_t", [P, SPLIT, PAIR, N])
        g_rows = sb_split(ctx, "g_rows", [P, PAIR, KT, D])
        hn_t = sb_split(ctx, "hn_t", [P, PAIR, N])
        h_t = sb_split(ctx, "h_t", [P, PAIR, N])
        h_full = scores
        probs_t = sb_split(ctx, "probs_t", [P, KT, N])
        w1_raw = sb(ctx, "w1_raw", [P, HID, D])
        w2_raw = sb(ctx, "w2_raw", [P, HID * P])
        diag = sb(ctx, "diag", [P, KT])
        deg = sb(ctx, "deg", [P, KT])
        cols_sum = sb(ctx, "cols_sum", [P, KT])
        dinv = sb(ctx, "dinv", [P, KT])
        diag_dinv = g_bias[:, 0, :].rearrange("p (k n) -> p k n", k=KT)
        ones_f = g_bias[:, 1, 0:P]
        dinv_row = g_bias[:, 2, :]
        l2_params_in = sem("l2_params_in")
        l_filled, l_hi, l_drained = sem("l2s_filled"), sem("l2s_hi"), sem("l2s_drained")
        l_scaled, l_lo = sem("l2s_scaled"), sem("l2s_lo")
        has_deg, has_dinv, has_diag_dinv = sem("has_deg"), sem("has_dinv"), sem("has_diag_dinv")
        has_dinv_row, link_l2 = sem("has_dinv_row"), sem("l2_link")
        neg_max = sb(ctx, "neg_max", [P, PAIR, KT])
        row_sum = sb(ctx, "row_sum", [P, PAIR, KT])
        inv_sum = sb(ctx, "inv_sum", [P, PAIR, KT])
        h_rows = hn_t.view("p b (k d) -> p b k d", k=KT)

        ln1 = Norm(sb, ctx, sem, passed, "ln1", rows, KT)
        a_filled, a_hi, a_drained = sem("a_filled"), sem("a_hi"), sem("a_drained")
        b_filled, b_hi, b_drained, b_full = sem("b_filled"), sem("b_hi"), sem("b_drained"), sem("b_full")
        has_xb, has_neg, has_mask, has_probs = sem("has_xb"), sem("has_neg"), sem("has_mask"), sem("has_probs")
        has_inv, o_filled, o_drained = sem("has_inv"), sem("out_filled"), sem("out_drained")

        A, A_BANKS, A_SPLITS = 18, 3, 10
        C, C_BANKS, C_SPLITS = 24, 4, 14
        banks_0, banks_1, bank_out = bank_a[:3], [bank_a[3]] + bank_b[:3], bank_b[3]
        SCORES, PROBS, OUT = (6, 14), (10, 19), (18, 23)

        def power_of(f):
            return (0, f) if f < 2 else ((f - 2) % 2 + 1, (f - 2) // 2)

        W_FILL, DINV_FILL, SCALED = 4, 5, 6

        with nc.Block() as block:
            @block.sync
            def _(sp):
                with nc.allow_non_contiguous_dma(reason="parameter columns"):
                    sp.dma_start(w1_raw[:, :, :], w1.rearrange("(a p) d -> p a d", p=P)).then_inc(l2_params_in, 16)
                    sp.dma_start(w2_raw[:, :], w2).then_inc(l2_params_in, 16)
                    for name, src in (("b1_col", b1), ("g1_col", g1), ("be1_col", be1)):
                        sp.dma_start(layer2[name][:, :], src.rearrange("(a p) -> p a", p=P)).then_inc(l2_params_in, 16)
                    for n, src in enumerate((b2, g2, be2)):
                        sp.dma_start(layer2["out_cols"][:, n:n + 1], src.rearrange("(p a) -> p a", a=1)).then_inc(l2_params_in, 16)

            @block.tensor
            def _(pe):
                def adj_transposes(fills):
                    for f in fills:
                        if f >= A_BANKS:
                            pe.wait_ge(l_drained, f - A_BANKS + 1)
                        transpose_tiles(banks_0[f % A_BANKS],
                                        [adj_rows[:, nt, (f % SCALED) * P:(f % SCALED + 1) * P] for nt in range(KT)]).then_inc(l_filled, 1)

                def weight_transposes():
                    pe.wait_ge(l2_params_in, 8 * 16)
                    pe.wait_ge(l_drained, W_FILL - A_BANKS + 1)
                    transpose_tiles(banks_0[W_FILL % A_BANKS], [w1_raw[:, a, :] for a in range(HID)]
                                    + [w2_raw[:, a * P:(a + 1) * P] for a in range(HID)]).then_inc(l_filled, 1)

                def dinv_by_column():
                    pe.wait_ge(has_diag_dinv, 1)
                    pe.wait_ge(l_drained, DINV_FILL - A_BANKS + 1)
                    for k in range(KT):
                        last = pe.matmul(banks_0[DINV_FILL % A_BANKS][:, k * P:(k + 1) * P], ones_f, diag_dinv[:, k, :],
                                         start=True, stop=True)
                    last.then_inc(l_filled, 1)

                def a_slot(i, f):
                    pe.wait_ge(a_drained, A * i + f + 1)
                    return banks_0[f % A_BANKS]

                def c_slot(j, f):
                    pe.wait_ge(b_drained, C * j + f + 1)
                    return banks_1[f % C_BANKS]

                def transpose_tiles(bank, tiles):
                    for k, tile in enumerate(tiles):
                        last = pe.transpose(bank[:, k * P:(k + 1) * P], tile, ident[:, :])
                    return last

                def x0_transposes(i):
                    pe.wait_ge(ln0.has_rows, i + 1)
                    for b in range(PAIR):
                        transpose_tiles(a_slot(i, b), [rows[:, k, b, :] for k in range(KT)]).then_inc(a_filled, 1)

                def m_powers(i, b):
                    pe.wait_ge(x0_lo, i + 1)
                    for q in (1, 2):
                        bank = a_slot(i, 2 + 2 * b + q - 1)
                        for k in range(KT):
                            last = split_matmul(pe, bank[:, :], x0[:, k, b, :], m_t[q][:, k, :], k == 0, k == KT - 1)
                        last.then_inc(a_filled, 1)

                def g_term(i, j):
                    stage = SPLIT - 1 - j
                    for b in range(PAIR):
                        f = 6 + 4 * stage + b
                        bank = a_slot(i, f)
                        if stage == 0:
                            pe.wait_ge(a_drained, A * i + 3 + 2 * b + A_BANKS + 1)
                        for q in range(SPLIT):
                            last = split_matmul(pe, bank[:, :], R[:, SPLIT * j + q, :], x_t[:, q, b, :],
                                                q == 0, stage == 0 and q == SPLIT - 1)
                        if stage:
                            pe.wait_ge(a_drained, A * i + f - 2 + A_BANKS + 1)
                            for k in range(KT):
                                last = split_matmul(pe, bank[:, :], g_rows[:, b, k, :], m_t[3][:, k, :], False, k == KT - 1)
                        last.then_inc(a_filled, 1)

                def g_transposes(i, j):
                    for b in range(PAIR):
                        f = 8 + 4 * (SPLIT - 1 - j) + b
                        bank = a_slot(i, f)
                        pe.wait_ge(a_drained, A * i + f - 2 + A_BANKS + 1)
                        transpose_tiles(bank, [g_full[:, b, k * P:(k + 1) * P] for k in range(KT)]).then_inc(a_filled, 1)

                def in_transposes(j):
                    pe.wait_ge(ln1.has_rows, j + 1)
                    for b in range(PAIR):
                        transpose_tiles(c_slot(j, b), [rows[:, k, b, :] for k in range(KT)]).then_inc(b_filled, 1)

                def project(j):
                    for b in range(PAIR):
                        bank = c_slot(j, 2 + b)
                        pe.wait_ge(b_drained, C * j + b + C_BANKS + 1)
                        split_matmul(pe, bank[:, :], w_l1, hn_t[:, b, :], True, True).then_inc(b_filled, 1)

                def h_transposes(j):
                    for b in range(PAIR):
                        bank = c_slot(j, 4 + b)
                        pe.wait_ge(b_full, PAIR * j + b + 1)
                        transpose_tiles(bank, [h_full[:, b, k * P:(k + 1) * P] for k in range(KT)]).then_inc(b_filled, 1)

                def score(j, b):
                    pe.wait_ge(b_drained, C * j + 2 + b + C_BANKS + 1)
                    for nt in range(KT):
                        bank = c_slot(j, SCORES[b] + nt)
                        split_matmul(pe, bank[:, :], h_t[:, b, nt * P:(nt + 1) * P], h_t[:, b, :], True, True).then_inc(b_filled, 1)

                def probs_transposes(j, b):
                    pe.wait_ge(has_probs, 2 * KT * j + KT * b + KT)
                    for kt in range(KT):
                        transpose_tiles(c_slot(j, PROBS[b] + kt),
                                        [probs[:, nt, kt * P:(kt + 1) * P] for nt in range(KT)]).then_inc(b_filled, 1)

                def attend(j, b):
                    bank = c_slot(j, OUT[b])
                    for kt in range(KT):
                        pe.wait_ge(b_drained, C * j + PROBS[b] + kt + C_BANKS + 1)
                        last = split_matmul(pe, bank[:, :], h_rows[:, b, kt, :], probs_t[:, kt, :], kt == 0, kt == KT - 1)
                    last.then_inc(b_filled, 1)

                def out_transposes(j, b):
                    pe.wait_ge(b_drained, C * j + OUT[b] + C_BANKS + 1)
                    pe.wait_ge(o_drained, PAIR * j + b + 1)
                    transpose_tiles(bank_out, [out_t[:, k * P:(k + 1) * P] for k in range(KT)]).then_inc(o_filled, 1)

                def turn(i, zero, one):
                    j = i - 1
                    final = not zero
                    if zero:
                        x0_transposes(i)
                        m_powers(i, 0)
                    if final:
                        pe.wait_ge(a_drained, A * i + A_BANKS)
                        adj_transposes(range(0, A_BANKS))
                        pe.wait_ge(o_drained, PAIR * j + 1)
                        keep_warm(pe, bank_out, ident, 24)
                    if zero:
                        m_powers(i, 1)
                    if one:
                        in_transposes(j)
                    if final:
                        adj_transposes(range(A_BANKS, KT))
                    if one:
                        project(j)
                    if zero:
                        g_term(i, 2)
                    if one:
                        h_transposes(j)
                    if zero:
                        g_transposes(i, 2)
                    if one:
                        score(j, 0)
                    if zero:
                        g_term(i, 1)
                    if one:
                        probs_transposes(j, 0)
                    if zero:
                        g_transposes(i, 1)
                    if one:
                        score(j, 1)
                    if final:
                        weight_transposes()
                        dinv_by_column()
                    if one:
                        attend(j, 0)
                    if final:
                        adj_transposes(range(SCALED, SCALED + 2))
                    if zero:
                        g_term(i, 0)
                    if one:
                        out_transposes(j, 0)
                        probs_transposes(j, 1)
                    if final:
                        adj_transposes(range(SCALED + 2, SCALED + KT))
                    if zero:
                        g_transposes(i, 0)
                    if one:
                        attend(j, 1)
                        out_transposes(j, 1)

                turn(0, True, False)
                with pe.Fori(1, PAIRS) as i:
                    turn(i, True, True)
                turn(PAIRS, False, True)

            @block.scalar
            def _(act):
                def a_round(i, f, n, dst, func=ACT.Copy):
                    act.wait_ge(a_filled, A * i + f + 1)
                    act.activation(dst, banks_0[f % A_BANKS][:, :], func).then_inc(a_hi, 1)

                def power_round(i, f):
                    q, b = power_of(f)
                    a_round(i, f, f, x_t.hi[:, q, b, :], ACT.Relu if q == 0 else ACT.Copy)

                def g_round(i, j):
                    for b in range(PAIR):
                        a_round(i, 8 + 4 * (SPLIT - 1 - j) + b, 0, g_rows.hi[:, b, :, :].rearrange("p k d -> p (k d)"))

                def c_round(j, f, dst, func=ACT.Copy):
                    act.wait_ge(b_filled, C * j + f + 1)
                    act.activation(dst, banks_1[f % C_BANKS][:, :], func).then_inc(b_hi, 1)

                def project(j):
                    for b in range(PAIR):
                        act.wait_ge(b_filled, C * j + 2 + b + 1)
                        bank = banks_1[2 + b]
                        act.activation(h_full[:, b, :], bank[:, :], ACT.Identity, bias=blin_col[:, 0:1]).then_inc(b_full, 1)
                        act.activation(h_t.hi[:, b, :], bank[:, :], ACT.Identity, bias=blin_col[:, 0:1]).then_inc(b_hi, 1)

                def exponentials(j, b):
                    for nt in range(KT):
                        act.wait_ge(has_neg, 2 * KT * j + KT * b + nt + 1)
                        act.activation(probs[:, nt, :], scores[:, nt, :], ACT.Exp, bias=neg_max[:, b, nt:nt + 1], scale=-1.0,
                                       accum_out=row_sum[:, b, nt:nt + 1]).then_inc(has_probs, 1)

                def round_probs(j, b):
                    for kt in range(KT):
                        c_round(j, PROBS[b] + kt, probs_t.hi[:, kt, :])

                def adj_round(fills):
                    for f in fills:
                        act.wait_ge(l_filled, f + 1)
                        act.activation(at.hi[:, f, :], banks_0[f % A_BANKS][:, :], ACT.Copy).then_inc(l_hi, 1)

                def weights_round():
                    act.wait_ge(l_filled, W_FILL + 1)
                    bank = banks_0[W_FILL % A_BANKS]
                    act.activation(w1_t.hi, bank[:, 0:HID * P], ACT.Copy)
                    act.activation(w2_t.hi.rearrange("p a d -> p (a d)"), bank[:, HID * P:2 * HID * P], ACT.Copy).then_inc(l_hi, 1)
                    act.wait_ge(l_filled, DINV_FILL + 1)
                    act.activation(dinv_row, banks_0[DINV_FILL % A_BANKS][:, :], ACT.Copy).then_inc(has_dinv_row, 1)

                def scaled_round(ks):
                    for k in ks:
                        act.wait_ge(l_scaled, k + 1)
                        act.activation(ah_t.hi[:, k, :], g_full[:, k % 2, :], ACT.Copy, scale=dinv[:, k:k + 1]).then_inc(l_hi, 1)

                def turn(i, zero, one, ahead):
                    j = i - 1
                    final = not zero
                    if final:
                        adj_round(range(0, A_BANKS))
                    if zero:
                        power_round(i, 0)
                        power_round(i, 1)
                    if one:
                        if zero:
                            act.wait_ge(x0_lo, i + 1)
                        ln1.normalise(act, X, j, j)
                    if final:
                        adj_round(range(A_BANKS, KT))
                    if zero:
                        power_round(i, 2)
                        power_round(i, 3)
                    if one:
                        for b in range(PAIR):
                            c_round(j, b, hn_t.hi[:, b, :], ACT.Relu)
                    if zero:
                        power_round(i, 4)
                        power_round(i, 5)
                    if one:
                        project(j)
                        for b in range(PAIR):
                            c_round(j, 4 + b, hn_t.hi[:, b, :])
                    if zero:
                        g_round(i, 2)
                    if one:
                        exponentials(j, 0)
                    if ahead:
                        ln0.normalise(act, X, i + 1, i + 1)
                        act.wait_ge(a_filled, A * i + 6)
                        round_x0(act, i + 1)
                    if one:
                        round_probs(j, 0)
                    if zero:
                        g_round(i, 1)
                    if final:
                        weights_round()
                    if one:
                        exponentials(j, 1)
                    if final:
                        scaled_round(range(0, 2))
                    if one:
                        round_probs(j, 1)
                    if final:
                        scaled_round(range(2, KT))

                turn(0, True, False, True)
                with act.Fori(1, PAIRS - 1) as i:
                    turn(i, True, True, True)
                turn(PAIRS - 1, True, True, False)
                turn(PAIRS, False, True, False)

            @block.gpsimd
            def _(pool):
                def add_b(j):
                    pool.wait_ge(ln1.has_rows, j + 1)
                    for b in range(PAIR):
                        xs = X[:, :, bass.ds(PAIR * j + b, 1), :].rearrange("p k a d -> p k (a d)")
                        last = pool.tensor_tensor(xs, xs, b_row[:, :].unsqueeze(1).to_broadcast([P, KT, D]), ALU.add)
                    last.then_inc(has_xb, 1)

                def turn(i, one, two, ahead, final=False):
                    if one:
                        ln1.scales(pool, pow_half, i - 1)
                    if two:
                        ln2.scales(pool, pow_half, i - 2)
                    if one:
                        add_b(i - 1)
                    if final:
                        pool.wait_ge(has_deg, 1)
                        pool.tensor_tensor(dinv[:, :], deg[:, :], pow_half[:, 0:KT], ALU.pow).then_inc(has_dinv, 1)
                    if ahead:
                        ln0.scales(pool, pow_half, i + 1)

                turn(0, False, False, True)
                turn(1, True, False, True)
                with pool.Fori(2, PAIRS - 1) as i:
                    turn(i, True, True, True)
                turn(PAIRS - 1, True, True, False)
                turn(PAIRS, True, True, False, True)

            @block.vector
            def _(dve):
                def power_rest(i, f):
                    dve.wait_ge(a_hi, A_SPLITS * i + f + 1)
                    q, b = power_of(f)
                    bank = banks_0[f % A_BANKS]
                    if q == 0:
                        ins = dve.scalar_tensor_tensor(x_t.lo[:, q, b, :], bank[:, :], 0.0, as_f32(x_t.hi[:, q, b, :]),
                                                       ALU.max, ALU.subtract)
                    else:
                        ins = dve.tensor_tensor(x_t.lo[:, q, b, :], bank[:, :], as_f32(x_t.hi[:, q, b, :]), ALU.subtract)
                    ins.then_inc(a_drained, 1)

                def g_full_of(i, j):
                    for b in range(PAIR):
                        f = 6 + 4 * (SPLIT - 1 - j) + b
                        dve.wait_ge(a_filled, A * i + f + 1)
                        dve.tensor_tensor(g_full[:, b, :], banks_0[f % A_BANKS][:, :], g_bias[:, j, :], ALU.add).then_inc(a_drained, 1)

                def g_rest(i, j):
                    stage = SPLIT - 1 - j
                    for b in range(PAIR):
                        f = 8 + 4 * stage + b
                        dve.wait_ge(a_hi, A_SPLITS * i + 6 + 2 * stage + b + 1)
                        flat = "p k d -> p (k d)"
                        dve.tensor_tensor(g_rows.lo[:, b, :, :].rearrange(flat), banks_0[f % A_BANKS][:, :],
                                          as_f32(g_rows.hi[:, b, :, :]).rearrange(flat), ALU.subtract).then_inc(a_drained, 1)

                def residual(i):
                    for b in range(PAIR):
                        dve.wait_ge(a_filled, A * i + 16 + b + 1)
                        xs = X[:, :, bass.ds(PAIR * i + b, 1), :].rearrange("p k a d -> p k (a d)")
                        dve.tensor_tensor(xs, banks_0[(16 + b) % A_BANKS][:, :].rearrange("p (k d) -> p k d", k=KT), xs,
                                          ALU.add).then_inc(a_drained, 1)

                def c_rest(j, f, n, hi, lo, relu=False):
                    dve.wait_ge(b_hi, C_SPLITS * j + n + 1)
                    bank = banks_1[f % C_BANKS]
                    if relu:
                        ins = dve.scalar_tensor_tensor(lo, bank[:, :], 0.0, as_f32(hi), ALU.max, ALU.subtract)
                    else:
                        ins = dve.tensor_tensor(lo, bank[:, :], as_f32(hi), ALU.subtract)
                    ins.then_inc(b_drained, 1)

                def edges(j, b, nt):
                    dve.wait_ge(b_filled, C * j + SCORES[b] + nt + 1)
                    if b == 1:
                        dve.wait_ge(has_probs, 2 * KT * j + nt + 1)
                    dve.tensor_tensor(scores[:, nt, :], banks_1[(SCORES[b] + nt) % C_BANKS][:, :], adj_rows[:, nt, :],
                                      ALU.mult).then_inc(b_drained, 1)

                def mask(j, b, nt):
                    dve.wait_ge(b_drained, C * j + SCORES[b] + nt + C_BANKS + 1)
                    dve.tensor_scalar(probs[:, nt, :], scores[:, nt, :], 0.0, MASKED, ALU.is_equal, ALU.mult).then_inc(has_mask, 1)

                def maximum(j, b, nt):
                    dve.wait_ge(has_mask, 2 * KT * j + KT * b + nt + 1)
                    apart(dve, passed)
                    dve.tensor_tensor_reduce(scores[:, nt, :], scores[:, nt, :], probs[:, nt, :], -1.0, 3.0e38,
                                             ALU.add, ALU.min, neg_max[:, b, nt:nt + 1]).then_inc(has_neg, 1)

                def softmax(j, b):
                    for step in range(KT + 2):
                        if step < KT:
                            edges(j, b, step)
                        if 0 <= step - 1 < KT:
                            mask(j, b, step - 1)
                        if 0 <= step - 2 < KT:
                            maximum(j, b, step - 2)

                def rest_of_probs(j, b):
                    dve.wait_ge(has_probs, 2 * KT * j + KT * b + KT)
                    dve.reciprocal(inv_sum[:, b, :], row_sum[:, b, :]).then_inc(has_inv, 1)
                    for kt in range(KT):
                        c_rest(j, PROBS[b] + kt, 6 + KT * b + kt, probs_t.hi[:, kt, :], probs_t.lo[:, kt, :])

                def attention(j, b):
                    dve.wait_ge(b_filled, C * j + OUT[b] + 1)
                    dve.tensor_copy(out_t[:, :], banks_1[OUT[b] % C_BANKS][:, :]).then_inc(b_drained, 1)

                def attention_rows(j, b):
                    if b == 0:
                        dve.wait_ge(has_xb, j + 1)
                    dve.wait_ge(has_inv, PAIR * j + b + 1)
                    dve.wait_ge(o_filled, PAIR * j + b + 1)
                    for nt in range(KT):
                        xs = X[:, nt, bass.ds(PAIR * j + b, 1), :].rearrange("p a d -> p (a d)")
                        last = dve.scalar_tensor_tensor(xs, bank_out[:, nt * D:(nt + 1) * D], inv_sum[:, b, nt:nt + 1],
                                                        xs, ALU.mult, ALU.add)
                    last.then_inc(o_drained, 1)

                def adj_rest(fills):
                    for f in fills:
                        dve.wait_ge(l_hi, f + 1)
                        dve.tensor_reduce(cols_sum[:, f:f + 1], banks_0[f % A_BANKS][:, :], AX.X, ALU.add)
                        dve.tensor_tensor(at.lo[:, f, :], banks_0[f % A_BANKS][:, :], as_f32(at.hi[:, f, :]),
                                          ALU.subtract).then_inc(l_drained, 1)

                def degrees():
                    dve.tensor_reduce(rows_sum[:, :], adj_rows[:, :, :], AX.X, ALU.add)
                    for k in range(KT):
                        last = dve.tensor_tensor_reduce(diag_dinv[:, k, :], adj_rows[:, k, k * P:(k + 1) * P], ident[:, :], 1.0, 0.0,
                                                        ALU.mult, ALU.add, diag[:, k:k + 1])
                    last.then_inc(link_l2, 1)
                    dve.wait_ge(link_l2, 1)
                    dve.scalar_tensor_tensor(deg[:, :], rows_sum[:, :], 1.0, cols_sum[:, :], ALU.add, ALU.add).then_inc(link_l2, 1)
                    dve.wait_ge(link_l2, 2)
                    dve.tensor_tensor(deg[:, :], deg[:, :], diag[:, :], ALU.subtract).then_inc(has_deg, 1)
                    dve.memset(ones_f, 1.0)

                def diagonal():
                    dve.wait_ge(has_dinv, 1)
                    for k in range(KT):
                        last = dve.tensor_scalar(diag_dinv[:, k, :], ident[:, :], dinv[:, k:k + 1], None, ALU.mult)
                    last.then_inc(has_diag_dinv, 1)

                def weights_rest():
                    dve.wait_ge(l_hi, W_FILL + 1)
                    bank = banks_0[W_FILL % A_BANKS]
                    dve.tensor_tensor(w1_t.lo, bank[:, 0:HID * P], as_f32(w1_t.hi), ALU.subtract)
                    flat = "p a d -> p (a d)"
                    dve.tensor_tensor(w2_t.lo.rearrange(flat), bank[:, HID * P:2 * HID * P], as_f32(w2_t.hi).rearrange(flat),
                                      ALU.subtract).then_inc(l_drained, 1)

                def scaled(ks):
                    for k in ks:
                        t = g_full[:, k % 2, :]
                        if k == 0:
                            dve.wait_ge(has_dinv_row, 1)
                            dve.engine_nop().then_inc(l_drained, 1)
                        dve.wait_ge(l_filled, SCALED + k + 1)
                        wait_some(dve, l_lo, k - 1)
                        dve.tensor_tensor(t, banks_0[(SCALED + k) % A_BANKS][:, :], dinv_row, ALU.mult).then_inc(l_drained, 1)
                        dve.wait_ge(l_drained, SCALED + k + 1)
                        dve.scalar_tensor_tensor(t[:, k * P:(k + 1) * P], ident[:, :], dinv[:, k:k + 1], t[:, k * P:(k + 1) * P],
                                                 ALU.mult, ALU.add).then_inc(l_scaled, 1)
                    for k in ks:
                        dve.wait_ge(l_hi, W_FILL + 1 + k + 1)
                        dve.scalar_tensor_tensor(ah_t.lo[:, k, :], g_full[:, k % 2, :], dinv[:, k:k + 1], as_f32(ah_t.hi[:, k, :]),
                                                 ALU.mult, ALU.subtract).then_inc(l_lo, 1)

                def turn(i, zero, one, ahead, two):
                    j = i - 1
                    final = not zero
                    if one:
                        dve.wait_ge(a_drained, A * i + A_BANKS)
                        ln1.statistics(dve, X, j, j)
                    if final:
                        adj_rest(range(0, A_BANKS))
                    if zero:
                        for f in range(2):
                            power_rest(i, f)
                    if two:
                        dve.wait_ge(o_drained, PAIR * j + 1)
                        ln2.statistics(dve, X, j - 1, j - 1)
                    if zero:
                        power_rest(i, 2)
                    if ahead:
                        ln0.statistics(dve, X, i + 1, i + 1)
                    if zero:
                        power_rest(i, 3)
                    if one:
                        for b in range(PAIR):
                            c_rest(j, b, b, hn_t.hi[:, b, :], hn_t.lo[:, b, :], relu=True)
                    if zero:
                        for f in (4, 5):
                            power_rest(i, f)
                    if one:
                        for b in range(PAIR):
                            dve.wait_ge(b_hi, C_SPLITS * j + 2 + b + 1)
                            dve.scalar_tensor_tensor(h_t.lo[:, b, :], banks_1[2 + b][:, :], blin_col[:, 0:1],
                                                     as_f32(h_t.hi[:, b, :]), ALU.add, ALU.subtract).then_inc(b_drained, 1)
                    if zero:
                        g_full_of(i, 2)
                    if one:
                        for b in range(PAIR):
                            c_rest(j, 4 + b, 4 + b, hn_t.hi[:, b, :], hn_t.lo[:, b, :])
                    if zero:
                        g_rest(i, 2)
                    if final:
                        adj_rest(range(A_BANKS, KT))
                    if one:
                        softmax(j, 0)
                    if final:
                        degrees()
                    if zero:
                        g_full_of(i, 1)
                    if one:
                        rest_of_probs(j, 0)
                    if zero:
                        g_rest(i, 1)
                    if final:
                        diagonal()
                    if one:
                        softmax(j, 1)
                    if final:
                        weights_rest()
                    if one:
                        attention(j, 0)
                    if final:
                        scaled(range(0, 2))
                    if ahead:
                        rest_of_x0(dve, i + 1)
                    if zero:
                        g_full_of(i, 0)
                    if one:
                        attention_rows(j, 0)
                        rest_of_probs(j, 1)
                    if zero:
                        residual(i)
                    if final:
                        scaled(range(2, KT))
                    if one:
                        attention(j, 1)
                        attention_rows(j, 1)

                for _ in range(A_BANKS):
                    dve.engine_nop().then_inc(a_drained, 1)
                for _ in range(C_BANKS):
                    dve.engine_nop().then_inc(b_drained, 1)
                dve.engine_nop().then_inc(o_drained, 1)
                dve.wait_ge(x_in, 16 * (B - PAIR))
                turn(0, True, False, True, False)
                turn(1, True, True, True, False)
                with dve.Fori(2, PAIRS - 1) as i:
                    turn(i, True, True, True, True)
                turn(PAIRS - 1, True, True, False, True)
                turn(PAIRS, False, True, False, True)



def phase_b(nc, sb, sb_split, sem, passed, bank_a, bank_b, X, ident, pow_half, ah_t, Y2, bn2, ln2, layer2,
            B, N, D, KT, PAIRS, HID):
    w1_t, w2_t, agg_t = layer2["w1_t"], layer2["w2_t"], layer2["agg_t"]
    b1_col, g1_col, be1_col, out_cols = layer2["b1_col"], layer2["g1_col"], layer2["be1_col"], layer2["out_cols"]
    ctx = ExitStack()
    with ctx:
        Y1 = sb(ctx, "Y1", [P, HID, B, N])
        bn1 = sb(ctx, "bn1", [P, HID, 2])
        stats1 = sb(ctx, "stats1", [P, HID, B, 6])
        stats2 = sb(ctx, "stats2", [P, B, 6])
        mv = sb(ctx, "mv", [P, 3, 2])
        bn_var = sb(ctx, "bn_var", [P, 4])
        bn_rstd = sb(ctx, "bn_rstd", [P, 4])

        with ExitStack() as tmp:
            rows = sb(tmp, "rows2", [P, KT, PAIR, D])
            f_in = sb_split(tmp, "f_in", [P, 2, KT, PAIR, D])
            f_hi, f_lo = sem("f2_hi"), sem("f2_lo")
            agg_filled, agg_hi, agg_drained = sem("agg_filled"), sem("agg_hi"), sem("agg_drained")
            y_filled, y_read, y_stats = sem("y_filled"), sem("y_read"), sem("y_stats")
            has_mv, has_bvar, has_brstd, has_bn, bn_link = sem("bn_mv"), sem("bn_var_s"), sem("bn_rstd_s"), sem("bn_done"), sem("bn_link")
            Y = PAIR * HID

            def columns(dve, turn, first, mvs, stats, scale_shift, gamma, beta, n):
                for a in range(n):
                    last = dve.bn_aggr(mvs[:, a, :], stats[a])
                last.then_inc(has_mv, 1)
                dve.wait_ge(has_mv, turn)
                dve.tensor_scalar(bn_var[:, first:first + n], mvs[:, :, 1], BN_EPS, None, ALU.add).then_inc(has_bvar, 1)
                dve.wait_ge(has_brstd, turn)
                dve.tensor_tensor(scale_shift[:, :, 0], gamma, bn_rstd[:, first:first + n], ALU.mult).then_inc(bn_link, 1)
                dve.wait_ge(bn_link, 2 * turn - 1)
                dve.tensor_tensor(scale_shift[:, :, 1], mvs[:, :, 0], scale_shift[:, :, 0], ALU.mult).then_inc(bn_link, 1)
                dve.wait_ge(bn_link, 2 * turn)
                dve.tensor_tensor(scale_shift[:, :, 1], beta, scale_shift[:, :, 1], ALU.subtract).then_inc(has_bn, 1)

            with nc.Block() as block:
                @block.tensor
                def _(pe):
                    def conv(i, s):
                        pe.wait_ge(f_lo, i + 1)
                        for b in range(PAIR):
                            for k in range(KT):
                                last = split_matmul(pe, bank_a[PAIR * s + b][:, :], f_in[:, s, k, b, :], ah_t[:, k, :],
                                                    k == 0, k == KT - 1)
                            last.then_inc(agg_filled, 1)

                    def product(i):
                        for b in range(PAIR):
                            pe.wait_ge(agg_drained, PAIR * i + b + 1)
                            for a in range(HID):
                                n = HID * b + a
                                wait_some(pe, y_read, Y * (i - 1) + n + 1)
                                split_matmul(pe, bank_b[n][:, :], w1_t[:, a * P:(a + 1) * P], agg_t[:, b, :],
                                             True, True).then_inc(y_filled, 1)

                    keep_warm(pe, bank_b[0], ident, 14)
                    conv(0, 0)
                    conv(1, 1)
                    product(0)
                    with pe.Fori(1, PAIRS // 2) as t:
                        for s in range(2):
                            conv(2 * t + s, s)
                            product(2 * t + s - 1)
                    product(PAIRS - 1)

                @block.scalar
                def _(act):
                    def split_f(i, s):
                        act.wait_ge(ln2.has_rows, i + 1)
                        act.activation(f_in.hi[:, s, :, :, :], rows[:, :, :, :], ACT.Relu).then_inc(f_hi, 1)

                    def turn(i, s, ahead):
                        for b in range(PAIR):
                            act.wait_ge(agg_filled, PAIR * i + b + 1)
                            act.activation(agg_t.hi[:, b, :], bank_a[PAIR * s + b][:, :], ACT.Copy).then_inc(agg_hi, 1)
                        if ahead:
                            split_f(i + 2, s)
                        for b in range(PAIR):
                            for a in range(HID):
                                n = HID * b + a
                                act.wait_ge(y_filled, Y * i + n + 1)
                                act.activation(Y1[:, a, bass.ds(PAIR * i + b, 1), :].rearrange("p a n -> p (a n)"), bank_b[n][:, :],
                                               ACT.Identity, bias=b1_col[:, a:a + 1]).then_inc(y_read, 1)

                    split_f(0, 0)
                    split_f(1, 1)
                    with act.Fori(0, PAIRS // 2 - 1) as t:
                        for s in range(2):
                            turn(2 * t + s, s, True)
                    for s in range(2):
                        turn(PAIRS - 2 + s, s, False)

                @block.gpsimd
                def _(pool):
                    ln2.scales(pool, pow_half, PAIRS - 1)
                    pool.wait_ge(has_bvar, 1)
                    pool.tensor_tensor(bn_rstd[:, 0:HID], bn_var[:, 0:HID], pow_half[:, 0:HID], ALU.pow).then_inc(has_brstd, 1)

                @block.vector
                def _(dve):
                    def split_f(i, s):
                        dve.wait_ge(f_hi, i + 1)
                        flat = "p k b d -> p (k b d)"
                        dve.scalar_tensor_tensor(f_in.lo[:, s, :, :, :].rearrange(flat), rows[:, :, :, :].rearrange(flat), 0.0,
                                                 as_f32(f_in.hi[:, s, :, :, :]).rearrange(flat), ALU.max, ALU.subtract).then_inc(f_lo, 1)

                    def normalise(i):
                        wait_some(dve, f_lo, i)
                        ln2.normalise_dve(dve, X, i, i, rows)

                    def turn(i, s, ahead, further):
                        for b in range(PAIR):
                            dve.wait_ge(agg_hi, PAIR * i + b + 1)
                            dve.tensor_tensor(agg_t.lo[:, b, :], bank_a[PAIR * s + b][:, :], as_f32(agg_t.hi[:, b, :]),
                                              ALU.subtract).then_inc(agg_drained, 1)
                        if ahead:
                            split_f(i + 2, s)
                        if further:
                            normalise(i + 3)
                        for b in range(PAIR):
                            for a in range(HID):
                                dve.wait_ge(y_read, Y * i + HID * b + a + 1)
                                apart(dve, passed)
                                dve.bn_stats(stats1[:, a, bass.ds(PAIR * i + b, 1), :].rearrange("p a n -> p (a n)"),
                                             Y1[:, a, bass.ds(PAIR * i + b, 1), :].rearrange("p a n -> p (a n)")).then_inc(y_stats, 1)

                    for i in range(2):
                        normalise(i)
                        split_f(i, i)
                    normalise(2)
                    ln2.statistics(dve, X, PAIRS - 1, PAIRS - 1)
                    with dve.Fori(0, PAIRS // 2 - 2) as t:
                        for s in range(2):
                            turn(2 * t + s, s, True, True)
                    for i in range(PAIRS - 4, PAIRS):
                        turn(i, i % 2, i + 2 < PAIRS, i + 3 < PAIRS)
                    dve.wait_ge(y_stats, Y * PAIRS)
                    columns(dve, 1, 0, mv[:, 0:HID, :], [stats1[:, a, :, :].rearrange("p b s -> p (b s)") for a in range(HID)],
                            bn1, g1_col[:, :], be1_col[:, :], HID)

        with ExitStack() as tmp:
            RING = 4
            AHEAD = 2
            z_own = sb_split(tmp, "z", [P, 2, HID, N])
            z = [z_own[:, 0, :, :], z_own[:, 1, :, :], ah_t[:, 0:HID, :], ah_t[:, HID:2 * HID, :]]
            has_z, z_hi_0, z_hi_1 = sem("has_z"), sem("z_hi_0"), sem("z_hi_1")
            z_lo_0, z_lo_1 = sem("z_lo_0"), sem("z_lo_1")
            o_filled, o_read = sem("o_filled"), sem("o_read")

            def hidden(j, a):
                return Y1[:, a, bass.ds(j, 1), :].rearrange("p a n -> p (a n)")

            with nc.Block() as block:
                @block.tensor
                def _(pe):
                    def product(j, s):
                        pe.wait_ge(z_lo_0, j + 1)
                        pe.wait_ge(z_lo_1, j + 1)
                        wait_some(pe, o_read, j + 1 - RING)
                        for a in range(HID):
                            last = split_matmul(pe, bank_a[s][:, :], w2_t[:, a, :], z[s][:, a, :], a == 0, a == HID - 1)
                        last.then_inc(o_filled, 1)

                    for s in range(RING):
                        product(s, s)
                    with pe.Fori(1, B // RING) as t:
                        for s in range(RING):
                            product(RING * t + s, s)

                @block.scalar
                def _(act):
                    def norm(j):
                        for a in range(HID):
                            act.activation(hidden(j, a), hidden(j, a), ACT.Relu, bias=bn1[:, a, 1:2],
                                           scale=bn1[:, a, 0:1]).then_inc(has_z, 1)

                    def product(j, s):
                        act.wait_ge(o_filled, j + 1)
                        act.activation(Y2[:, bass.ds(j, 1), :].rearrange("p a n -> p (a n)"), bank_a[s][:, :], ACT.Identity,
                                       bias=out_cols[:, 0:1]).then_inc(o_read, 1)

                    for j in range(AHEAD):
                        norm(j)
                    with act.Fori(0, B // RING - 1) as t:
                        for s in range(RING):
                            norm(RING * t + s + AHEAD)
                            product(RING * t + s, s)
                    for s in range(RING):
                        j = B - RING + s
                        if j + AHEAD < B:
                            norm(j + AHEAD)
                        product(j, s)

                @block.gpsimd
                def _(pool):
                    with pool.Fori(0, B // RING) as t:
                        for s in range(RING):
                            j = RING * t + s
                            pool.wait_ge(z_hi_1, j + 1)
                            pool.tensor_tensor(z[s].lo[:, 1, :], hidden(j, 1), as_f32(z[s].hi[:, 1, :]), ALU.subtract).then_inc(z_lo_1, 1)
                    pool.wait_ge(has_bvar, 2)
                    pool.tensor_tensor(bn_rstd[:, 2:3], bn_var[:, 2:3], pow_half[:, 0:1], ALU.pow).then_inc(has_brstd, 1)

                @block.vector
                def _(dve):
                    def split_z(j, s):
                        dve.wait_ge(has_z, HID * j + HID)
                        wait_some(dve, o_filled, j + 1 - RING)
                        for a in reversed(range(HID)):
                            last = dve.tensor_copy(z[s].hi[:, a, :], hidden(j, a))
                            if a == 1:
                                last.then_inc(z_hi_1, 1)
                        last.then_inc(z_hi_0, 1)
                        dve.wait_ge(z_hi_0, j + 1)
                        dve.tensor_tensor(z[s].lo[:, 0, :], hidden(j, 0), as_f32(z[s].hi[:, 0, :]), ALU.subtract).then_inc(z_lo_0, 1)

                    def product_stats(j):
                        dve.wait_ge(o_read, j + 1)
                        apart(dve, passed)
                        dve.bn_stats(stats2[:, bass.ds(j, 1), :].rearrange("p a s -> p (a s)"),
                                     Y2[:, bass.ds(j, 1), :].rearrange("p a n -> p (a n)")).then_inc(y_stats, 1)

                    LAG = 2
                    for s in range(RING):
                        split_z(s, s)
                        if s >= LAG:
                            product_stats(s - LAG)
                    with dve.Fori(1, B // RING) as t:
                        for s in range(RING):
                            split_z(RING * t + s, s)
                            product_stats(RING * t + s - LAG)
                    for j in range(B - LAG, B):
                        product_stats(j)
                    dve.wait_ge(y_stats, Y * PAIRS + B)
                    columns(dve, 2, 2, mv[:, 2:3, :], [stats2[:, :, :].rearrange("p b s -> p (b s)")],
                            bn2[:, :].unsqueeze(1), out_cols[:, 1:2], out_cols[:, 2:3], 1)



def phase_c(nc, sb, sb_split, sem, passed, bank_a, bank_b, X, ident, pow_half, at, Y2, bn2, rows_sum,
            wg0, bg0, wg1, bg1, wih, whh, bih, bhh, out_rows, B, N, D, KT, PAIRS, SKIP, GATES):
    STREAMS = 2
    GROUPS = PAIRS // STREAMS
    INPUT, FORGET, CELL, OUTPUT = range(GATES)
    UNITS = [(1, 0, 0, 1), (1, 0, 1, 2)] + [(p, t, 0, PAIR) for p in range(2, SKIP + 1) for t in range(p)]
    gates_of = lambda t: (INPUT, CELL, OUTPUT) if t == 0 else (INPUT, CELL, FORGET, OUTPUT)
    before = [sum(len(gates_of(u[1])) for u in UNITS[:n]) for n in range(len(UNITS) + 1)]
    READS = before[-1]
    CONV = 8
    AGG_0, ROWS, AGG_1, FEATURES = 0, 2, 4, 6
    HI_FIRST = 3
    NORMALISE_AT, SPLIT_AT = 2, 4
    wrapped = ExitStack()
    with wrapped as ctx:
        wih_t = sb_split(ctx, "wih_t", [P, SKIP, GATES * P])
        whh_t = sb_split(ctx, "whh_t", [P, SKIP - 1, GATES * P])
        wg = sb_split(ctx, "wg", [P, 2, D])
        gate_bias = sb(ctx, "gate_bias", [P, SKIP, GATES])
        bias0 = sb(ctx, "bias0", [P, KT, D])
        bias1 = sb(ctx, "bias1", [P, N])

        with ExitStack() as tmp:
            raw = sb(tmp, "lstm_raw", [P, 2 * SKIP - 1, GATES, D])
            wg_raw = sb(tmp, "wg_raw", [P, 2, D])
            bg_raw = sb(tmp, "bg_raw", [P, 2, D])
            diag_rows = sb(tmp, "diag_rows", [P, KT, P])
            has_diag_rows, bias_filled = sem("has_diag_rows"), sem("l3_bias_filled")
            bih_col = sb(tmp, "bih_col", [P, SKIP, GATES])
            bhh_col = sb(tmp, "bhh_col", [P, SKIP, GATES])
            params_in, small_hi = sem("l3_params_in"), sem("l3_small_hi")
            s_filled, s_hi, s_drained = sem("l3s_filled"), sem("l3s_hi"), sem("l3s_drained")
            has_y, y_filled, x2_done = sem("has_y"), sem("yt_filled"), sem("x2_done")
            LOADS = 6 + 2 * SKIP

            RING = 4
            y_norm = sb(tmp, "y_norm", [P, RING, N])

            with nc.Block() as block:
                @block.sync
                def _(sp):
                    with nc.allow_non_contiguous_dma(reason="parameter columns"):
                        sp.dma_start(raw[:, 0:SKIP, :, :], wih.rearrange("l (g p) h -> p l g h", p=P)).then_inc(params_in, 16)
                        sp.dma_start(raw[:, SKIP:2 * SKIP - 1, :, :],
                                     whh[1:SKIP].rearrange("l (g p) h -> p l g h", p=P)).then_inc(params_in, 16)
                        sp.dma_start(wg_raw[:, 0, :], wg0).then_inc(params_in, 16)
                        sp.dma_start(wg_raw[:, 1, :], wg1).then_inc(params_in, 16)
                        sp.dma_start(bg_raw[:, 0, :], bg0.partition_broadcast(P)).then_inc(params_in, 16)
                        sp.dma_start(bg_raw[:, 1, :], bg1.partition_broadcast(P)).then_inc(params_in, 16)
                        for l in range(SKIP):
                            sp.dma_start(bih_col[:, l, :], bih[l].rearrange("(g p) -> p g", p=P)).then_inc(params_in, 16)
                            sp.dma_start(bhh_col[:, l, :], bhh[l].rearrange("(g p) -> p g", p=P)).then_inc(params_in, 16)

                W = 2 * SKIP - 1

                def weights(f):
                    return (wih_t[:, f, :] if f < SKIP else whh_t[:, f - SKIP, :])

                @block.tensor
                def _(pe):
                    with pe.Fori(0, B // RING) as t:
                        for r in range(RING):
                            pe.wait_ge(has_y, RING * t + r + 1)
                            pe.wait_ge(x2_done, RING * t + r + 1)
                            for k in range(KT):
                                last = pe.transpose(bank_b[r][:, k * P:(k + 1) * P], y_norm[:, r, k * P:(k + 1) * P], ident[:, :])
                            last.then_inc(y_filled, 1)
                    pe.wait_ge(params_in, 16 * LOADS)
                    for f in range(W):
                        if f >= 4:
                            pe.wait_ge(s_drained, f - 3)
                        for g in range(GATES):
                            last = pe.transpose(bank_a[f % 4][:, g * P:(g + 1) * P], raw[:, f, g, :], ident[:, :])
                        last.then_inc(s_filled, 1)
                    pe.wait_ge(has_diag_rows, 1)
                    for k in range(KT):
                        last = pe.matmul(bank_b[0][:, k * P:(k + 1) * P], bg_raw[:, 1, :], diag_rows[:, k, :], start=True, stop=True)
                    last.then_inc(bias_filled, 1)

                @block.scalar
                def _(act):
                    with act.Fori(0, B // RING) as t:
                        for r in range(RING):
                            act.wait_ge(x2_done, RING * t + r + 1)
                            act.activation(y_norm[:, r, :], Y2[:, bass.ds(RING * t + r, 1), :].rearrange("p a n -> p (a n)"),
                                           ACT.Identity, bias=bn2[:, 1:2], scale=bn2[:, 0:1]).then_inc(has_y, 1)
                    act.wait_ge(params_in, 16 * LOADS)
                    act.activation(wg.hi[:, :, :], wg_raw[:, :, :], ACT.Copy).then_inc(small_hi, 1)
                    for f in range(W):
                        act.wait_ge(s_filled, f + 1)
                        act.activation(weights(f).hi, bank_a[f % 4][:, :], ACT.Copy).then_inc(s_hi, 1)

                @block.vector
                def _(dve):
                    for _ in range(RING):
                        dve.engine_nop().then_inc(x2_done, 1)
                    with dve.Fori(0, B // RING) as t:
                        for r in range(RING):
                            dve.wait_ge(y_filled, RING * t + r + 1)
                            xs = X[:, :, bass.ds(RING * t + r, 1), :].rearrange("p k a d -> p k (a d)")
                            dve.tensor_tensor(xs, bank_b[r][:, :].rearrange("p (k d) -> p k d", k=KT), xs, ALU.add).then_inc(x2_done, 1)
                    dve.wait_ge(small_hi, 1)
                    dve.tensor_tensor(wg.lo[:, :, :], wg_raw[:, :, :], as_f32(wg.hi[:, :, :]), ALU.subtract)
                    for k in range(KT):
                        last = dve.tensor_scalar(diag_rows[:, k, :], ident[:, :], rows_sum[:, k:k + 1], None, ALU.mult)
                    last.then_inc(has_diag_rows, 1)
                    for k in range(KT):
                        dve.tensor_scalar(bias0[:, k, :], bg_raw[:, 0, :], rows_sum[:, k:k + 1], None, ALU.mult)
                    dve.tensor_tensor(gate_bias[:, :, :], bih_col[:, :, :], bhh_col[:, :, :], ALU.add)
                    for f in range(W):
                        dve.wait_ge(s_hi, f + 1)
                        dve.tensor_tensor(weights(f).lo, bank_a[f % 4][:, :], as_f32(weights(f).hi), ALU.subtract).then_inc(s_drained, 1)
                    dve.wait_ge(bias_filled, 1)
                    dve.tensor_copy(bias1[:, :], bank_b[0][:, :])

        class Stream:
            def __init__(self, s):
                n = f"s{s}_"
                self.number = s
                self.banks = (bank_a, bank_b)[s]
                self.rows = sb(ctx, n + "rows", [P, PAIR, KT, D])
                self.h = sb_split(ctx, n + "h", [P, PAIR, N])
                self.agg = sb_split(ctx, n + "agg", [P, PAIR, N])
                self.f = self.agg.view("p b (k d) -> p b k d", k=KT)
                self.h1 = sb_split(ctx, n + "h1", [P, PAIR, KT, D])
                self.step = self.h1.view("p b k d -> p (b k d)")
                self.gates = sb(ctx, n + "gates", [P, GATES, N])
                self.full = self.gates[:, 0:2, :]
                self.c = sb(ctx, n + "c", [P, N])
                self.tc = sb(ctx, n + "tc", [P, N])
                self.h_full = self.rows[:, :, :, :].rearrange("p b k d -> p (b k d)")
                self.ln = Norm(sb, ctx, sem, passed, n + "ln3", self.rows[:, :, :, :].rearrange("p b k d -> p k b d"), KT)
                self.filled = sem(n + "filled")
                self.hi = sem(n + "hi")
                self.drained = sem(n + "drained")
                self.f_hi = sem(n + "f_hi")
                self.f_lo = sem(n + "f_lo")
                self.has_full = sem(n + "has_full")
                self.relu_hi = sem(n + "relu_hi")
                self.relu_lo = sem(n + "relu_lo")
                self.gates_full = sem(n + "gates_full")
                self.gates_read = sem(n + "gates_read")
                self.kept = sem(n + "kept")
                self.added = sem(n + "added")
                self.has_c = sem(n + "has_c")
                self.has_tc = sem(n + "has_tc")
                self.has_h = sem(n + "has_h")
                self.h_hi = sem(n + "h_hi")
                self.h_lo = sem(n + "h_lo")
                self.has_h_full = sem(n + "has_h_full")
                self.out_filled = sem(n + "out_filled")
                self.x_done = sem(n + "x_done")
                self.stored = sem(n + "stored")

        streams = [Stream(s) for s in range(STREAMS)]

        def columns(unit, q=None):
            p, t, b0, b1 = unit
            n = N // p
            return n, b1 - b0, slice(b0, b1), slice(t, t + (n - 1) * p + 1, p)

        def windows(part, unit):
            _, _, bs, ts = columns(unit)
            return part[:, bs, ts]

        def by_batch(ap, unit):
            n, nb, _, _ = columns(unit)
            return ap[:, 0:nb * n].rearrange("p (b n) -> p b n", b=nb)

        UN = len(UNITS)
        ORDER = [(s, n) for n in range(UN) for s in streams]
        later = [n for n, unit in enumerate(UNITS) if unit[1] > 0]

        def bank_of(s, f):
            return s.banks[(f + 2) % 4]

        with nc.Block() as block:
            @block.scalar
            def _(act):
                def split_input(s, u):
                    act.wait_ge(s.ln.has_rows, u + 1)
                    act.activation(s.f.hi, s.rows[:, :, :, :], ACT.Relu).then_inc(s.f_hi, 1)

                def agg(s, u, first, n, batches=range(PAIR)):
                    for b in batches:
                        act.wait_ge(s.filled, CONV * u + first + b + 1)
                        act.activation(s.agg.hi[:, b, :], bank_of(s, first + b)[:, :], ACT.Copy).then_inc(s.hi, 1)

                def relu(s, u, n, dst):
                    for b in range(PAIR):
                        act.wait_ge(s.has_full, 2 * PAIR * u + PAIR * n + b + 1)
                        act.activation(dst[:, b, :], s.full[:, b, :], ACT.Relu).then_inc(s.relu_hi, 1)

                def lstm_step(s, u, n):
                    p, t, _, _ = UNITS[n]
                    width = columns(UNITS[n])[0] * columns(UNITS[n])[1]
                    if n == 0:
                        act.wait_ge(s.relu_lo, 2 * PAIR * u + 2 * PAIR)
                    else:
                        act.wait_ge(s.has_h, UN * u + n)
                    for m, g in enumerate(gates_of(t)):
                        act.wait_ge(s.gates_full, READS * u + before[n] + m + 1)
                        act.activation(s.gates[:, g, 0:width], s.banks[g][:, 0:width], ACT.Tanh if g == CELL else ACT.Sigmoid,
                                       bias=gate_bias[:, p - 1, g:g + 1]).then_inc(s.gates_read, 1)
                    act.wait_ge(s.has_c, UN * u + n + 1)
                    act.activation(s.tc[:, 0:width], s.c[:, 0:width], ACT.Tanh).then_inc(s.has_tc, 1)

                def turn(u, ahead):
                    for s in streams:
                        relu(s, u, 0, s.h1.hi[:, :, :, :].rearrange("p b k d -> p b (k d)"))
                    s0, s1 = streams
                    agg(s0, u, AGG_1, 1)
                    agg(s1, u, AGG_1, 1, (0,))
                    relu(s0, u, 1, s0.h.hi)
                    agg(s1, u, AGG_1, 1, (1,))
                    relu(s1, u, 1, s1.h.hi)
                    for s, n in ORDER:
                        lstm_step(s, u, n)
                        if ahead and n == SPLIT_AT:
                            split_input(s, u + 1)
                    if ahead:
                        for s in streams:
                            agg(s, u + 1, AGG_0, 0)

                for s in streams:
                    split_input(s, 0)
                for s in streams:
                    agg(s, 0, AGG_0, 0)
                with act.Fori(0, GROUPS - 1) as u:
                    turn(u, True)
                turn(GROUPS - 1, False)

            @block.gpsimd
            def _(pool):
                def lstm_product(s, u, n):
                    width = columns(UNITS[n])[0] * columns(UNITS[n])[1]
                    pool.wait_ge(s.gates_read, READS * u + before[n] + 2)
                    pool.tensor_tensor(s.gates[:, CELL, 0:width], s.gates[:, INPUT, 0:width], s.gates[:, CELL, 0:width],
                                       ALU.mult).then_inc(s.added, 1)

                def turn(u, ahead):
                    if ahead:
                        for s in streams:
                            s.ln.scales(pool, pow_half, u + 1)
                    for s, n in ORDER:
                        if n in later:
                            lstm_product(s, u, n)

                for s in streams:
                    s.ln.scales(pool, pow_half, 0)
                with pool.Fori(0, GROUPS - 1) as u:
                    turn(u, True)
                turn(GROUPS - 1, False)

            @block.tensor
            def _(pe):
                def convolve(s, first, src, b):
                    for k in range(KT):
                        last = split_matmul(pe, bank_of(s, first + b)[:, :], src[:, b, k, :], at[:, k, :], k == 0, k == KT - 1)
                    last.then_inc(s.filled, 1)

                def conv_input(s, u):
                    pe.wait_ge(s.f_lo, u + 1)
                    for b in range(PAIR):
                        convolve(s, AGG_0, s.f, b)

                def by_rows(s, u):
                    pe.wait_ge(s.x_done, PAIR * u + 1)
                    for b in range(PAIR):
                        pe.wait_ge(s.drained, 4 * u + b + 1)
                        for nt in range(KT):
                            last = split_matmul(pe, bank_of(s, ROWS + b)[:, nt * D:(nt + 1) * D], s.agg[:, b, nt * P:(nt + 1) * P],
                                                wg[:, 0, :], True, True)
                        last.then_inc(s.filled, 1)

                def conv_h1(s, u, batches=range(PAIR)):
                    for b in batches:
                        pe.wait_ge(s.relu_lo, 2 * PAIR * u + b + 1)
                        convolve(s, AGG_1, s.h1, b)

                def by_features(s, u):
                    for b in range(PAIR):
                        pe.wait_ge(s.drained, 4 * u + PAIR + b + 1)
                        split_matmul(pe, bank_of(s, FEATURES + b)[:, :], wg[:, 1, :], s.agg[:, b, :], True, True).then_inc(s.filled, 1)

                def lstm_product(s, u, n, gates, out, w, x, start):
                    pe.wait_ge(s.h_hi, UN * u + n)
                    for g in gates[:HI_FIRST]:
                        pe.matmul(out(g), w(g).hi, x.hi, start=start, stop=False)
                        pe.matmul(out(g), w(g).lo, x.hi, start=False, stop=False)
                    pe.wait_ge(s.h_lo, UN * u + n)
                    for g in gates[:HI_FIRST]:
                        pe.matmul(out(g), w(g).hi, x.lo, start=False, stop=True).then_inc(s.gates_full, 1)
                    for g in gates[HI_FIRST:]:
                        split_matmul(pe, out(g), w(g), x, start, True).then_inc(s.gates_full, 1)

                def lstm_step(s, u, n):
                    unit = UNITS[n]
                    p, t, b0, b1 = unit
                    width = columns(unit)[0] * columns(unit)[1]
                    x = Split(windows(s.h.hi, unit), windows(s.h.lo, unit))
                    w_x = lambda g: wih_t[:, p - 1, g * P:(g + 1) * P]
                    w_h = lambda g: whh_t[:, p - 2, g * P:(g + 1) * P]
                    out_x = lambda g: by_batch(s.banks[g], unit)
                    out_h = lambda g: s.banks[g][:, 0:width]
                    if p == 1:
                        pe.wait_ge(s.relu_lo, 2 * PAIR * u + PAIR + b1)
                    for g in gates_of(t):
                        users = [k for k in range(n) if g in gates_of(UNITS[k][1])]
                        if users:
                            pe.wait_ge(s.gates_read, READS * u + before[users[-1]] + gates_of(UNITS[users[-1]][1]).index(g) + 1)
                        if p == 1:
                            split_matmul(pe, out_x(g), w_x(g), x, True, True).then_inc(s.gates_full, 1)
                        elif t > 0:
                            split_matmul(pe, out_x(g), w_x(g), x, True, False)
                    if p > 1 and t == 0:
                        lstm_product(s, u, n, gates_of(t), out_x, w_x, x, True)
                    if t > 0:
                        lstm_product(s, u, n, gates_of(t), out_h, w_h, s.step[:, 0:width], False)

                def out_rows_of(s, u):
                    pe.wait_ge(s.has_h_full, u + 1)
                    for b in range(PAIR):
                        for k in range(KT):
                            c = b * N + k * P
                            last = pe.transpose(s.banks[b][:, k * P:(k + 1) * P], s.h_full[:, c:c + P], ident[:, :])
                        last.then_inc(s.out_filled, 1)

                def turn(u, ahead):
                    for s in streams:
                        by_rows(s, u)
                    s0, s1 = streams
                    conv_h1(s0, u)
                    conv_h1(s1, u, (0,))
                    by_features(s0, u)
                    conv_h1(s1, u, (1,))
                    by_features(s1, u)
                    for s, n in ORDER:
                        lstm_step(s, u, n)
                    for s in streams:
                        pe.wait_ge(s.gates_read, READS * (u + 1))
                        if ahead:
                            conv_input(s, u + 1)
                        out_rows_of(s, u)

                keep_warm(pe, bank_a[0], ident, 40)
                for s in streams:
                    conv_input(s, 0)
                with pe.Fori(0, GROUPS - 1) as u:
                    turn(u, True)
                turn(GROUPS - 1, False)

            @block.vector
            def _(dve):
                def pair_of(s, u):
                    return STREAMS * u + s.number

                def split_input(s, u):
                    dve.wait_ge(s.f_hi, u + 1)
                    flat = "p b k d -> p (b k d)"
                    dve.scalar_tensor_tensor(s.f.lo.rearrange(flat), s.rows[:, :, :, :].rearrange(flat), 0.0,
                                             as_f32(s.f.hi).rearrange(flat), ALU.max, ALU.subtract).then_inc(s.f_lo, 1)

                def agg(s, u, first, n, batches=range(PAIR)):
                    for b in batches:
                        dve.wait_ge(s.hi, 2 * PAIR * u + PAIR * n + b + 1)
                        dve.tensor_tensor(s.agg.lo[:, b, :], bank_of(s, first + b)[:, :], as_f32(s.agg.hi[:, b, :]),
                                          ALU.subtract).then_inc(s.drained, 1)

                def with_bias(s, u, first, bias):
                    for b in range(PAIR):
                        dve.wait_ge(s.filled, CONV * u + first + b + 1)
                        dve.tensor_tensor(s.full[:, b, :], bank_of(s, first + b)[:, :], bias, ALU.add).then_inc(s.has_full, 1)

                def relu_rest(s, u, n, hi, lo):
                    for b in range(PAIR):
                        dve.wait_ge(s.relu_hi, 2 * PAIR * u + PAIR * n + b + 1)
                        dve.scalar_tensor_tensor(lo[:, b, :], s.full[:, b, :], 0.0, as_f32(hi[:, b, :]), ALU.max, ALU.subtract)\
                            .then_inc(s.relu_lo, 1)

                def lstm_cell(s, u, n):
                    width = columns(UNITS[n])[0] * columns(UNITS[n])[1]
                    t = UNITS[n][1]
                    c = s.c[:, 0:width]
                    if t == 0:
                        dve.wait_ge(s.gates_read, READS * u + before[n] + 2)
                        dve.tensor_tensor(c, s.gates[:, INPUT, 0:width], s.gates[:, CELL, 0:width], ALU.mult).then_inc(s.has_c, 1)
                        return
                    dve.wait_ge(s.gates_read, READS * u + before[n] + 3)
                    dve.tensor_tensor(c, c, s.gates[:, FORGET, 0:width], ALU.mult).then_inc(s.kept, 1)
                    dve.wait_ge(s.kept, len(later) * u + later.index(n) + 1)
                    dve.wait_ge(s.added, len(later) * u + later.index(n) + 1)
                    dve.tensor_tensor(c, c, s.gates[:, CELL, 0:width], ALU.add).then_inc(s.has_c, 1)

                def lstm_h(s, u, n):
                    unit = UNITS[n]
                    p, t, _, _ = unit
                    width = columns(unit)[0] * columns(unit)[1]
                    tc, o = s.tc[:, 0:width], s.gates[:, OUTPUT, 0:width]
                    if t == p - 1:
                        tc_w, o_w = by_batch(s.tc, unit), by_batch(s.gates[:, OUTPUT, :], unit)
                        hi, lo = windows(s.h.hi, unit), windows(s.h.lo, unit)
                    else:
                        tc_w, o_w, hi, lo = tc, o, s.step.hi[:, 0:width], s.step.lo[:, 0:width]
                    dve.wait_ge(s.has_tc, UN * u + n + 1)
                    dve.tensor_tensor(hi, tc_w, o_w, ALU.mult).then_inc(s.h_hi, 1)
                    dve.wait_ge(s.h_hi, UN * u + n + 1)
                    dve.tensor_tensor(tc, tc, o, ALU.mult).then_inc(s.has_h, 1)
                    dve.wait_ge(s.has_h, UN * u + n + 1)
                    dve.tensor_tensor(lo, tc_w, as_f32(hi), ALU.subtract).then_inc(s.h_lo, 1)

                def whole_h(s, u):
                    dve.wait_ge(s.h_lo, UN * (u + 1))
                    dve.tensor_tensor(s.h_full, as_f32(s.h.hi[:, :, :]).rearrange("p b n -> p (b n)"),
                                      as_f32(s.h.lo[:, :, :]).rearrange("p b n -> p (b n)"), ALU.add).then_inc(s.has_h_full, 1)

                def x3(s, u):
                    for b in range(PAIR):
                        dve.wait_ge(s.out_filled, PAIR * u + b + 1)
                        xs = X[:, :, bass.ds(PAIR * pair_of(s, u) + b, 1), :].rearrange("p k a d -> p k (a d)")
                        dve.tensor_tensor(xs, s.banks[b][:, :].rearrange("p (k d) -> p k d", k=KT), xs, ALU.add).then_inc(s.x_done, 1)

                def turn(u, ahead):
                    for s in streams:
                        with_bias(s, u, ROWS, bias0[:, :, :].rearrange("p k d -> p (k d)"))
                        relu_rest(s, u, 0, s.h1.hi[:, :, :, :].rearrange("p b k d -> p b (k d)"),
                                  s.h1.lo[:, :, :, :].rearrange("p b k d -> p b (k d)"))
                    s0, s1 = streams
                    if ahead:
                        s0.ln.statistics(dve, X, pair_of(s0, u + 1), u + 1)
                    agg(s0, u, AGG_1, 1)
                    if ahead:
                        s1.ln.statistics(dve, X, pair_of(s1, u + 1), u + 1)
                    agg(s1, u, AGG_1, 1, (0,))
                    with_bias(s0, u, FEATURES, bias1[:, :])
                    relu_rest(s0, u, 1, s0.h.hi, s0.h.lo)
                    agg(s1, u, AGG_1, 1, (1,))
                    with_bias(s1, u, FEATURES, bias1[:, :])
                    relu_rest(s1, u, 1, s1.h.hi, s1.h.lo)
                    for s, n in ORDER:
                        lstm_cell(s, u, n)
                        lstm_h(s, u, n)
                        if ahead and n == NORMALISE_AT:
                            s.ln.normalise_dve(dve, X, pair_of(s, u + 1), u + 1)
                        if ahead and n == SPLIT_AT:
                            split_input(s, u + 1)
                        if n == UN - 1:
                            whole_h(s, u)
                    for s in streams:
                        if ahead:
                            agg(s, u + 1, AGG_0, 0)
                        x3(s, u)

                for s in streams:
                    s.ln.statistics(dve, X, pair_of(s, 0), 0)
                for s in streams:
                    s.ln.normalise_dve(dve, X, pair_of(s, 0), 0)
                    split_input(s, 0)
                for s in streams:
                    dve.engine_nop().then_inc(s.x_done, 1)
                for s in streams:
                    agg(s, 0, AGG_0, 0)
                with dve.Fori(0, GROUPS - 1) as u:
                    turn(u, True)
                turn(GROUPS - 1, False)

            @block.sync
            def _(sp):
                with sp.Fori(0, GROUPS) as u:
                    for s in streams:
                        for b in range(PAIR):
                            sp.wait_ge(s.x_done, PAIR * u + b + 2)
                            at_b = PAIR * (STREAMS * u + s.number) + b
                            sp.dma_start(out_rows[bass.ds(at_b, 1)].rearrange("a p k d -> p k (a d)"),
                                         X[:, :, bass.ds(at_b, 1), :].rearrange("p k a d -> p k (a d)")).then_inc(s.stored, 16)
                for s in streams:
                    sp.wait_ge(s.stored, 16 * PAIR * GROUPS)


_INS = ['x', 'adj', 'L0_gnn_alpha_train', 'L0_gnn_w', 'L0_gnn_d', 'L0_gnn_fc_in_w', 'L0_gnn_fc_in_b',
        'L1_gnn_W', 'L1_gnn_b_lin', 'L1_gnn_b',
        'L2_gnn_W1', 'L2_gnn_b1', 'L2_gnn_g1', 'L2_gnn_be1', 'L2_gnn_W2', 'L2_gnn_b2', 'L2_gnn_g2', 'L2_gnn_be2',
        'L3_gnn_Wg0', 'L3_gnn_bg0', 'L3_gnn_Wg1', 'L3_gnn_bg1', 'L3_gnn_Wih', 'L3_gnn_Whh', 'L3_gnn_bih', 'L3_gnn_bhh']
_OUTS = [((16, 512, 128), 'float32')]


def kernel(**inputs):
    import numpy as _np
    import concourse.bacc as _bacc
    from concourse import mybir as _mybir
    from concourse.bass_utils import run_bass_kernel_spmd as _run

    nc = _bacc.Bacc("TRN2", target_bir_lowering=False, num_devices=1)
    arrays, args = {}, []
    for name in _INS:
        a = _np.ascontiguousarray(inputs[name])
        arrays[f"in_{name}_dram"] = a
        args.append(nc.dram_tensor(f"in_{name}_dram", a.shape, _mybir.dt.from_np(a.dtype), kind="ExternalInput").ap())
    for i, (shape, dtype) in enumerate(_OUTS):
        dt = _mybir.dt.from_np(_np.dtype(dtype))
        args.append(nc.dram_tensor(f"out_{i}_dram", shape, dt, kind="ExternalOutput").ap())
    build(nc, *args)
    r = _run(nc, [arrays], core_ids=[0])
    got = tuple(r.results[0][f"out_{i}_dram"] for i in range(len(_OUTS)))
    return got[0]
```
